# Optimizing a Trainium2 kernel written in Bass

```python
import numpy as np
import jax
import jax.numpy as jnp

def _softmax(x, axis=-1):
    return jax.nn.softmax(x, axis=axis)

def _gelu(x):
    return jax.nn.gelu(x, approximate=True)

def _silu(x):
    return jax.nn.silu(x)

def _sigmoid(x):
    return jax.nn.sigmoid(x)

def _layernorm(x, axis=-1, eps=1e-05):
    m = jnp.mean(x, axis=axis, keepdims=True)
    v = jnp.var(x, axis=axis, keepdims=True)
    return (x - m) / jnp.sqrt(v + eps)

def _scatter_add(tgt, idx, src, axis=0):
    return tgt.at[idx].add(src)

def _segment_sum(src, seg, n):
    return jax.ops.segment_sum(src, seg, n)
kernel_name = 'mk_vit_tower_d2_tok_img256_r4_98cb6f'

def setup_inputs(seed: int=0):
    np.random.seed(seed)
    _w = jnp.asarray

    def _rec_inputs():
        import jax
        import jax.numpy as jnp
        _rk = jax.random.key(seed)
        x = -7.10856e-05 + 0.999911 * jax.random.normal(jax.random.fold_in(_rk, 1), (64, 1, 128, 128), jnp.float32)
        return x
    x = _rec_inputs()

    def _L0_tok_setup():
        import jax, jax.numpy as jnp
        import numpy as np
        INV_SQRT2 = 0.7071067811865476

        def haar_dwt2(x):
            lo = (x[..., ::2] + x[..., 1::2]) * INV_SQRT2
            hi = (x[..., ::2] - x[..., 1::2]) * INV_SQRT2
            cA = (lo[..., ::2, :] + lo[..., 1::2, :]) * INV_SQRT2
            cH = (lo[..., ::2, :] - lo[..., 1::2, :]) * INV_SQRT2
            cV = (hi[..., ::2, :] + hi[..., 1::2, :]) * INV_SQRT2
            cD = (hi[..., ::2, :] - hi[..., 1::2, :]) * INV_SQRT2
            return (cA, (cH, cV, cD))

        def wavedec2_maps(x, levels):
            a = x
            details = []
            for _ in range(levels):
                a, d = haar_dwt2(a)
                details.append(d)
            maps = [a]
            for d in reversed(details):
                maps.extend(d)
            return maps
        key = jax.random.key(seed)
        k1, k2 = jax.random.split(key)
        B, H, W_img = (64, 256, 256)
        x = jax.random.normal(k1, (B, 1, H, W_img), dtype=jnp.float32)
        n_maps = 1 + 3 * 2
        W = jax.random.normal(k2, (n_maps, 64), dtype=jnp.float32) * (1.0 / np.sqrt(n_maps))
        b = jnp.zeros((64,), dtype=jnp.float32)
        return {'x': x, 'W': W, 'b': b}
    _L0_tok_all = _L0_tok_setup()
    _L0_tok_in = {k: v for k, v in _L0_tok_all.items() if k in ('W', 'b')}
    del _L0_tok_all

    def _L0_attn_setup():
        import jax, jax.numpy as jnp
        import numpy as np
        B, L, D = (4, 1024, 64)
        key = jax.random.key(seed)
        kx, kq, kk, kv, ko = jax.random.split(key, 5)
        std = 0.02
        return {'x': jax.random.normal(kx, (B, L, D), dtype=jnp.float32), 'Wq': std * jax.random.normal(kq, (D, D), dtype=jnp.float32), 'Wk': std * jax.random.normal(kk, (D, D), dtype=jnp.float32), 'Wv': std * jax.random.normal(kv, (D, D), dtype=jnp.float32), 'Wo': std * jax.random.normal(ko, (D, D), dtype=jnp.float32)}
    _L0_attn_all = _L0_attn_setup()
    _L0_attn_in = {k: v for k, v in _L0_attn_all.items() if k in ('Wq', 'Wk', 'Wv', 'Wo')}
    del _L0_attn_all

    def _L0_ffn_setup():
        import jax, jax.numpy as jnp
        import numpy as np
        B, T, C = (64, 96, 64)
        NH, NKV = (4, 2)
        HD = C // NH
        NREP = NH // NKV
        NE, TOPK = (8, 2)
        HID = int(8 / 3 * C)
        EPS_RMS = 1e-06

        def _rope_tables(t_len):
            inv_freq = 1.0 / 10000.0 ** (np.arange(0, HD, 2, dtype=np.float32) / HD)
            t = np.arange(t_len, dtype=np.float32)
            freqs = np.outer(t, inv_freq)
            emb = np.concatenate([freqs, freqs], axis=-1)
            return (jnp.asarray(np.cos(emb)), jnp.asarray(np.sin(emb)))

        def _rotate_half(x):
            h = x.shape[-1] // 2
            return jnp.concatenate([-x[..., h:], x[..., :h]], axis=-1)

        def _rmsnorm(v, w):
            return v * jax.lax.rsqrt(jnp.mean(v * v, axis=-1, keepdims=True) + EPS_RMS) * w
        key = jax.random.key(seed)
        ks = jax.random.split(key, 10)
        s = lambda k, shape: jax.random.normal(k, shape, jnp.float32) * 0.02
        return {'x': jax.random.normal(ks[0], (B, T, C), jnp.float32), 'ln1_w': jnp.ones((C,), jnp.float32), 'ln2_w': jnp.ones((C,), jnp.float32), 'wq': s(ks[1], (NH * HD, C)), 'wk': s(ks[2], (NKV * HD, C)), 'wv': s(ks[3], (NKV * HD, C)), 'wo': s(ks[4], (C, C)), 'router_w': s(ks[5], (NE, C)), 'w1': s(ks[6], (NE, HID, C)), 'w2': s(ks[7], (NE, C, HID)), 'w3': s(ks[8], (NE, HID, C))}
    _L0_ffn_all = _L0_ffn_setup()
    _L0_ffn_in = {k: v for k, v in _L0_ffn_all.items() if k in ('ln1_w', 'ln2_w', 'wq', 'wk', 'wv', 'wo', 'router_w', 'w1', 'w2', 'w3')}
    del _L0_ffn_all

    def _L1_attn_setup():
        import jax, jax.numpy as jnp
        import numpy as np
        import math
        H = 8
        DH = 16
        DEPTH = 1
        LAMBDA_INIT = 0.8 - 0.6 * math.exp(-0.3 * DEPTH)
        LN_EPS = 1e-05
        key = jax.random.key(seed)
        ks = jax.random.split(key, 12)
        dim = 64
        inner = 2 * H * DH
        b, n = (2, 512)
        s = lambda fan_in: 1.0 / math.sqrt(fan_in)
        return {'x': jax.random.normal(ks[0], (b, n, dim), jnp.float32), 'Wq': jax.random.normal(ks[1], (dim, inner), jnp.float32) * s(dim), 'Wkv': jax.random.normal(ks[2], (dim, 2 * inner), jnp.float32) * s(dim), 'Wout': jax.random.normal(ks[3], (inner, dim), jnp.float32) * s(inner), 'bout': jnp.zeros((dim,), jnp.float32), 'Wg': jax.random.normal(ks[4], (dim, inner), jnp.float32) * s(dim), 'bg': jnp.ones((inner,), jnp.float32), 'lq1': jax.random.normal(ks[5], (DH,), jnp.float32) * 0.1, 'lk1': jax.random.normal(ks[6], (DH,), jnp.float32) * 0.1, 'lq2': jax.random.normal(ks[7], (DH,), jnp.float32) * 0.1, 'lk2': jax.random.normal(ks[8], (DH,), jnp.float32) * 0.1, 'ln_gamma': jnp.ones((2 * DH,), jnp.float32), 'ln_beta': jnp.zeros((2 * DH,), jnp.float32)}
    _L1_attn_all = _L1_attn_setup()
    _L1_attn_in = {k: v for k, v in _L1_attn_all.items() if k in ('Wq', 'Wkv', 'Wout', 'bout', 'Wg', 'bg', 'lq1', 'lk1', 'lq2', 'lk2', 'ln_gamma', 'ln_beta')}
    del _L1_attn_all

    def _L1_ffn_setup():
        import jax, jax.numpy as jnp
        import numpy as np
        N_EXPERTS = 8
        TOP_K = 2
        key = jax.random.key(seed)
        ks = jax.random.split(key, 5)
        B, T, C, E, H = (8, 512, 64, 8, 682)
        scale = 1.0 / np.sqrt(C)
        return {'x': jax.random.normal(ks[0], (B, T, C), dtype=jnp.float32), 'router_w': jax.random.normal(ks[1], (E, C), dtype=jnp.float32) * scale, 'w1': jax.random.normal(ks[2], (E, H, C), dtype=jnp.float32) * scale, 'w2': jax.random.normal(ks[3], (E, C, H), dtype=jnp.float32) * (1.0 / np.sqrt(H)), 'w3': jax.random.normal(ks[4], (E, H, C), dtype=jnp.float32) * scale}
    _L1_ffn_all = _L1_ffn_setup()
    _L1_ffn_in = {k: v for k, v in _L1_ffn_all.items() if k in ('router_w', 'w1', 'w2', 'w3')}
    del _L1_ffn_all
    return {'x': x, 'L0_tok_W': _L0_tok_in['W'], 'L0_tok_b': _L0_tok_in['b'], 'L0_attn_Wq': _L0_attn_in['Wq'], 'L0_attn_Wk': _L0_attn_in['Wk'], 'L0_attn_Wv': _L0_attn_in['Wv'], 'L0_attn_Wo': _L0_attn_in['Wo'], 'L0_ffn_ln1_w': _L0_ffn_in['ln1_w'], 'L0_ffn_ln2_w': _L0_ffn_in['ln2_w'], 'L0_ffn_wq': _L0_ffn_in['wq'], 'L0_ffn_wk': _L0_ffn_in['wk'], 'L0_ffn_wv': _L0_ffn_in['wv'], 'L0_ffn_wo': _L0_ffn_in['wo'], 'L0_ffn_router_w': _L0_ffn_in['router_w'], 'L0_ffn_w1': _L0_ffn_in['w1'], 'L0_ffn_w2': _L0_ffn_in['w2'], 'L0_ffn_w3': _L0_ffn_in['w3'], 'L1_attn_Wq': _L1_attn_in['Wq'], 'L1_attn_Wkv': _L1_attn_in['Wkv'], 'L1_attn_Wout': _L1_attn_in['Wout'], 'L1_attn_bout': _L1_attn_in['bout'], 'L1_attn_Wg': _L1_attn_in['Wg'], 'L1_attn_bg': _L1_attn_in['bg'], 'L1_attn_lq1': _L1_attn_in['lq1'], 'L1_attn_lk1': _L1_attn_in['lk1'], 'L1_attn_lq2': _L1_attn_in['lq2'], 'L1_attn_lk2': _L1_attn_in['lk2'], 'L1_attn_ln_gamma': _L1_attn_in['ln_gamma'], 'L1_attn_ln_beta': _L1_attn_in['ln_beta'], 'L1_ffn_router_w': _L1_ffn_in['router_w'], 'L1_ffn_w1': _L1_ffn_in['w1'], 'L1_ffn_w2': _L1_ffn_in['w2'], 'L1_ffn_w3': _L1_ffn_in['w3']}

def reference(x, L0_tok_W, L0_tok_b, L0_attn_Wq, L0_attn_Wk, L0_attn_Wv, L0_attn_Wo, L0_ffn_ln1_w, L0_ffn_ln2_w, L0_ffn_wq, L0_ffn_wk, L0_ffn_wv, L0_ffn_wo, L0_ffn_router_w, L0_ffn_w1, L0_ffn_w2, L0_ffn_w3, L1_attn_Wq, L1_attn_Wkv, L1_attn_Wout, L1_attn_bout, L1_attn_Wg, L1_attn_bg, L1_attn_lq1, L1_attn_lk1, L1_attn_lq2, L1_attn_lk2, L1_attn_ln_gamma, L1_attn_ln_beta, L1_ffn_router_w, L1_ffn_w1, L1_ffn_w2, L1_ffn_w3):
    import jax
    import jax.numpy as jnp

    def _L0_tok_ref(x, W, b):
        import jax, jax.numpy as jnp
        import numpy as np
        INV_SQRT2 = 0.7071067811865476

        def haar_dwt2(x):
            lo = (x[..., ::2] + x[..., 1::2]) * INV_SQRT2
            hi = (x[..., ::2] - x[..., 1::2]) * INV_SQRT2
            cA = (lo[..., ::2, :] + lo[..., 1::2, :]) * INV_SQRT2
            cH = (lo[..., ::2, :] - lo[..., 1::2, :]) * INV_SQRT2
            cV = (hi[..., ::2, :] + hi[..., 1::2, :]) * INV_SQRT2
            cD = (hi[..., ::2, :] - hi[..., 1::2, :]) * INV_SQRT2
            return (cA, (cH, cV, cD))

        def wavedec2_maps(x, levels):
            a = x
            details = []
            for _ in range(levels):
                a, d = haar_dwt2(a)
                details.append(d)
            maps = [a]
            for d in reversed(details):
                maps.extend(d)
            return maps
        imgs = x[:, 0]
        B = imgs.shape[0]
        maps = wavedec2_maps(imgs, 2)
        proc = [jax.image.resize(m, (B, 8, 8), method='bilinear') for m in maps]
        feat = jnp.stack(proc, axis=1)
        feat = feat.reshape(B, feat.shape[1], 64).transpose(0, 2, 1)
        return feat @ W + b

    def _L0_attn_ref(x, Wq, Wk, Wv, Wo):
        import jax, jax.numpy as jnp
        import numpy as np
        B, L, D = (4, 1024, 64)
        q = x @ Wq.T
        k = x @ Wk.T
        v = x @ Wv.T
        logits = jnp.einsum('bld,bmd->blm', q, k)
        Lq = x.shape[1]
        causal_mask = jnp.triu(jnp.ones((Lq, Lq), dtype=bool), k=1)
        logits = jnp.where(causal_mask[None], jnp.asarray(0.0, logits.dtype), logits)
        attn = jax.nn.relu(logits)
        row_counts = jnp.maximum(jnp.arange(Lq, dtype=attn.dtype), 1.0)
        attn = attn / row_counts[None, :, None]
        ctx = jnp.einsum('blm,bmd->bld', attn, v)
        return ctx @ Wo.T

    def _L0_ffn_ref(x, ln1_w, ln2_w, wq, wk, wv, wo, router_w, w1, w2, w3):
        import jax, jax.numpy as jnp
        import numpy as np
        B, T, C = (64, 96, 64)
        NH, NKV = (4, 2)
        HD = C // NH
        NREP = NH // NKV
        NE, TOPK = (8, 2)
        HID = int(8 / 3 * C)
        EPS_RMS = 1e-06

        def _rope_tables(t_len):
            inv_freq = 1.0 / 10000.0 ** (np.arange(0, HD, 2, dtype=np.float32) / HD)
            t = np.arange(t_len, dtype=np.float32)
            freqs = np.outer(t, inv_freq)
            emb = np.concatenate([freqs, freqs], axis=-1)
            return (jnp.asarray(np.cos(emb)), jnp.asarray(np.sin(emb)))

        def _rotate_half(x):
            h = x.shape[-1] // 2
            return jnp.concatenate([-x[..., h:], x[..., :h]], axis=-1)

        def _rmsnorm(v, w):
            return v * jax.lax.rsqrt(jnp.mean(v * v, axis=-1, keepdims=True) + EPS_RMS) * w
        Bx, Tx, Cx = x.shape
        h = _rmsnorm(x, ln1_w)
        q = (h @ wq.T).reshape(Bx, Tx, NH, HD).transpose(0, 2, 1, 3)
        k = (h @ wk.T).reshape(Bx, Tx, NKV, HD).transpose(0, 2, 1, 3)
        v = (h @ wv.T).reshape(Bx, Tx, NKV, HD).transpose(0, 2, 1, 3)
        cos, sin = _rope_tables(Tx)
        cos, sin = (cos[None, None], sin[None, None])
        q = q * cos + _rotate_half(q) * sin
        k = k * cos + _rotate_half(k) * sin
        k = jnp.repeat(k, NREP, axis=1)
        v = jnp.repeat(v, NREP, axis=1)
        scores = jnp.einsum('bhtd,bhsd->bhts', q, k) / jnp.sqrt(jnp.float32(HD))
        causal = jnp.tril(jnp.ones((Tx, Tx), dtype=bool))
        scores = jnp.where(causal[None, None], scores, jnp.float32(-1e+30))
        att = jax.nn.softmax(scores, axis=-1)
        y = jnp.einsum('bhts,bhsd->bhtd', att, v).transpose(0, 2, 1, 3).reshape(Bx, Tx, Cx)
        x = x + y @ wo.T
        flat = _rmsnorm(x, ln2_w).reshape(-1, Cx)
        probs = jax.nn.softmax(flat @ router_w.T, axis=-1)
        tp, ti = jax.lax.top_k(probs, TOPK)
        tp = tp / (jnp.sum(tp, axis=-1, keepdims=True) + 1e-09)
        weights = jnp.sum(tp[..., None] * jax.nn.one_hot(ti, NE, dtype=flat.dtype), axis=1)
        out = jnp.zeros_like(flat)
        for e in range(NE):
            hh = jax.nn.silu(flat @ w1[e].T) * (flat @ w3[e].T)
            out = out + weights[:, e:e + 1] * (hh @ w2[e].T)
        return x + out.reshape(Bx, Tx, Cx)

    def _L1_attn_ref(x, Wq, Wkv, Wout, bout, Wg, bg, lq1, lk1, lq2, lk2, ln_gamma, ln_beta):
        import jax, jax.numpy as jnp
        import numpy as np
        import math
        H = 8
        DH = 16
        DEPTH = 1
        LAMBDA_INIT = 0.8 - 0.6 * math.exp(-0.3 * DEPTH)
        LN_EPS = 1e-05
        b, n, dim = x.shape
        scale = DH ** (-0.5)
        q = x @ Wq
        kv = x @ Wkv
        k, v = jnp.split(kv, 2, axis=-1)
        q = q.reshape(b, n, 2 * H, DH).transpose(0, 2, 1, 3) * scale
        k = k.reshape(b, n, 2 * H, DH).transpose(0, 2, 1, 3)
        v = v.reshape(b, n, H, 2 * DH).transpose(0, 2, 1, 3)
        dots = jnp.einsum('bhid,bhjd->bhij', q, k)
        attn = jax.nn.softmax(dots, axis=-1)
        lam1 = jnp.exp(jnp.sum(lq1 * lk1))
        lam2 = jnp.exp(jnp.sum(lq2 * lk2))
        lam = lam1 - lam2 + LAMBDA_INIT
        attn = attn.reshape(b, H, 2, n, n)
        attn = attn[:, :, 0] - lam * attn[:, :, 1]
        out = jnp.einsum('bhij,bhjd->bhid', attn, v)
        mu = jnp.mean(out, axis=-1, keepdims=True)
        var = jnp.var(out, axis=-1, keepdims=True)
        out = (out - mu) * jax.lax.rsqrt(var + LN_EPS) * ln_gamma + ln_beta
        out = out * (1.0 - LAMBDA_INIT)
        out = out.transpose(0, 2, 1, 3).reshape(b, n, H * 2 * DH)
        gates = x @ Wg + bg
        out = out * jax.nn.sigmoid(gates)
        return out @ Wout + bout

    def _L1_ffn_ref(x, router_w, w1, w2, w3):
        import jax, jax.numpy as jnp
        import numpy as np
        N_EXPERTS = 8
        TOP_K = 2
        B, T, C = x.shape
        flat = x.reshape(-1, C)
        logits = flat @ router_w.T
        probs = jax.nn.softmax(logits, axis=-1)
        topk_probs, topk_idx = jax.lax.top_k(probs, TOP_K)
        topk_probs = topk_probs / (jnp.sum(topk_probs, axis=-1, keepdims=True) + 1e-09)
        onehot = jax.nn.one_hot(topk_idx, N_EXPERTS, dtype=flat.dtype)
        gates = jnp.einsum('nk,nke->ne', topk_probs, onehot)
        h1 = jnp.einsum('nc,ehc->neh', flat, w1)
        h3 = jnp.einsum('nc,ehc->neh', flat, w3)
        h = jax.nn.silu(h1) * h3
        y = jnp.einsum('neh,ech->nec', h, w2)
        out = jnp.einsum('ne,nec->nc', gates, y)
        return out.reshape(B, T, C)
    h = _L0_tok_ref(x, L0_tok_W, L0_tok_b)
    h = h + _L0_attn_ref(_layernorm(h, axis=-1), L0_attn_Wq, L0_attn_Wk, L0_attn_Wv, L0_attn_Wo)
    h = h + _L0_ffn_ref(_layernorm(h, axis=-1), L0_ffn_ln1_w, L0_ffn_ln2_w, L0_ffn_wq, L0_ffn_wk, L0_ffn_wv, L0_ffn_wo, L0_ffn_router_w, L0_ffn_w1, L0_ffn_w2, L0_ffn_w3)
    h = h + _L1_attn_ref(_layernorm(h, axis=-1), L1_attn_Wq, L1_attn_Wkv, L1_attn_Wout, L1_attn_bout, L1_attn_Wg, L1_attn_bg, L1_attn_lq1, L1_attn_lk1, L1_attn_lq2, L1_attn_lk2, L1_attn_ln_gamma, L1_attn_ln_beta)
    h = h + _L1_ffn_ref(_layernorm(h, axis=-1), L1_ffn_router_w, L1_ffn_w1, L1_ffn_w2, L1_ffn_w3)
    return h

_drawn_inputs = setup_inputs


def setup_inputs(seed=0):
    import zlib

    import numpy as np

    out = dict(_drawn_inputs(seed))
    spreads = {'L0_tok_b': (0.0, 0.1),
     'L0_ffn_ln1_w': (1.0, 0.6),
     'L0_ffn_ln2_w': (1.0, 0.6),
     'L1_attn_bout': (0.0, 0.1),
     'L1_attn_bg': (1.0, 0.6),
     'L1_attn_ln_gamma': (1.0, 0.6),
     'L1_attn_ln_beta': (0.0, 0.537)}
    factors = {'L0_attn_Wq': 3.308,
     'L0_attn_Wk': 2.847,
     'L0_attn_Wv': 3.17,
     'L0_ffn_wq': 8.0,
     'L0_ffn_wk': 8.0,
     'L0_ffn_router_w': 8.0,
     'L0_ffn_w1': 6.673,
     'L0_ffn_w2': 8.0,
     'L0_ffn_w3': 8.0,
     'L1_attn_lq1': 20.986,
     'L1_attn_lq2': 5.577,
     'L1_attn_lk2': 3.336}
    for name, (base, spread) in spreads.items():
        noise = np.random.default_rng([zlib.crc32(name.encode()), seed]).standard_normal(out[name].shape)
        drawn = base * np.exp(spread * noise) if base else spread * noise
        out[name] = jnp.asarray(drawn.astype(out[name].dtype))
    for name, factor in factors.items():
        out[name] = (out[name] * factor).astype(out[name].dtype)
    return out
```

```python
import math

import numpy as np
import concourse.bass as bass
from concourse import mybir
from contextlib import ExitStack

B = 64
IMG = 128
SIDE = 8
L = SIDE * SIDE
C = 64
P = 128
NTOK = B * L
NT = NTOK // P
GT = 4
NG = NT // GT
GTOK = GT * P
GB = GTOK // L
NF = 7
NOP = 4
NE = 8
HID0, HID1 = 170, 682
NH0, HD = 4, 16
NH1 = 8
DV = 32
LAMBDA_INIT = 0.8 - 0.6 * math.exp(-0.3)
LN_EPS, RMS_EPS = 1e-5, 1e-6
WSCALE = 64.0
STREAMS = 2

MAPS = [(0, 0), (1, 0), (0, 1), (1, 1), (3, 2), (2, 3), (3, 3)]


def constants():
    def resize(n):
        scale = n / SIDE
        centre = (np.arange(SIDE) + 0.5) * scale - 0.5
        w = np.maximum(0, 1 - np.abs(centre[None, :] - np.arange(n)[:, None]) / scale)
        return (w / w.sum(0, keepdims=True)).T

    def haar(n, sign):
        m = np.zeros((n // 2, n))
        m[np.arange(n // 2), 2 * np.arange(n // 2)] = 1
        m[np.arange(n // 2), 2 * np.arange(n // 2) + 1] = sign
        return m * 0.7071067811865476

    ops = np.concatenate([resize(IMG // 4) @ haar(IMG // 2, 1) @ haar(IMG, 1),
                          resize(IMG // 4) @ haar(IMG // 2, -1) @ haar(IMG, 1),
                          resize(IMG // 2) @ haar(IMG, 1),
                          resize(IMG // 2) @ haar(IMG, -1)])
    parts = {}

    def add(name, a):
        full = np.zeros((P, a.shape[1]), np.float32)
        full[:a.shape[0]] = a
        parts[name] = full

    p = np.arange(P)
    add("ident", np.eye(P))
    add("fold", (p[:, None] % C == p[None, :] % C).astype(float))
    add("ops_t", ops.T)
    sel = np.zeros((NF, NOP, NOP * SIDE))
    for f, (ro, co) in enumerate(MAPS):
        sel[f, ro, co * SIDE:(co + 1) * SIDE] = 1
    add("map_sel", sel.reshape(NF, -1))
    add("x_diag", (p[:NOP * SIDE, None] % SIDE == np.arange(SIDE)[None, :]).astype(float))
    same = (p[:, None] // L == p[None, :] // L) & (p[:, None] <= p[None, :])
    add("lin_mask", same / np.maximum(p[None, :] % L, 1))
    inv_freq = 1.0 / 10000.0 ** (np.arange(0, HD, 2, dtype=np.float32) / HD)
    angle = np.outer(np.arange(L, dtype=np.float32), inv_freq).astype(np.float32)
    angle = np.concatenate([angle, angle], -1).T
    add("cos_sin", np.concatenate([np.tile(np.cos(angle), (NH0, 1)), np.tile(np.sin(angle), (NH0, 1))]))
    rot = np.zeros((HD, HD))
    rot[np.arange(8), np.arange(8) + 8] = -1
    rot[np.arange(8) + 8, np.arange(8)] = 1
    q_rot = np.kron(np.eye(NH0), rot)
    add("q_sel", np.concatenate([np.eye(C), q_rot.T], 1))
    rep = np.zeros((C, C // 2))
    for h in range(NH0):
        rep[h * HD:(h + 1) * HD, (h // 2) * HD:(h // 2 + 1) * HD] = np.eye(HD)
    add("k_sel", np.concatenate([rep.T, (q_rot @ rep).T], 1))
    add("causal", np.where(p[:, None] % L >= np.arange(L)[None, :], 0.0, -1e30))
    add("head_mask", ((p[:, None] % C) // HD == np.arange(NH0)[None, :]).astype(float))
    add("first", np.tile(np.arange(NE, 0, -1.0), (P, 1)))
    cols, at = {}, 0
    for name, a in parts.items():
        cols[name] = (at, at + a.shape[1])
        at += a.shape[1]
    return np.concatenate(list(parts.values()), 1).astype(np.float32), cols


def build(nc, d, out, cols):
    F32, F16 = mybir.dt.float32, mybir.dt.float16
    ALU, ACT, AX = mybir.AluOpType, mybir.ActivationFunctionType, mybir.AxisListType
    with ExitStack() as top:
        def tile(ctx, name, shape, dt=F32):
            return ctx.enter_context(nc.sbuf_tensor(name, shape, dt))

        phase_sems = []

        def sem(ctx, name):
            s = ctx.enter_context(nc.semaphore(name))
            if ctx is not top:
                phase_sems.append(s)
            return s

        def phase_block(ctx):
            def clear():
                for s in phase_sems:
                    nc.gpsimd.sem_clear(s)
                phase_sems.clear()
                nc.all_engine_barrier()

            ctx.callback(clear)
            return ctx.enter_context(nc.Block())

        def bc(ap, dims):
            return ap.unsqueeze(2).broadcast_to(list(ap.shape) + [dims])

        def over(ap, n):
            return ap.unsqueeze(1).broadcast_to([ap.shape[0], n, ap.shape[1]])

        PS = top.enter_context(nc.psum_tensor("PS", [P, 8, 512], F32))
        H = tile(top, "H", [P, NT, C])
        KC = tile(top, "KC", [P, sum(b - a for a, b in [cols[k] for k in cols])])

        def k(name, rows=P):
            a, b = cols[name]
            return KC[0:rows, a:b]

        ident = k("ident")
        M1 = tile(top, "M1", [C, C])
        M2 = tile(top, "M2", [C, C])
        WQ2 = tile(top, "WQ2", [C, P])
        WK2 = tile(top, "WK2", [C, P])
        WV0 = tile(top, "WV0", [C, 32])
        WO0 = tile(top, "WO0", [C, C])
        WQKV = tile(top, "WQKV", [C, 768])
        WG = tile(top, "WG", [C + 1, 256])
        WOUT = tile(top, "WOUT", [P, 2, C])
        RW = tile(top, "RW", [C, 2, NE])
        LNW = tile(top, "LNW", [C, 2])
        BTOK = tile(top, "BTOK", [P, C])
        BOUT = tile(top, "BOUT", [P, C])
        GAMMA = tile(top, "GAMMA", [P, DV])
        BETA = tile(top, "BETA", [P, DV])
        LAM = tile(top, "LAM", [P, 1])
        NHALF = tile(top, "NHALF", [P, NT * 8])

        consts_ok = sem(top, "consts_ok")

        with ExitStack() as ctx:
            IM = tile(ctx, "IM", [P, B, IMG])
            A1 = tile(ctx, "A1", [P, B, NOP * SIDE])
            A2 = tile(ctx, "A2", [NOP * SIDE, NOP, B * SIDE])
            WT = tile(ctx, "WT", [NF, C])
            WX = tile(ctx, "WX", [NOP * SIDE, NOP, C])
            WD = tile(ctx, "WD", [NOP * SIDE, NOP, SIDE, C])
            HT = tile(ctx, "HT", [P, NG // 2, SIDE * C])
            RAW = tile(ctx, "RAW", [C, 7, C])
            WKR = tile(ctx, "WKR", [32, C])
            WV0R = tile(ctx, "WV0R", [C, 32])
            VM = tile(ctx, "VM", [C, NH1])
            LQ = tile(ctx, "LQ", [P, 4, HD])
            LP = tile(ctx, "LP", [P, 2, HD])
            LS = tile(ctx, "LS", [P, 2])
            LE = tile(ctx, "LE", [P, 2])
            tok_dram = nc.dram_tensor("tok_scratch", (NTOK, C), F32, kind="Internal").ap()
            NIM = 8
            img_in = [sem(ctx, f"img_in{i}") for i in range(B // NIM)]
            consts_in, weights_in = sem(ctx, "consts_in"), sem(ctx, "weights_in")
            prep_mm, prep_done, w_step = sem(ctx, "prep_mm"), sem(ctx, "prep_done"), sem(ctx, "w_step")
            lam_exp = sem(ctx, "lam_exp")
            rows_mm, rows_copied = sem(ctx, "rows_mm"), sem(ctx, "rows_copied")
            cols_mm, cols_copied = sem(ctx, "cols_mm"), sem(ctx, "cols_copied")
            tok_mm, tok_ready, tok_out, tok_in = (sem(ctx, n) for n in ("tok_mm", "tok_ready", "tok_out", "tok_in"))
            wd_ready = sem(ctx, "wd_ready")
            NWL = 20
            block = phase_block(ctx)

            @block.sync
            def _(sp):
                sp.dma_start(KC[:], d["consts"]).then_inc(consts_in, 16)
                sp.dma_start(WT[:], d["L0_tok_W"]).then_inc(consts_in, 16)
                for i in range(B // NIM):
                    sp.dma_start(IM[:, i * NIM:(i + 1) * NIM, :],
                                 d["x"][i * NIM:(i + 1) * NIM].rearrange("b r c -> r b c")).then_inc(img_in[i], 16)
                tok_rows = tok_dram.rearrange("(t p x) c -> t p (x c)", p=P, x=SIDE)
                for t in range(NG // 2):
                    sp.wait_ge(tok_ready, t + 1)
                    sp.dma_start(tok_rows[t], HT[:, t, :]).then_inc(tok_out, 16)
                sp.wait_ge(tok_out, 16 * (NG // 2))
                sp.dma_start(H[:], tok_dram.rearrange("(t p) c -> p t c", p=P)).then_inc(tok_in, 16)
                sp.wait_ge(tok_in, 16)

            @block.scalar
            def _(act):
                for dst, name in ((RAW[:, 0, :], "L0_attn_Wq"), (RAW[:, 1, :], "L0_attn_Wk"), (RAW[:, 2, :], "L0_attn_Wv"),
                                  (RAW[:, 3, :], "L0_attn_WoT"), (RAW[:, 4, :], "L0_ffn_wq"), (WKR[:], "L0_ffn_wk"),
                                  (WV0R[:], "L0_ffn_wvT"), (WO0[:], "L0_ffn_woT"), (WQKV[:], "L1_qkv"), (WG[:], "L1_gate"),
                                  (WOUT[:], "L1_out"), (RW[:], "router"), (LNW[:], "ln_w"), (BTOK[:], "tok_b"),
                                  (BOUT[:], "bout"), (GAMMA[:], "gamma"), (BETA[:], "beta"), (LQ[:], "lam_q")):
                    act.dma_start(dst, d[name]).then_inc(weights_in, 16)
                act.wait_ge(w_step, 3)
                nc.scalar.activation(LE[:], LS[:], ACT.Exp).then_inc(lam_exp, 1)
                for i in range(B // 16):
                    act.wait_ge(rows_mm, i + 1)
                    nc.scalar.activation(A1[:, i * 16:(i + 1) * 16, :].rearrange("p b o -> p (b o)"),
                                         PS[:, i % 4, :], ACT.Copy).then_inc(rows_copied, 1)
                    act.wait_ge(cols_mm, i + 1)
                    nc.scalar.activation(A2[:, :, i * P:(i + 1) * P].rearrange("p o (b y) -> p b o y", b=16),
                                         PS[0:32, 4 + i % 2, :].rearrange("p (b o y) -> p b o y", o=NOP, y=SIDE),
                                         ACT.Copy).then_inc(cols_copied, 1)

            @block.tensor
            def _(pe):
                pe.wait_ge(consts_in, 32)
                for ro in range(NOP):
                    last = nc.tensor.matmul(PS[0:32, 7, ro * C:(ro + 1) * C],
                                            k("map_sel", NF)[:, ro * 32:(ro + 1) * 32], WT[:], start=True, stop=True)
                last.then_inc(prep_mm, 1)
                pe.wait_ge(weights_in, 16 * 18)
                for col, lhs, rhs, n in ((0, RAW[:, 0, :], RAW[:, 1, :], C), (64, RAW[:, 2, :], RAW[:, 3, :], C),
                                         (128, RAW[:, 4, :], k("q_sel", C), P), (256, WKR[:], k("k_sel", 32), P)):
                    last = nc.tensor.matmul(PS[0:C, 6, col:col + n], lhs, rhs, start=True, stop=True)
                last.then_inc(prep_mm, 1)
                for i in range(B // 16):
                    for b in range(16):
                        im = i * 16 + b
                        if im % NIM == 0:
                            pe.wait_ge(img_in[im // NIM], 16)
                        last = nc.tensor.matmul(PS[:, i % 4, b * 32:(b + 1) * 32], IM[:, im, :], k("ops_t"),
                                                start=True, stop=True)
                    last.then_inc(rows_mm, 1)
                    pe.wait_ge(rows_copied, i + 1)
                    if i >= 2:
                        pe.wait_ge(cols_copied, i - 1)
                    nc.tensor.matmul(PS[0:32, 4 + i % 2, :], k("ops_t"),
                                     A1[:, i * 16:(i + 1) * 16, :].rearrange("p b o -> p (b o)"),
                                     start=True, stop=True).then_inc(cols_mm, 1)
                pe.wait_ge(wd_ready, 1)
                for t in range(NG // 2):
                    pe.wait_ge(cols_copied, t + 1)
                    for ro in range(NOP):
                        last = nc.tensor.matmul(PS[:, t, :], A2[:, ro, t * P:(t + 1) * P],
                                                WD[:, ro, :, :].rearrange("p x c -> p (x c)"),
                                                start=(ro == 0), stop=(ro == NOP - 1))
                    last.then_inc(tok_mm, 1)

            @block.vector
            def _(dve):
                dve.wait_ge(weights_in, 16 * 18)
                nc.vector.memset(NHALF[:], -0.5).then_inc(consts_ok, 1)
                nc.vector.tensor_tensor(LP[:], LQ[:, 0::2, :], LQ[:, 1::2, :], ALU.mult).then_inc(w_step, 1)
                dve.wait_ge(w_step, 1)
                nc.vector.tensor_reduce(LS[:], LP[:], op=ALU.add, axis=AX.X).then_inc(w_step, 2)
                dve.wait_ge(prep_mm, 1)
                nc.vector.tensor_copy(WX[:], PS[0:32, 7, 0:256].rearrange("p (o c) -> p o c", o=NOP)).then_inc(w_step, 1)
                dve.wait_ge(w_step, 4)
                for ro in range(NOP):
                    last = nc.vector.tensor_tensor(WD[:, ro, :, :], over(WX[:, ro, :], SIDE), bc(k("x_diag", 32), C), ALU.mult)
                last.then_inc(wd_ready, 1)
                wv = WQKV[:, 512:768].rearrange("p (h e) -> p h e", h=NH1)
                nc.vector.tensor_reduce(VM[:], wv, op=ALU.add, axis=AX.X).then_inc(w_step, 1)
                dve.wait_ge(w_step, 5)
                nc.vector.scalar_tensor_tensor(out=wv, in0=bc(VM[:], DV), scalar=-1.0 / DV, in1=wv, op0=ALU.mult, op1=ALU.add)
                nc.vector.tensor_scalar(GAMMA[:], GAMMA[:], 0.5 * (1 - LAMBDA_INIT), None, ALU.mult)
                nc.vector.tensor_scalar(BETA[:], BETA[:], 0.5 * (1 - LAMBDA_INIT), None, ALU.mult)
                dve.wait_ge(lam_exp, 1)
                nc.vector.scalar_tensor_tensor(out=LAM[:], in0=LE[:, 1:2], scalar=-LAMBDA_INIT, in1=LE[:, 0:1],
                                               op0=ALU.add, op1=ALU.subtract)
                dve.wait_ge(prep_mm, 2)
                nc.vector.tensor_copy(M1[:], PS[0:C, 6, 0:64])
                nc.vector.tensor_copy(M2[:], PS[0:C, 6, 64:128])
                nc.vector.tensor_scalar(WQ2[:], PS[0:C, 6, 128:256], LNW[:, 0:1], HD ** -0.5, ALU.mult, ALU.mult)
                nc.vector.tensor_scalar(WK2[:], PS[0:C, 6, 256:384], LNW[:, 0:1], None, ALU.mult)
                nc.vector.tensor_scalar(WV0[:], WV0R[:], LNW[:, 0:1], None, ALU.mult).then_inc(prep_done, 1)
                for t in range(NG // 2):
                    dve.wait_ge(tok_mm, t + 1)
                    nc.vector.tensor_tensor(HT[:, t, :].rearrange("p (x c) -> p x c", x=SIDE),
                                            PS[:, t, :].rearrange("p (x c) -> p x c", x=SIDE),
                                            over(BTOK[:], SIDE), ALU.add).then_inc(tok_ready, 1)

        X2 = tile(top, "X2", [P, NT, C])
        XS = tile(top, "XS", [P, NTOK], F16)
        LG = tile(top, "LG", [P, NT, NE])
        GATES = tile(top, "GATES", [P, NE, NT])

        def wait_apart(pe, what, n):
            n = pe.snap(pe.to_reg(n))
            pe.wait_ge(consts_ok, 1)
            pe.wait_ge(what, n)

        class Norm:
            def __init__(self, ctx, name):
                self.total, self.ssq, self.var, self.rstd = (
                    tile(ctx, f"{name}_{f}", [P, STREAMS, GT]) for f in ("total", "ssq", "var", "rstd"))
                self.cen, self.sq, self.z = (tile(ctx, f"{name}_{f}", [P, STREAMS, GT, C]) for f in ("cen", "sq", "z"))
                self.total_ok, self.cen_ok, self.sq_ok, self.ssq_ok, self.var_ok, self.rstd_ok, self.z_ok = (
                    sem(ctx, f"{name}_{f}_ok") for f in ("total", "cen", "sq", "ssq", "var", "rstd", "z"))

            def centre(self, dve, s, n, src):
                nc.vector.tensor_reduce(self.total[:, s], src, op=ALU.add, axis=AX.X).then_inc(self.total_ok, 1)
                dve.wait_ge(self.total_ok, n)
                nc.vector.scalar_tensor_tensor(out=self.cen[:, s], in0=bc(self.total[:, s], C), scalar=-1.0 / C,
                                               in1=src, op0=ALU.mult, op1=ALU.add).then_inc(self.cen_ok, 1)

            def square(self, act, s, n):
                act.wait_ge(self.cen_ok, n)
                nc.scalar.activation(self.sq[:, s], self.cen[:, s], ACT.Square).then_inc(self.sq_ok, 1)

            def variance(self, dve, s, n, eps):
                dve.wait_ge(self.sq_ok, n)
                nc.vector.tensor_reduce(self.ssq[:, s], self.sq[:, s], op=ALU.add, axis=AX.X).then_inc(self.ssq_ok, 1)
                dve.wait_ge(self.ssq_ok, n)
                nc.vector.tensor_scalar(self.var[:, s], self.ssq[:, s], 1.0 / C, eps, ALU.mult, ALU.add).then_inc(self.var_ok, 1)

            def power(self, pool, s, n):
                pool.wait_ge(self.var_ok, n)
                nc.gpsimd.tensor_tensor(self.rstd[:, s], self.var[:, s], NHALF[:, 0:GT], ALU.pow).then_inc(self.rstd_ok, 1)

            def scale(self, dve, s, n):
                dve.wait_ge(self.rstd_ok, n)
                nc.vector.tensor_tensor(self.z[:, s], self.cen[:, s], bc(self.rstd[:, s], C), ALU.mult).then_inc(self.z_ok, 1)

        def tiles(a, g):
            return a[:, bass.ds(g * GT, GT), :]

        with ExitStack() as ctx:
            ln = Norm(ctx, "b_ln")
            zT = tile(ctx, "b_zT", [C, STREAMS, GTOK])
            uT = tile(ctx, "b_uT", [C, STREAMS, GTOK])
            val = tile(ctx, "b_val", [P, STREAMS, GT, C])
            att = tile(ctx, "b_att", [P, STREAMS, GT, P])
            zT_mm, zT_ok, u_mm, u_ok, v_mm, v_ok, sc_mm, att_ok, ctx_mm, h_ok = (
                sem(ctx, "b_" + n) for n in ("zT_mm", "zT_ok", "u_mm", "u_ok", "v_mm", "v_ok", "sc_mm", "att_ok", "ctx_mm", "h_ok"))
            block = phase_block(ctx)

            @block.vector
            def _(dve):
                with dve.Fori(0, NG // STREAMS) as it:
                    ns = [it * STREAMS + s + 1 for s in range(STREAMS)]
                    hs = [tiles(H, it * STREAMS + s) for s in range(STREAMS)]
                    for s, n in enumerate(ns):
                        ln.centre(dve, s, n, hs[s])
                    for s, n in enumerate(ns):
                        ln.variance(dve, s, n, LN_EPS)
                    for s, n in enumerate(ns):
                        ln.scale(dve, s, n)
                    for s, n in enumerate(ns):
                        dve.wait_ge(v_mm, n)
                        nc.vector.tensor_copy(val[:, s], PS[:, 4 * s + 2, 0:GT * C].rearrange("p (t c) -> p t c", c=C)).then_inc(v_ok, 1)
                    for s, n in enumerate(ns):
                        dve.wait_ge(sc_mm, n)
                        nc.vector.scalar_tensor_tensor(
                            out=att[:, s], in0=PS[:, 4 * s + 3, :].rearrange("p (t l) -> p t l", l=P), scalar=0.0,
                            in1=over(k("lin_mask"), GT), op0=ALU.max, op1=ALU.mult).then_inc(att_ok, 1)
                    for s, n in enumerate(ns):
                        dve.wait_ge(ctx_mm, n)
                        nc.vector.tensor_tensor(hs[s], hs[s], PS[:, 4 * s, 0:GT * C].rearrange("p (t c) -> p t c", c=C),
                                                ALU.add).then_inc(h_ok, 1)

            @block.scalar
            def _(act):
                with act.Fori(0, NG // STREAMS) as it:
                    ns = [it * STREAMS + s + 1 for s in range(STREAMS)]
                    for s, n in enumerate(ns):
                        ln.square(act, s, n)
                    for s, n in enumerate(ns):
                        act.wait_ge(zT_mm, n)
                        nc.scalar.activation(zT[:, s], PS[0:C, 4 * s, :], ACT.Copy).then_inc(zT_ok, 1)
                    for s, n in enumerate(ns):
                        act.wait_ge(u_mm, n)
                        nc.scalar.activation(uT[:, s], PS[0:C, 4 * s + 1, :], ACT.Copy).then_inc(u_ok, 1)

            @block.gpsimd
            def _(pool):
                with pool.Fori(0, NG // STREAMS) as it:
                    for s in range(STREAMS):
                        ln.power(pool, s, it * STREAMS + s + 1)

            @block.tensor
            def _(pe):
                with pe.Fori(0, NG // STREAMS) as it:
                    ns = [it * STREAMS + s + 1 for s in range(STREAMS)]
                    for s, n in enumerate(ns):
                        wait_apart(pe, ln.z_ok, n)
                        for t in range(GT):
                            last = nc.tensor.transpose(PS[0:C, 4 * s, t * P:(t + 1) * P], ln.z[:, s, t, :], ident)
                        last.then_inc(zT_mm, 1)
                    for s, n in enumerate(ns):
                        wait_apart(pe, zT_ok, n)
                        nc.tensor.matmul(PS[0:C, 4 * s + 1, :], M1[:], zT[:, s], start=True, stop=True).then_inc(u_mm, 1)
                        for t in range(GT):
                            last = nc.tensor.matmul(PS[:, 4 * s + 2, t * C:(t + 1) * C], zT[:, s, t * P:(t + 1) * P], M2[:],
                                                    start=True, stop=True)
                        last.then_inc(v_mm, 1)
                    for s, n in enumerate(ns):
                        pe.wait_ge(u_ok, n)
                        for t in range(GT):
                            last = nc.tensor.matmul(PS[:, 4 * s + 3, t * P:(t + 1) * P], zT[:, s, t * P:(t + 1) * P],
                                                    uT[:, s, t * P:(t + 1) * P], start=True, stop=True)
                        last.then_inc(sc_mm, 1)
                    for s, n in enumerate(ns):
                        pe.wait_ge(att_ok, n)
                        pe.wait_ge(v_ok, n)
                        for t in range(GT):
                            last = nc.tensor.matmul(PS[:, 4 * s, t * C:(t + 1) * C], att[:, s, t, :], val[:, s, t, :],
                                                    start=True, stop=True)
                        last.then_inc(ctx_mm, 1)

        with ExitStack() as ctx:
            ln = Norm(ctx, "c_ln")
            rq = tile(ctx, "c_rq", [P, STREAMS, GT])
            rr = tile(ctx, "c_rr", [P, STREAMS, GT])
            vz = tile(ctx, "c_vz", [P, STREAMS, GT])
            nz = tile(ctx, "c_nz", [P, STREAMS, GT, C])
            nT = tile(ctx, "c_nT", [C, STREAMS, GTOK])
            q2 = tile(ctx, "c_q2", [P, STREAMS, GTOK])
            k2 = tile(ctx, "c_k2", [P, STREAMS, GTOK])
            kb = tile(ctx, "c_kb", [P, STREAMS, GB, NH0, L])
            vb = tile(ctx, "c_vb", [P, STREAMS, GB, 2, 2, HD + 1])
            sc = tile(ctx, "c_sc", [P, STREAMS, GT * NH0, L])
            mx = tile(ctx, "c_mx", [P, STREAMS, GT * NH0])
            eT = tile(ctx, "c_eT", [P, STREAMS, GT, 2, P])
            rs = tile(ctx, "c_rs", [P, STREAMS, GT * NH0])
            y = tile(ctx, "c_y", [P, STREAMS, GT, C])
            yT = tile(ctx, "c_yT", [C, STREAMS, GTOK])
            names = ("vz_ok", "rq_ok", "rr_ok", "nz_ok", "nT_mm", "nT_ok", "q_mm", "k_mm", "v_mm", "q_ok", "k_ok", "kr_mm",
                     "kb_ok", "vb_ok", "sc_mm", "sm_ok", "mx_ok", "sub_ok", "exp_ok", "eT_mm", "eT_ok", "av_mm", "rs_ok", "y_ok",
                     "yT_mm", "yT_ok", "o_mm", "x2_ok", "h_ok", "init")
            (vz_ok, rq_ok, rr_ok, nz_ok, nT_mm, nT_ok, q_mm, k_mm, v_mm, q_ok, k_ok, kr_mm, kb_ok, vb_ok, sc_mm, sm_ok, mx_ok,
             sub_ok, exp_ok, eT_mm, eT_ok, av_mm, rs_ok, y_ok, yT_mm, yT_ok, o_mm, x2_ok, h_ok, init) = (sem(ctx, "c_" + n) for n in names)
            block = phase_block(ctx)

            def by_seq(ap):
                return ap.rearrange("p (b l) -> p b l", l=L)

            @block.vector
            def _(dve):
                with dve.Fori(0, NG // STREAMS) as it:
                    ns = [it * STREAMS + s + 1 for s in range(STREAMS)]
                    gs = [it * STREAMS + s for s in range(STREAMS)]
                    for s, n in enumerate(ns):
                        ln.centre(dve, s, n, tiles(H, gs[s]))
                    for s, n in enumerate(ns):
                        ln.variance(dve, s, n, LN_EPS)
                    for s, n in enumerate(ns):
                        ln.scale(dve, s, n)
                        nc.vector.scalar_tensor_tensor(out=vz[:, s], in0=ln.ssq[:, s], scalar=1.0 / C, in1=ln.rstd[:, s],
                                                       op0=ALU.mult, op1=ALU.mult).then_inc(vz_ok, 1)
                        dve.wait_ge(vz_ok, 2 * n - 1)
                        nc.vector.tensor_tensor(vz[:, s], vz[:, s], ln.rstd[:, s], ALU.mult).then_inc(vz_ok, 1)
                        dve.wait_ge(vz_ok, 2 * n)
                        nc.vector.tensor_scalar(rq[:, s], vz[:, s], RMS_EPS, None, ALU.add).then_inc(rq_ok, 1)
                    for s, n in enumerate(ns):
                        dve.wait_ge(rr_ok, n)
                        nc.vector.tensor_tensor(nz[:, s], ln.z[:, s], bc(rr[:, s], C), ALU.mult).then_inc(nz_ok, 1)
                    for s, n in enumerate(ns):
                        for mm, dst, bank, ok in ((q_mm, q2, 1, q_ok), (k_mm, k2, 2, k_ok)):
                            dve.wait_ge(mm, n)
                            nc.vector.tensor_tensor(by_seq(dst[:, s]), by_seq(PS[:, 4 * s + bank, :]), over(k("cos_sin"), GB),
                                                    ALU.mult).then_inc(ok, 1)
                    for s, n in enumerate(ns):
                        dve.wait_ge(v_mm, n)
                        for h in range(2):
                            last = nc.vector.tensor_copy(vb[h * L:(h + 1) * L, s, :, :, h, 0:HD],
                                                         PS[h * L:(h + 1) * L, 4 * s, 0:GB * 32].rearrange("p (b k e) -> p b k e", k=2, e=HD))
                        last.then_inc(vb_ok, 1)
                    for s, n in enumerate(ns):
                        dve.wait_ge(sc_mm, n)
                        s4 = PS[:, 4 * s + 1:4 * s + 3, :].rearrange("p k (h l) -> p (k h) l", l=L)
                        nc.vector.tensor_tensor(sc[:, s], s4, over(k("causal"), GT * NH0), ALU.add).then_inc(sm_ok, 1)
                        dve.wait_ge(sm_ok, n)
                        nc.vector.tensor_reduce(mx[:, s], sc[:, s], op=ALU.max, axis=AX.X).then_inc(mx_ok, 1)
                        dve.wait_ge(mx_ok, n)
                        nc.vector.tensor_tensor(sc[:, s], sc[:, s], bc(mx[:, s], L), ALU.subtract).then_inc(sub_ok, 1)
                    for s, n in enumerate(ns):
                        dve.wait_ge(av_mm, n)
                        av = PS[:, 4 * s, 0:GT * NH0 * (HD + 1)].rearrange("p (h e) -> p h e", e=HD + 1)
                        nc.vector.reciprocal(rs[:, s], av[:, :, HD]).then_inc(rs_ok, 1)
                        dve.wait_ge(rs_ok, n)
                        nc.vector.tensor_tensor(y[:, s].rearrange("p t (h e) -> p (t h) e", e=HD), av[:, :, 0:HD],
                                                bc(rs[:, s], HD), ALU.mult).then_inc(y_ok, 1)
                    for s, n in enumerate(ns):
                        dve.wait_ge(o_mm, n)
                        x2 = tiles(X2, gs[s])
                        nc.vector.tensor_tensor(x2, ln.z[:, s], PS[:, 4 * s, 0:GT * C].rearrange("p (t c) -> p t c", c=C),
                                                ALU.add).then_inc(x2_ok, 1)
                        dve.wait_ge(x2_ok, n)
                        h = tiles(H, gs[s])
                        nc.vector.tensor_tensor(h, h, x2, ALU.add).then_inc(h_ok, 1)

            @block.scalar
            def _(act):
                with act.Fori(0, NG // STREAMS) as it:
                    ns = [it * STREAMS + s + 1 for s in range(STREAMS)]
                    for s, n in enumerate(ns):
                        ln.square(act, s, n)
                    for s, n in enumerate(ns):
                        act.wait_ge(nT_mm, n)
                        nc.scalar.activation(nT[:, s], PS[0:C, 4 * s, :], ACT.Copy).then_inc(nT_ok, 1)
                    for s, n in enumerate(ns):
                        act.wait_ge(kr_mm, n)
                        for h in range(NH0):
                            last = nc.scalar.activation(kb[:, s, :, h, :], by_seq(PS[:, 4 * s + 3, :]), ACT.Copy,
                                                        scale=k("head_mask")[:, h:h + 1])
                        last.then_inc(kb_ok, 1)
                    for s, n in enumerate(ns):
                        act.wait_ge(sub_ok, n)
                        nc.scalar.activation(sc[:, s], sc[:, s], ACT.Exp).then_inc(exp_ok, 1)
                    for s, n in enumerate(ns):
                        act.wait_ge(eT_mm, n)
                        nc.scalar.activation(eT[:, s].rearrange("p t k l -> p (t k l)"),
                                             PS[:, 4 * s + 1:4 * s + 3, :].rearrange("p k n -> p (k n)"), ACT.Copy).then_inc(eT_ok, 1)
                    for s, n in enumerate(ns):
                        act.wait_ge(yT_mm, n)
                        nc.scalar.activation(yT[:, s], PS[0:C, 4 * s + 3, :], ACT.Copy).then_inc(yT_ok, 1)

            @block.gpsimd
            def _(pool):
                nc.gpsimd.memset(vb[:], 0.0).then_inc(init, 1)
                pool.wait_ge(init, 1)
                for h in range(2):
                    nc.gpsimd.memset(vb[h * L:(h + 1) * L, :, :, :, h, HD:HD + 1], 1.0).then_inc(init, 1)
                    pool.wait_ge(init, h + 2)
                with pool.Fori(0, NG // STREAMS) as it:
                    ns = [it * STREAMS + s + 1 for s in range(STREAMS)]
                    for s, n in enumerate(ns):
                        ln.power(pool, s, n)
                    for s, n in enumerate(ns):
                        pool.wait_ge(rq_ok, n)
                        nc.gpsimd.tensor_tensor(rr[:, s], rq[:, s], NHALF[:, 0:GT], ALU.pow).then_inc(rr_ok, 1)

            @block.tensor
            def _(pe):
                pe.wait_ge(init, 3)
                with pe.Fori(0, NG // STREAMS) as it:
                    ns = [it * STREAMS + s + 1 for s in range(STREAMS)]
                    for s, n in enumerate(ns):
                        wait_apart(pe, nz_ok, n)
                        for t in range(GT):
                            last = nc.tensor.transpose(PS[0:C, 4 * s, t * P:(t + 1) * P], nz[:, s, t, :], ident)
                        last.then_inc(nT_mm, 1)
                    for s, n in enumerate(ns):
                        pe.wait_ge(nT_ok, n)
                        nc.tensor.matmul(PS[:, 4 * s + 1, :], WQ2[:], nT[:, s], start=True, stop=True).then_inc(q_mm, 1)
                        nc.tensor.matmul(PS[:, 4 * s + 2, :], WK2[:], nT[:, s], start=True, stop=True).then_inc(k_mm, 1)
                        for b in range(GB):
                            for h in range(2):
                                last = nc.tensor.matmul(PS[h * L:(h + 1) * L, 4 * s, b * 32:(b + 1) * 32], nT[:, s, b * L:(b + 1) * L],
                                                        WV0[:], start=True, stop=True)
                        last.then_inc(v_mm, 1)
                    for s, n in enumerate(ns):
                        pe.wait_ge(k_ok, n)
                        nc.tensor.matmul(PS[:, 4 * s + 3, :], k("fold"), k2[:, s], start=True, stop=True).then_inc(kr_mm, 1)
                    for s, n in enumerate(ns):
                        wait_apart(pe, q_ok, n)
                        pe.wait_ge(kb_ok, n)
                        for b in range(GB):
                            at = (b // 2) * NH0 * L
                            last = nc.tensor.matmul(PS[b % 2 * L:(b % 2 + 1) * L, 4 * s + 1 + at // 512, at % 512:at % 512 + NH0 * L],
                                                    q2[:, s, b * L:(b + 1) * L], kb[:, s, b].rearrange("p h l -> p (h l)"),
                                                    start=True, stop=True)
                        last.then_inc(sc_mm, 1)
                    for s, n in enumerate(ns):
                        pe.wait_ge(exp_ok, n)
                        for t in range(GT):
                            for m in range(2):
                                i = 2 * t + m
                                last = nc.tensor.transpose(PS[:, 4 * s + 1 + i // 4, i % 4 * P:(i % 4 + 1) * P],
                                                           sc[:, s, 2 * i:2 * i + 2, :].rearrange("p h l -> p (h l)"), ident)
                        last.then_inc(eT_mm, 1)
                    for s, n in enumerate(ns):
                        pe.wait_ge(eT_ok, n)
                        pe.wait_ge(vb_ok, n)
                        for b in range(GB):
                            for m in range(2):
                                at = ((b // 2) * 2 + m) * 2 * (HD + 1)
                                last = nc.tensor.matmul(PS[b % 2 * L:(b % 2 + 1) * L, 4 * s, at:at + 2 * (HD + 1)],
                                                        eT[:, s, b // 2, m, b % 2 * L:(b % 2 + 1) * L],
                                                        vb[:, s, b, m].rearrange("p h e -> p (h e)"), start=True, stop=True)
                        last.then_inc(av_mm, 1)
                    for s, n in enumerate(ns):
                        wait_apart(pe, y_ok, n)
                        for t in range(GT):
                            last = nc.tensor.transpose(PS[0:C, 4 * s + 3, t * P:(t + 1) * P], y[:, s, t, :], ident)
                        last.then_inc(yT_mm, 1)
                    for s, n in enumerate(ns):
                        pe.wait_ge(yT_ok, n)
                        for t in range(GT):
                            last = nc.tensor.matmul(PS[:, 4 * s, t * C:(t + 1) * C], yT[:, s, t * P:(t + 1) * P], WO0[:],
                                                    start=True, stop=True)
                        last.then_inc(o_mm, 1)

        def features(layer):
            src = X2 if layer == 0 else H
            with ExitStack() as ctx:
                nm = f"f{layer}"
                ln = Norm(ctx, nm + "_ln")
                fT = tile(ctx, nm + "_fT", [C, STREAMS, GTOK])
                fT_mm, fT_ok, hi_ok, lo_ok, lg_mm, lg_ok = (sem(ctx, f"{nm}_{n}") for n in ("fT_mm", "fT_ok", "hi_ok", "lo_ok", "lg_mm", "lg_ok"))
                block = phase_block(ctx)

                @block.vector
                def _(dve):
                    with dve.Fori(0, NG // STREAMS) as it:
                        ns = [it * STREAMS + s + 1 for s in range(STREAMS)]
                        gs = [it * STREAMS + s for s in range(STREAMS)]
                        for s, n in enumerate(ns):
                            if layer == 0:
                                nc.vector.tensor_copy(ln.cen[:, s], tiles(src, gs[s])).then_inc(ln.cen_ok, 1)
                            else:
                                ln.centre(dve, s, n, tiles(src, gs[s]))
                        for s, n in enumerate(ns):
                            ln.variance(dve, s, n, RMS_EPS if layer == 0 else LN_EPS)
                        for s, n in enumerate(ns):
                            ln.scale(dve, s, n)
                        for s, n in enumerate(ns):
                            dve.wait_ge(fT_ok, n)
                            dve.wait_ge(hi_ok, n)
                            at = bass.ds(gs[s] * GTOK, GTOK)
                            nc.vector.tensor_tensor(XS[C:P, at], fT[:, s], XS[0:C, at], ALU.subtract).then_inc(lo_ok, 1)
                        for s, n in enumerate(ns):
                            dve.wait_ge(lg_mm, n)
                            nc.vector.tensor_copy(tiles(LG, gs[s]), PS[:, 4 * s + 1, 0:GT * NE].rearrange("p (t e) -> p t e", e=NE)).then_inc(lg_ok, 1)

                @block.scalar
                def _(act):
                    with act.Fori(0, NG // STREAMS) as it:
                        ns = [it * STREAMS + s + 1 for s in range(STREAMS)]
                        for s, n in enumerate(ns):
                            ln.square(act, s, n)
                        for s, n in enumerate(ns):
                            act.wait_ge(fT_mm, n)
                            scale = LNW[:, 1:2] if layer == 0 else 1.0
                            nc.scalar.activation(fT[:, s], PS[0:C, 4 * s, :], ACT.Copy, scale=scale).then_inc(fT_ok, 1)
                            nc.scalar.activation(XS[0:C, bass.ds((it * STREAMS + s) * GTOK, GTOK)], PS[0:C, 4 * s, :], ACT.Copy,
                                                 scale=scale).then_inc(hi_ok, 1)

                @block.gpsimd
                def _(pool):
                    with pool.Fori(0, NG // STREAMS) as it:
                        for s in range(STREAMS):
                            ln.power(pool, s, it * STREAMS + s + 1)

                @block.tensor
                def _(pe):
                    with pe.Fori(0, NG // STREAMS) as it:
                        ns = [it * STREAMS + s + 1 for s in range(STREAMS)]
                        for s, n in enumerate(ns):
                            wait_apart(pe, ln.z_ok, n)
                            for t in range(GT):
                                last = nc.tensor.transpose(PS[0:C, 4 * s, t * P:(t + 1) * P], ln.z[:, s, t, :], ident)
                            last.then_inc(fT_mm, 1)
                        for s, n in enumerate(ns):
                            pe.wait_ge(fT_ok, n)
                            pe.wait_ge(hi_ok, n)
                            for t in range(GT):
                                last = nc.tensor.matmul(PS[:, 4 * s + 1, t * NE:(t + 1) * NE], fT[:, s, t * P:(t + 1) * P],
                                                        RW[:, layer, :], start=True, stop=True)
                            last.then_inc(lg_mm, 1)

        def experts(layer):
            hid = HID0 if layer == 0 else HID1
            full, rest = hid // P, hid % P
            wcols = (2 * full + 1) * P
            if layer == 0:
                body = [(s, j, (3 * s + 2 * j, 3 * s + 1)) for s in range(STREAMS) for j in range(full + 1)]
            else:
                body = [(s, j, (2 * (j % 3), 2 * (j % 3) + 1)) for s in range(STREAMS) for j in range(full + 1)]
            NU, LAG, HB = len(body), 2, 3
            YB, TB = 6, 7
            with ExitStack() as ctx:
                nm = f"x{layer}"
                stage = tile(ctx, nm + "_stage", [P, 2, wcols])
                whi = tile(ctx, nm + "_whi", [P, 2, wcols], F16)
                wlo = tile(ctx, nm + "_wlo", [P, 2, wcols], F16)
                w2 = tile(ctx, nm + "_w2", [P, 2, full + 1, C])
                sil = tile(ctx, nm + "_sil", [P, HB, GTOK])
                hid_t = tile(ctx, nm + "_hid", [P, HB, GTOK])
                yT = tile(ctx, nm + "_yT", [P, 2, GTOK])
                gy = tile(ctx, nm + "_gy", [P, 2, GT, C])
                rt = {n: tile(ctx, f"{nm}_{n}", [P, NT, NE]) for n in ("e", "p", "w", "one1", "p2", "one2")}
                rv = {n: tile(ctx, f"{nm}_{n}", [P, NT]) for n in ("mx", "sum", "m1", "m2", "wm", "den")}
                whi_ok, wlo_ok, up_mm, sil_ok, hid_ok, y_mm, yT_ok, yt_mm, gy_ok, h_ok, r_step, r_exp, scaled = (
                    sem(ctx, f"{nm}_{n}") for n in ("whi_ok", "wlo_ok", "up_mm", "sil_ok", "hid_ok", "y_mm", "yT_ok", "yt_mm",
                                                     "gy_ok", "h_ok", "r_step", "r_exp", "scaled"))
                w_in, w2_in = ([sem(ctx, f"{nm}_{n}{i}") for i in range(2)] for n in ("w_in", "w2_in"))
                block = phase_block(ctx)
                GP = NG // STREAMS

                @block.sync
                def _(sp):
                    w13, w2d = d[f"w13_{layer}"], d[f"w2_{layer}"]
                    for e in range(NE):
                        if e >= 2:
                            sp.wait_ge(wlo_ok, e - 1)
                        sp.dma_start(stage[:, e % 2, :], w13[e]).then_inc(w_in[e % 2], 16)
                        if e >= 2:
                            sp.wait_ge(gy_ok, NG * (e - 1))
                        sp.dma_start(w2[:, e % 2], w2d[e]).then_inc(w2_in[e % 2], 16)

                @block.gpsimd
                def _(pool):
                    for e in range(NE):
                        pool.wait_ge(whi_ok, e + 1)
                        nc.gpsimd.tensor_scalar(stage[:, e % 2], stage[:, e % 2], WSCALE, None, ALU.mult).then_inc(scaled, 1)
                        pool.wait_ge(scaled, e + 1)
                        nc.gpsimd.tensor_tensor(wlo[:, e % 2], stage[:, e % 2], whi[:, e % 2], ALU.subtract).then_inc(wlo_ok, 1)

                @block.scalar
                def _(act):
                    act.wait_ge(r_step, 2)
                    nc.scalar.activation(rt["e"][:], rt["e"][:], ACT.Exp).then_inc(r_exp, 1)
                    act.wait_ge(w_in[0], 16)
                    nc.scalar.activation(whi[:, 0], stage[:, 0], ACT.Copy, scale=WSCALE).then_inc(whi_ok, 1)
                    for e in range(NE):
                        if e + 1 < NE:
                            act.wait_ge(w_in[(e + 1) % 2], 16 * ((e + 1) // 2 + 1))
                            if e >= 1:
                                act.wait_ge(gy_ok, NG * e)
                            nc.scalar.activation(whi[:, (e + 1) % 2], stage[:, (e + 1) % 2], ACT.Copy, scale=WSCALE).then_inc(whi_ok, 1)
                        with act.Fori(0, GP) as it:
                            def out_copy(s):
                                i = it * STREAMS + s + e * NG
                                act.wait_ge(y_mm, i + 1)
                                nc.scalar.activation(yT[:, s], PS[:, YB, :], ACT.Copy).then_inc(yT_ok, 1)

                            for u, (s, j, banks) in enumerate(body):
                                q = it * NU + e * GP * NU + u
                                act.wait_ge(up_mm, q + 1)
                                rows = P if j < full else rest
                                nc.scalar.activation(sil[0:rows, u % HB], PS[0:rows, banks[0], :], ACT.Silu,
                                                     scale=1.0 / WSCALE).then_inc(sil_ok, 1)
                                if s == 1 and j == (LAG if full >= LAG else full):
                                    out_copy(0)
                            out_copy(1)

                @block.tensor
                def _(pe):
                    for e in range(NE):
                        pe.wait_ge(wlo_ok, e + 1)
                        pe.wait_ge(w2_in[e % 2], 16 * (e // 2 + 1))
                        with pe.Fori(0, GP) as it:
                            def up(u):
                                s, j, banks = body[u]
                                xs = XS[:, bass.ds((it * STREAMS + s) * GTOK, GTOK)]
                                parts = ((banks[0], j * P), (banks[1], (full + j) * P)) if j < full else ((banks[0], 2 * full * P),)
                                for bank, col in parts:
                                    nc.tensor.matmul(PS[:, bank, :], whi[:, e % 2, col:col + P], xs, start=True, stop=False)
                                    last = nc.tensor.matmul(PS[:, bank, :], wlo[:, e % 2, col:col + P], xs, start=False, stop=True)
                                last.then_inc(up_mm, 1)

                            def down(u):
                                s, j, _ = body[u]
                                q = it * NU + e * GP * NU + u
                                i = it * STREAMS + s + e * NG
                                wait_apart(pe, hid_ok, q + 1)
                                rows = P if j < full else rest
                                half = j % 2 * C
                                last = nc.tensor.matmul(PS[half:half + C, YB, :], w2[0:rows, e % 2, j, :], hid_t[0:rows, u % HB, :],
                                                        start=(j < 2), stop=(j + 2 > full))
                                if j == full:
                                    last.then_inc(y_mm, 1)

                            def turn(s):
                                i = it * STREAMS + s + e * NG
                                pe.wait_ge(yT_ok, i + 1)
                                if s == 1:
                                    pe.wait_ge(gy_ok, i)
                                for t in range(GT):
                                    last = nc.tensor.matmul(PS[:, TB, t * C:(t + 1) * C], yT[:, s, t * P:(t + 1) * P],
                                                            k("fold")[:, 0:C], start=True, stop=True)
                                last.then_inc(yt_mm, 1)

                            for u in range(LAG):
                                up(u)
                            for u in range(NU):
                                if u + LAG < NU:
                                    up(u + LAG)
                                if u == full + 1:
                                    turn(0)
                                down(u)
                            turn(1)
                            pe.wait_ge(gy_ok, it * STREAMS + e * NG + 2)

                @block.vector
                def _(dve):
                    lg = LG[:]
                    r_at = [0]

                    def step(ins):
                        r_at[0] += 1
                        ins.then_inc(r_step, 1)
                        dve.wait_ge(r_step, r_at[0])

                    step(nc.vector.tensor_reduce(rv["mx"][:], lg, op=ALU.max, axis=AX.X))
                    step(nc.vector.tensor_tensor(rt["e"][:], lg, bc(rv["mx"][:], NE), ALU.subtract))
                    dve.wait_ge(r_exp, 1)
                    step(nc.vector.tensor_reduce(rv["sum"][:], rt["e"][:], op=ALU.add, axis=AX.X))
                    step(nc.vector.reciprocal(rv["sum"][:], rv["sum"][:]))
                    step(nc.vector.tensor_tensor(rt["p"][:], rt["e"][:], bc(rv["sum"][:], NE), ALU.mult))

                    def pick(prob, top, one):
                        step(nc.vector.tensor_reduce(rv[top][:], prob[:], op=ALU.max, axis=AX.X))
                        step(nc.vector.tensor_tensor(rt["w"][:], prob[:], bc(rv[top][:], NE), ALU.is_equal))
                        step(nc.vector.tensor_tensor(rt["w"][:], rt["w"][:], over(k("first"), NT), ALU.mult))
                        step(nc.vector.tensor_reduce(rv["wm"][:], rt["w"][:], op=ALU.max, axis=AX.X))
                        step(nc.vector.tensor_tensor(rt[one][:], rt["w"][:], bc(rv["wm"][:], NE), ALU.is_equal))

                    pick(rt["p"], "m1", "one1")
                    step(nc.vector.scalar_tensor_tensor(out=rt["p2"][:], in0=rt["one1"][:], scalar=-2.0, in1=rt["p"][:], op0=ALU.mult, op1=ALU.add))
                    pick(rt["p2"], "m2", "one2")
                    step(nc.vector.tensor_tensor(rt["one1"][:], rt["one1"][:], rt["one2"][:], ALU.add))
                    step(nc.vector.tensor_tensor(rt["p"][:], rt["p"][:], rt["one1"][:], ALU.mult))
                    step(nc.vector.scalar_tensor_tensor(out=rv["den"][:], in0=rv["m1"][:], scalar=1e-9, in1=rv["m2"][:], op0=ALU.add, op1=ALU.add))
                    step(nc.vector.reciprocal(rv["den"][:], rv["den"][:]))
                    step(nc.vector.tensor_scalar(rv["den"][:], rv["den"][:], 1.0 / WSCALE, None, ALU.mult))
                    step(nc.vector.tensor_tensor(GATES[:].rearrange("p e t -> p t e"), rt["p"][:], bc(rv["den"][:], NE), ALU.mult))
                    for e in range(NE):
                        with dve.Fori(0, GP) as it:
                            def gated(s):
                                i = it * STREAMS + s + e * NG
                                dve.wait_ge(yt_mm, i + 1)
                                gate = GATES[:, e, bass.ds((it * STREAMS + s) * GT, GT)]
                                nc.vector.tensor_tensor(gy[:, s], PS[:, TB, 0:GT * C].rearrange("p (t c) -> p t c", c=C), bc(gate, C),
                                                        ALU.mult).then_inc(gy_ok, 1)
                                dve.wait_ge(gy_ok, i + 1)
                                h = tiles(H, it * STREAMS + s)
                                nc.vector.tensor_tensor(h, h, gy[:, s], ALU.add).then_inc(h_ok, 1)

                            for u, (s, j, banks) in enumerate(body):
                                q = it * NU + e * GP * NU + u
                                dve.wait_ge(sil_ok, q + 1)
                                if j < full:
                                    nc.vector.tensor_tensor(hid_t[:, u % HB], sil[:, u % HB], PS[:, banks[1], :], ALU.mult).then_inc(hid_ok, 1)
                                else:
                                    nc.vector.tensor_tensor(hid_t[0:rest, u % HB], sil[0:rest, u % HB], PS[C:C + rest, banks[0], :],
                                                            ALU.mult).then_inc(hid_ok, 1)
                                if s == 1 and j == (LAG if full >= LAG else full):
                                    gated(0)
                            gated(1)

        features(0)
        experts(0)

        with ExitStack() as ctx:
            ln = Norm(ctx, "e_ln")
            HP = 2 * NH1
            BLK = 2 * L
            zT = tile(ctx, "e_zT", [C + 1, GTOK])
            qT = tile(ctx, "e_qT", [P, 2, GTOK])
            kb = tile(ctx, "e_kb", [P, GB, 2, 4, L])
            vb = tile(ctx, "e_vb", [P, GB, NH1, 2, DV + 1])
            tg = tile(ctx, "e_tg", [P, GT, 256])
            sc = tile(ctx, "e_sc", [P, 2, HP, L])
            mx = tile(ctx, "e_mx", [P, 2, HP])
            eT = tile(ctx, "e_eT", [P, 2, NH1, P])
            rs = tile(ctx, "e_rs", [P, NH1, 2])
            o2 = tile(ctx, "e_o2", [P, 2, NH1, 2, DV])
            o = tile(ctx, "e_o", [P, GT, NH1, DV])
            osq = tile(ctx, "e_osq", [P, GT, NH1, DV])
            ov = tile(ctx, "e_ov", [P, GT * NH1])
            orr = tile(ctx, "e_or", [P, GT * NH1])
            oT = tile(ctx, "e_oT", [P, GT, 2, P])
            ob = tile(ctx, "e_ob", [P, GT, C])
            names = ("init", "zT_mm", "zT_ok", "q_mm", "k_mm", "g_mm", "q_ok", "kb_ok", "tg_ok", "v_mm", "vb_ok", "sc_mm", "mx_ok",
                     "sub_ok", "exp_ok", "eT_mm", "eT_ok", "av_mm", "rs_ok", "lam_ok", "o2_ok", "o_ok", "osq_ok", "ov_ok", "var_ok",
                     "or_ok", "on_ok", "gam_ok", "bet_ok", "og_ok", "oT_mm", "oT_ok", "out_mm", "ob_ok", "h_ok")
            (init, zT_mm, zT_ok, q_mm, k_mm, g_mm, q_ok, kb_ok, tg_ok, v_mm, vb_ok, sc_mm, mx_ok, sub_ok, exp_ok, eT_mm, eT_ok,
             av_mm, rs_ok, lam_ok, o2_ok, o_ok, osq_ok, ov_ok, var_ok, or_ok, on_ok, gam_ok, bet_ok, og_ok, oT_mm, oT_ok, out_mm,
             ob_ok, h_ok) = (sem(ctx, "e_" + n) for n in names)
            block = phase_block(ctx)

            def sbank(t):
                return 2 * (t % 2)

            @block.vector
            def _(dve):
                with dve.Fori(0, NG) as it:
                    n = it + 1
                    ln.centre(dve, 0, n, tiles(H, it))
                    ln.variance(dve, 0, n, LN_EPS)
                    ln.scale(dve, 0, n)

                    def softmax(t):
                        m = it * GT + t + 1
                        s4 = PS[:, sbank(t):sbank(t) + 2, :].rearrange("p k (h l) -> p (k h) l", l=L)
                        dve.wait_ge(sc_mm, m)
                        nc.vector.tensor_reduce(mx[:, t % 2], s4, op=ALU.max, axis=AX.X).then_inc(mx_ok, 1)
                        dve.wait_ge(mx_ok, m)
                        nc.vector.tensor_tensor(sc[:, t % 2], s4, bc(mx[:, t % 2], L), ALU.subtract).then_inc(sub_ok, 1)

                    def combine(t):
                        m = it * GT + t + 1
                        dve.wait_ge(av_mm, m)
                        av = PS[:, 6:8, 0:4 * 2 * (DV + 1)].rearrange("p k (m e) -> p k m e", e=DV + 1)
                        nc.vector.reciprocal(rs[:].rearrange("p (k m) u -> p k (m u)", k=2), av[:, :, :, DV]).then_inc(rs_ok, 1)
                        dve.wait_ge(rs_ok, m)
                        nc.vector.tensor_scalar(rs[:, :, 1], rs[:, :, 1], LAM[:], None, ALU.mult).then_inc(lam_ok, 1)
                        dve.wait_ge(lam_ok, m)
                        if t >= 2:
                            dve.wait_ge(o_ok, it * GT + t - 1)
                        for kk in range(2):
                            last = nc.vector.tensor_tensor(
                                o2[:, t % 2, 4 * kk:4 * kk + 4].rearrange("p m u e -> p (m u) e"), av[:, kk, :, 0:DV],
                                bc(rs[:, 4 * kk:4 * kk + 4, :].rearrange("p m u -> p (m u)"), DV), ALU.mult)
                        last.then_inc(o2_ok, 1)

                    softmax(0)
                    for t in range(1, GT):
                        softmax(t)
                        combine(t - 1)
                    combine(GT - 1)
                    dve.wait_ge(osq_ok, n)
                    nc.vector.tensor_reduce(ov[:], osq[:].rearrange("p t m e -> p (t m) e"), op=ALU.add, axis=AX.X).then_inc(ov_ok, 1)
                    dve.wait_ge(ov_ok, n)
                    nc.vector.tensor_scalar(ov[:], ov[:], 1.0 / DV, LN_EPS, ALU.mult, ALU.add).then_inc(var_ok, 1)
                    dve.wait_ge(or_ok, n)
                    om = o[:].rearrange("p t m e -> p (t m) e")
                    nc.vector.tensor_tensor(om, om, bc(orr[:], DV), ALU.mult).then_inc(on_ok, 1)
                    dve.wait_ge(bet_ok, n)
                    nc.vector.scalar_tensor_tensor(out=tg[:], in0=tg[:], scalar=1.0, in1=o[:].rearrange("p t m e -> p t (m e)"),
                                                   op0=ALU.add, op1=ALU.mult).then_inc(og_ok, 1)
                    dve.wait_ge(out_mm, n)
                    nc.vector.tensor_tensor(ob[:], PS[:, 4, 0:GT * C].rearrange("p (t c) -> p t c", c=C), over(BOUT[:], GT),
                                            ALU.add).then_inc(ob_ok, 1)
                    dve.wait_ge(ob_ok, n)
                    h = tiles(H, it)
                    nc.vector.tensor_tensor(h, h, ob[:], ALU.add).then_inc(h_ok, 1)
                    dve.wait_ge(h_ok, n)

            @block.gpsimd
            def _(pool):
                nc.gpsimd.memset(vb[:], 0.0).then_inc(init, 1)
                pool.wait_ge(init, 1)
                nc.gpsimd.memset(zT[C:C + 1, :], 1.0).then_inc(init, 1)
                pool.wait_ge(init, 2)
                for u in range(2):
                    nc.gpsimd.memset(vb[u * L:(u + 1) * L, :, :, u, DV:DV + 1], 1.0).then_inc(init, 1)
                    pool.wait_ge(init, u + 3)
                with pool.Fori(0, NG) as it:
                    n = it + 1
                    ln.power(pool, 0, n)
                    for t in range(GT):
                        m = it * GT + t + 1
                        pool.wait_ge(o2_ok, m)
                        nc.gpsimd.tensor_tensor(o[:, t], o2[:, t % 2, :, 0, :], o2[:, t % 2, :, 1, :], ALU.add).then_inc(o_ok, 1)
                    pool.wait_ge(o_ok, GT * n)
                    nc.gpsimd.tensor_tensor(osq[:], o[:], o[:], ALU.mult).then_inc(osq_ok, 1)
                    pool.wait_ge(var_ok, n)
                    nc.gpsimd.tensor_tensor(orr[:], ov[:], NHALF[:, 0:GT * NH1], ALU.pow).then_inc(or_ok, 1)
                    pool.wait_ge(on_ok, n)
                    om = o[:].rearrange("p t m e -> p (t m) e")
                    nc.gpsimd.tensor_tensor(om, om, over(GAMMA[:], GT * NH1), ALU.mult).then_inc(gam_ok, 1)
                    pool.wait_ge(gam_ok, n)
                    nc.gpsimd.tensor_tensor(om, om, over(BETA[:], GT * NH1), ALU.add).then_inc(bet_ok, 1)

            @block.scalar
            def _(act):
                with act.Fori(0, NG) as it:
                    n = it + 1
                    ln.square(act, 0, n)
                    act.wait_ge(zT_mm, n)
                    nc.scalar.activation(zT[0:C, :], PS[0:C, 4, :], ACT.Copy).then_inc(zT_ok, 1)
                    act.wait_ge(q_mm, n)
                    nc.scalar.activation(qT[:].rearrange("p k n -> p (k n)"), PS[:, 0:2, :].rearrange("p k n -> p (k n)"), ACT.Copy,
                                         scale=HD ** -0.5).then_inc(q_ok, 1)
                    act.wait_ge(k_mm, n)
                    for hf in range(2):
                        for h in range(4):
                            last = nc.scalar.activation(kb[:, :, hf, h, :], PS[:, 2 + hf, :].rearrange("p (b l) -> p b l", l=L), ACT.Copy,
                                                        scale=k("head_mask")[:, h:h + 1])
                    last.then_inc(kb_ok, 1)
                    act.wait_ge(v_mm, n)
                    for kk in range(2):
                        for u in range(2):
                            last = nc.scalar.activation(vb[u * L:(u + 1) * L, 4 * kk:4 * kk + 4, :, u, 0:DV],
                                                        PS[u * L:(u + 1) * L, 2 * kk:2 * kk + 2, :].rearrange("p k (b m e) -> p (k b) m e", m=NH1, e=DV), ACT.Copy)
                    last.then_inc(vb_ok, 1)
                    act.wait_ge(g_mm, n)
                    nc.scalar.activation(tg[:].rearrange("p t n -> p (t n)"), PS[:, 6:8, :].rearrange("p k n -> p (k n)"), ACT.Tanh,
                                         scale=0.5).then_inc(tg_ok, 1)

                    def exps(t):
                        act.wait_ge(sub_ok, it * GT + t + 1)
                        nc.scalar.activation(sc[:, t % 2], sc[:, t % 2], ACT.Exp).then_inc(exp_ok, 1)

                    def turned(t):
                        act.wait_ge(eT_mm, it * GT + t + 1)
                        nc.scalar.activation(eT[:, t % 2].rearrange("p m l -> p (m l)"), PS[:, 4:6, :].rearrange("p k n -> p (k n)"),
                                             ACT.Copy).then_inc(eT_ok, 1)

                    exps(0)
                    for t in range(1, GT):
                        turned(t - 1)
                        exps(t)
                    turned(GT - 1)
                    act.wait_ge(oT_mm, n)
                    nc.scalar.activation(oT[:].rearrange("p t k l -> p (t k l)"), PS[:, 0:2, :].rearrange("p k n -> p (k n)"),
                                         ACT.Copy).then_inc(oT_ok, 1)

            @block.tensor
            def _(pe):
                pe.wait_ge(init, 4)
                with pe.Fori(0, NG) as it:
                    n = it + 1
                    wait_apart(pe, ln.z_ok, n)
                    for t in range(GT):
                        last = nc.tensor.transpose(PS[0:C, 4, t * P:(t + 1) * P], ln.z[:, 0, t, :], ident)
                    last.then_inc(zT_mm, 1)
                    wait_apart(pe, zT_ok, n)
                    for col in range(2):
                        last = nc.tensor.matmul(PS[:, col, :], WQKV[:, col * P:(col + 1) * P], zT[0:C, :], start=True, stop=True)
                    last.then_inc(q_mm, 1)
                    for col in range(2, 4):
                        last = nc.tensor.matmul(PS[:, col, :], WQKV[:, col * P:(col + 1) * P], zT[0:C, :], start=True, stop=True)
                    last.then_inc(k_mm, 1)
                    for t in range(GT):
                        last = nc.tensor.matmul(PS[:, 6 + t // 2, t % 2 * 256:(t % 2 + 1) * 256], zT[:, t * P:(t + 1) * P], WG[:],
                                                start=True, stop=True)
                    last.then_inc(g_mm, 1)
                    wait_apart(pe, q_ok, n)
                    pe.wait_ge(kb_ok, n)
                    for b in range(GB):
                        for u in range(2):
                            last = nc.tensor.matmul(PS[u * L:(u + 1) * L, b // 2, b % 2 * 256:(b % 2 + 1) * 256],
                                                    zT[0:C, b * L:(b + 1) * L], WQKV[:, 512:768], start=True, stop=True)
                    last.then_inc(v_mm, 1)
                    wait_apart(pe, vb_ok, n)

                    def scores(t):
                        for hf in range(2):
                            for r in range(2):
                                for b in range(2):
                                    last = nc.tensor.matmul(
                                        PS[b * L:(b + 1) * L, sbank(t) + r, hf * 256:(hf + 1) * 256],
                                        qT[r * L:(r + 1) * L, hf, (2 * t + b) * L:(2 * t + b + 1) * L],
                                        kb[r * L:(r + 1) * L, 2 * t + b, hf].rearrange("p h l -> p (h l)"), start=True, stop=True)
                        last.then_inc(sc_mm, 1)

                    def turn(t):
                        pe.wait_ge(exp_ok, it * GT + t + 1)
                        for m in range(NH1):
                            last = nc.tensor.transpose(PS[:, 4 + m // 4, m % 4 * P:(m % 4 + 1) * P],
                                                       sc[:, t % 2, 2 * m:2 * m + 2, :].rearrange("p h l -> p (h l)"), ident)
                        last.then_inc(eT_mm, 1)

                    def weigh(t):
                        pe.wait_ge(eT_ok, it * GT + t + 1)
                        if t == 0:
                            pe.wait_ge(tg_ok, n)
                        else:
                            pe.wait_ge(o2_ok, it * GT + t)
                        for b in range(2):
                            for c in range(NH1):
                                r, hf = c // 4, c % 4 // 2
                                m = hf * 4 + r * 2 + c % 2
                                last = nc.tensor.matmul(
                                    PS[b * L:(b + 1) * L, 6 + m // 4, m % 4 * 2 * (DV + 1):(m % 4 + 1) * 2 * (DV + 1)],
                                    eT[:, t % 2, c, b * L:(b + 1) * L], vb[:, 2 * t + b, m].rearrange("p u e -> p (u e)"),
                                    start=True, stop=True)
                        last.then_inc(av_mm, 1)

                    scores(0)
                    scores(1)
                    for t in range(GT):
                        turn(t)
                        if t + 2 < GT:
                            scores(t + 2)
                        weigh(t)
                    pe.wait_ge(og_ok, n)
                    for t in range(GT):
                        for hf in range(2):
                            i = 2 * t + hf
                            last = nc.tensor.transpose(PS[:, i // 4, i % 4 * P:(i % 4 + 1) * P], tg[:, t, hf * P:(hf + 1) * P], ident)
                    last.then_inc(oT_mm, 1)
                    pe.wait_ge(oT_ok, n)
                    for t in range(GT):
                        for hf in range(2):
                            last = nc.tensor.matmul(PS[:, 4, t * C:(t + 1) * C], oT[:, t, hf, :], WOUT[:, hf, :],
                                                    start=(hf == 0), stop=(hf == 1))
                    last.then_inc(out_mm, 1)

        features(1)
        experts(1)

        with ExitStack() as ctx:
            out_done = sem(ctx, "out_done")
            block = phase_block(ctx)

            @block.sync
            def _(sp):
                sp.dma_start(out.rearrange("(t p) c -> p t c", p=P), H[:]).then_inc(out_done, 16)
                sp.wait_ge(out_done, 16)


def kernel(**inputs):
    import numpy as _np
    import concourse.bacc as _bacc
    from concourse import mybir as _mybir
    from concourse.bass_utils import run_bass_kernel_spmd as _run

    a = {n: _np.asarray(v) for n, v in inputs.items()}
    consts, cols = constants()

    def rows(v):
        return _np.broadcast_to(v[None], (P,) + v.shape)

    def up_weights(w1, w3):
        ne, hid, c = w1.shape
        full = hid // P * P
        t1, t3 = w1.transpose(0, 2, 1), w3.transpose(0, 2, 1)
        last = _np.zeros((ne, c, P), w1.dtype)
        last[:, :, 0:hid - full] = t1[:, :, full:]
        last[:, :, C:C + hid - full] = t3[:, :, full:]
        one = _np.concatenate([t1[:, :, :full], t3[:, :, :full], last], 2)
        return _np.concatenate([one, one], 1)

    def down_weights(w2):
        ne, c, hid = w2.shape
        chunks = hid // P + 1
        t = _np.zeros((ne, chunks * P, c), w2.dtype)
        t[:, :hid] = w2.transpose(0, 2, 1)
        return t.reshape(ne, chunks, P, c).transpose(0, 2, 1, 3)

    host = {
        "consts": consts,
        "x": a["x"][:, 0],
        "L0_tok_W": a["L0_tok_W"],
        "L0_attn_Wq": a["L0_attn_Wq"], "L0_attn_Wk": a["L0_attn_Wk"], "L0_attn_Wv": a["L0_attn_Wv"],
        "L0_attn_WoT": a["L0_attn_Wo"].T,
        "L0_ffn_wq": a["L0_ffn_wq"], "L0_ffn_wk": a["L0_ffn_wk"],
        "L0_ffn_wvT": a["L0_ffn_wv"].T, "L0_ffn_woT": a["L0_ffn_wo"].T,
        "L1_qkv": _np.concatenate([a["L1_attn_Wq"], a["L1_attn_Wkv"]], 1),
        "L1_gate": _np.concatenate([a["L1_attn_Wg"], a["L1_attn_bg"][None]], 0),
        "L1_out": a["L1_attn_Wout"].reshape(2, P, C).transpose(1, 0, 2),
        "router": _np.stack([a["L0_ffn_router_w"].T, a["L1_ffn_router_w"].T], 1),
        "ln_w": _np.stack([a["L0_ffn_ln1_w"], a["L0_ffn_ln2_w"]], 1),
        "tok_b": rows(a["L0_tok_b"]), "bout": rows(a["L1_attn_bout"]),
        "gamma": rows(a["L1_attn_ln_gamma"]), "beta": rows(a["L1_attn_ln_beta"]),
        "lam_q": rows(_np.stack([a["L1_attn_lq1"], a["L1_attn_lk1"], a["L1_attn_lq2"], a["L1_attn_lk2"]])),
        "w13_0": up_weights(a["L0_ffn_w1"], a["L0_ffn_w3"]), "w2_0": down_weights(a["L0_ffn_w2"]),
        "w13_1": up_weights(a["L1_ffn_w1"], a["L1_ffn_w3"]), "w2_1": down_weights(a["L1_ffn_w2"]),
    }
    nc = _bacc.Bacc("TRN2", target_bir_lowering=False, num_devices=1)
    arrays, dram = {}, {}
    for name, v in host.items():
        v = _np.ascontiguousarray(v)
        arrays[f"in_{name}"] = v
        dram[name] = nc.dram_tensor(f"in_{name}", v.shape, _mybir.dt.from_np(v.dtype), kind="ExternalInput").ap()
    out = nc.dram_tensor("out", (NTOK, C), _mybir.dt.float32, kind="ExternalOutput").ap()
    build(nc, dram, out, cols)
    r = _run(nc, [arrays], core_ids=[0])
    return r.results[0]["out"].reshape(B, L, C)
```

```python
import math

import numpy as np
import concourse.bass as bass
from concourse import mybir
from contextlib import ExitStack

B = 64
IMG = 128
SIDE = 8
L = SIDE * SIDE
C = 64
P = 128
NTOK = B * L
NT = NTOK // P
GT = 4
NG = NT // GT
GTOK = GT * P
GB = GTOK // L
NF = 7
NOP = 4
NE = 8
HID0, HID1 = 170, 682
NH0, HD = 4, 16
NH1 = 8
DV = 32
LAMBDA_INIT = 0.8 - 0.6 * math.exp(-0.3)
LN_EPS, RMS_EPS = 1e-5, 1e-6
WSCALE = 64.0
STREAMS = 2
ETOK = 256
NET = 40
RW_ = C + 2
assert NET % 8 == 0 and NET * ETOK >= 2 * NTOK + (NE - 1) * ETOK

MAPS = [(0, 0), (1, 0), (0, 1), (1, 1), (3, 2), (2, 3), (3, 3)]


def constants():
    def resize(n):
        scale = n / SIDE
        centre = (np.arange(SIDE) + 0.5) * scale - 0.5
        w = np.maximum(0, 1 - np.abs(centre[None, :] - np.arange(n)[:, None]) / scale)
        return (w / w.sum(0, keepdims=True)).T

    def haar(n, sign):
        m = np.zeros((n // 2, n))
        m[np.arange(n // 2), 2 * np.arange(n // 2)] = 1
        m[np.arange(n // 2), 2 * np.arange(n // 2) + 1] = sign
        return m * 0.7071067811865476

    ops = np.concatenate([resize(IMG // 4) @ haar(IMG // 2, 1) @ haar(IMG, 1),
                          resize(IMG // 4) @ haar(IMG // 2, -1) @ haar(IMG, 1),
                          resize(IMG // 2) @ haar(IMG, 1),
                          resize(IMG // 2) @ haar(IMG, -1)])
    parts = {}

    def add(name, a):
        full = np.zeros((P, a.shape[1]), np.float32)
        full[:a.shape[0]] = a
        parts[name] = full

    p = np.arange(P)
    add("ident", np.eye(P))
    add("fold", (p[:, None] % C == p[None, :] % C).astype(float))
    add("ops_t", ops.T)
    sel = np.zeros((NF, NOP, NOP * SIDE))
    for f, (ro, co) in enumerate(MAPS):
        sel[f, ro, co * SIDE:(co + 1) * SIDE] = 1
    add("map_sel", sel.reshape(NF, -1))
    add("x_diag", (p[:NOP * SIDE, None] % SIDE == np.arange(SIDE)[None, :]).astype(float))
    same = (p[:, None] // L == p[None, :] // L) & (p[:, None] <= p[None, :])
    add("lin_mask", same / np.maximum(p[None, :] % L, 1))
    inv_freq = 1.0 / 10000.0 ** (np.arange(0, HD, 2, dtype=np.float32) / HD)
    angle = np.outer(np.arange(L, dtype=np.float32), inv_freq).astype(np.float32)
    angle = np.concatenate([angle, angle], -1).T
    add("cos_sin", np.concatenate([np.tile(np.cos(angle), (NH0, 1)), np.tile(np.sin(angle), (NH0, 1))]))
    rot = np.zeros((HD, HD))
    rot[np.arange(8), np.arange(8) + 8] = -1
    rot[np.arange(8) + 8, np.arange(8)] = 1
    q_rot = np.kron(np.eye(NH0), rot)
    add("q_sel", np.concatenate([np.eye(C), q_rot.T], 1))
    rep = np.zeros((C, C // 2))
    for h in range(NH0):
        rep[h * HD:(h + 1) * HD, (h // 2) * HD:(h // 2 + 1) * HD] = np.eye(HD)
    add("k_sel", np.concatenate([rep.T, (q_rot @ rep).T], 1))
    add("causal", np.where(p[:, None] % L >= np.arange(L)[None, :], 0.0, -1e30))
    add("head_mask", ((p[:, None] % C) // HD == np.arange(NH0)[None, :]).astype(float))
    add("before", (p[:, None] < p[None, :]).astype(float))
    add("ones", np.ones((P, P)))
    add("token", p[:, None] + P * np.arange(2 * NT)[None, :])
    add("tile_at", np.tile(ETOK * np.arange(NET, dtype=float), (P, 1)))
    add("first", np.tile(np.arange(NE, 0, -1.0), (P, 1)))
    cols, at = {}, 0
    for name, a in parts.items():
        cols[name] = (at, at + a.shape[1])
        at += a.shape[1]
    return np.concatenate(list(parts.values()), 1).astype(np.float32), cols


def build(nc, d, out, cols):
    F32, F16, I32, U32 = mybir.dt.float32, mybir.dt.float16, mybir.dt.int32, mybir.dt.uint32
    ALU, ACT, AX = mybir.AluOpType, mybir.ActivationFunctionType, mybir.AxisListType
    with ExitStack() as top:
        def tile(ctx, name, shape, dt=F32):
            return ctx.enter_context(nc.sbuf_tensor(name, shape, dt))

        phase_sems = []

        def sem(ctx, name):
            s = ctx.enter_context(nc.semaphore(name))
            if ctx is not top:
                phase_sems.append(s)
            return s

        def phase_block(ctx):
            def clear():
                for s in phase_sems:
                    nc.gpsimd.sem_clear(s)
                phase_sems.clear()
                nc.all_engine_barrier()

            ctx.callback(clear)
            return ctx.enter_context(nc.Block())

        def bc(ap, dims):
            return ap.unsqueeze(2).broadcast_to(list(ap.shape) + [dims])

        def over(ap, n):
            return ap.unsqueeze(1).broadcast_to([ap.shape[0], n, ap.shape[1]])

        PS = top.enter_context(nc.psum_tensor("PS", [P, 8, 512], F32))
        H = tile(top, "H", [P, NT, C])
        KC = tile(top, "KC", [P, sum(b - a for a, b in [cols[k] for k in cols])])

        def k(name, rows=P):
            a, b = cols[name]
            return KC[0:rows, a:b]

        ident = k("ident")
        M1 = tile(top, "M1", [C, C])
        M2 = tile(top, "M2", [C, C])
        WQ2 = tile(top, "WQ2", [C, P])
        WK2 = tile(top, "WK2", [C, P])
        WV0 = tile(top, "WV0", [C, 32])
        WO0 = tile(top, "WO0", [C, C])
        WQKV = tile(top, "WQKV", [C, 768])
        WG = tile(top, "WG", [C + 1, 256])
        WOUT = tile(top, "WOUT", [P, 2, C])
        RW = tile(top, "RW", [C, 2, NE])
        LNW = tile(top, "LNW", [C, 2])
        BTOK = tile(top, "BTOK", [P, C])
        BOUT = tile(top, "BOUT", [P, C])
        WOUT2 = tile(top, "WOUT2", [P, 2, 2, C])
        LNH = tile(top, "LNH", [P, 2])
        LAMU = tile(top, "LAMU", [P, 1])
        QMASK = tile(top, "QMASK", [P, NH0])
        NHALF = tile(top, "NHALF", [P, NT * 8])

        consts_ok = sem(top, "consts_ok")

        with ExitStack() as ctx:
            IM = tile(ctx, "IM", [P, B, IMG])
            A1 = tile(ctx, "A1", [P, B, NOP * SIDE])
            A2 = tile(ctx, "A2", [NOP * SIDE, NOP, B * SIDE])
            WT = tile(ctx, "WT", [NF, C])
            WX = tile(ctx, "WX", [NOP * SIDE, NOP, C])
            WD = tile(ctx, "WD", [NOP * SIDE, NOP, SIDE, C])
            HT = tile(ctx, "HT", [P, NG // 2, SIDE * C])
            RAW = tile(ctx, "RAW", [C, 7, C])
            WKR = tile(ctx, "WKR", [32, C])
            WV0R = tile(ctx, "WV0R", [C, 32])
            VM = tile(ctx, "VM", [C, NH1])
            LQ = tile(ctx, "LQ", [P, 4, HD])
            LP = tile(ctx, "LP", [P, 2, HD])
            LS = tile(ctx, "LS", [P, 2])
            LE = tile(ctx, "LE", [P, 2])
            tok_dram = nc.dram_tensor("tok_scratch", (NTOK, C), F32, kind="Internal").ap()
            NIM = 8
            img_in = [sem(ctx, f"img_in{i}") for i in range(B // NIM)]
            consts_in, weights_in = sem(ctx, "consts_in"), sem(ctx, "weights_in")
            prep_mm, prep_done, w_step = sem(ctx, "prep_mm"), sem(ctx, "prep_done"), sem(ctx, "w_step")
            lam_exp = sem(ctx, "lam_exp")
            rows_mm, rows_copied = sem(ctx, "rows_mm"), sem(ctx, "rows_copied")
            cols_mm, cols_copied = sem(ctx, "cols_mm"), sem(ctx, "cols_copied")
            tok_mm, tok_ready, tok_out, tok_in = (sem(ctx, n) for n in ("tok_mm", "tok_ready", "tok_out", "tok_in"))
            wd_ready = sem(ctx, "wd_ready")
            NWL = 17
            block = phase_block(ctx)

            @block.sync
            def _(sp):
                sp.dma_start(KC[:], d["consts"]).then_inc(consts_in, 16)
                sp.dma_start(WT[:], d["L0_tok_W"]).then_inc(consts_in, 16)
                for i in range(B // NIM):
                    sp.dma_start(IM[:, i * NIM:(i + 1) * NIM, :],
                                 d["x"][i * NIM:(i + 1) * NIM].rearrange("b r c -> r b c")).then_inc(img_in[i], 16)
                tok_rows = tok_dram.rearrange("(t p x) c -> t p (x c)", p=P, x=SIDE)
                for t in range(NG // 2):
                    sp.wait_ge(tok_ready, t + 1)
                    sp.dma_start(tok_rows[t], HT[:, t, :]).then_inc(tok_out, 16)
                sp.wait_ge(tok_out, 16 * (NG // 2))
                sp.dma_start(H[:], tok_dram.rearrange("(t p) c -> p t c", p=P)).then_inc(tok_in, 16)
                sp.wait_ge(tok_in, 16)

            @block.scalar
            def _(act):
                for dst, name in ((RAW[:, 0, :], "L0_attn_Wq"), (RAW[:, 1, :], "L0_attn_Wk"), (RAW[:, 2, :], "L0_attn_Wv"),
                                  (RAW[:, 3, :], "L0_attn_WoT"), (RAW[:, 4, :], "L0_ffn_wq"), (WKR[:], "L0_ffn_wk"),
                                  (WV0R[:], "L0_ffn_wvT"), (WO0[:], "L0_ffn_woT"), (WQKV[:], "L1_qkv"), (WG[:], "L1_gate"),
                                  (WOUT[:], "L1_out"), (RW[:], "router"), (LNW[:], "ln_w"), (BTOK[:], "tok_b"),
                                  (BOUT[:], "bout"), (LNH[:], "ln_head"), (LQ[:], "lam_q")):
                    act.dma_start(dst, d[name]).then_inc(weights_in, 16)
                act.wait_ge(w_step, 3)
                nc.scalar.activation(LE[:], LS[:], ACT.Exp).then_inc(lam_exp, 1)
                for i in range(B // 16):
                    act.wait_ge(rows_mm, i + 1)
                    nc.scalar.activation(A1[:, i * 16:(i + 1) * 16, :].rearrange("p b o -> p (b o)"),
                                         PS[:, i % 4, :], ACT.Copy).then_inc(rows_copied, 1)
                    act.wait_ge(cols_mm, i + 1)
                    nc.scalar.activation(A2[:, :, i * P:(i + 1) * P].rearrange("p o (b y) -> p b o y", b=16),
                                         PS[0:32, 4 + i % 2, :].rearrange("p (b o y) -> p b o y", o=NOP, y=SIDE),
                                         ACT.Copy).then_inc(cols_copied, 1)

            @block.tensor
            def _(pe):
                pe.wait_ge(consts_in, 32)
                for ro in range(NOP):
                    last = nc.tensor.matmul(PS[0:32, 7, ro * C:(ro + 1) * C],
                                            k("map_sel", NF)[:, ro * 32:(ro + 1) * 32], WT[:], start=True, stop=True)
                last.then_inc(prep_mm, 1)
                pe.wait_ge(weights_in, 16 * NWL)
                for col, lhs, rhs, n in ((0, RAW[:, 0, :], RAW[:, 1, :], C), (64, RAW[:, 2, :], RAW[:, 3, :], C),
                                         (128, RAW[:, 4, :], k("q_sel", C), P), (256, WKR[:], k("k_sel", 32), P)):
                    last = nc.tensor.matmul(PS[0:C, 6, col:col + n], lhs, rhs, start=True, stop=True)
                last.then_inc(prep_mm, 1)
                for i in range(B // 16):
                    for b in range(16):
                        im = i * 16 + b
                        if im % NIM == 0:
                            pe.wait_ge(img_in[im // NIM], 16)
                        last = nc.tensor.matmul(PS[:, i % 4, b * 32:(b + 1) * 32], IM[:, im, :], k("ops_t"),
                                                start=True, stop=True)
                    last.then_inc(rows_mm, 1)
                    pe.wait_ge(rows_copied, i + 1)
                    if i >= 2:
                        pe.wait_ge(cols_copied, i - 1)
                    nc.tensor.matmul(PS[0:32, 4 + i % 2, :], k("ops_t"),
                                     A1[:, i * 16:(i + 1) * 16, :].rearrange("p b o -> p (b o)"),
                                     start=True, stop=True).then_inc(cols_mm, 1)
                pe.wait_ge(wd_ready, 1)
                for t in range(NG // 2):
                    pe.wait_ge(cols_copied, t + 1)
                    for ro in range(NOP):
                        last = nc.tensor.matmul(PS[:, t, :], A2[:, ro, t * P:(t + 1) * P],
                                                WD[:, ro, :, :].rearrange("p x c -> p (x c)"),
                                                start=(ro == 0), stop=(ro == NOP - 1))
                    last.then_inc(tok_mm, 1)

            @block.vector
            def _(dve):
                dve.wait_ge(weights_in, 16 * NWL)
                nc.vector.memset(NHALF[:], -0.5).then_inc(consts_ok, 1)
                nc.vector.tensor_tensor(LP[:], LQ[:, 0::2, :], LQ[:, 1::2, :], ALU.mult).then_inc(w_step, 1)
                dve.wait_ge(w_step, 1)
                nc.vector.tensor_reduce(LS[:], LP[:], op=ALU.add, axis=AX.X).then_inc(w_step, 2)
                dve.wait_ge(prep_mm, 1)
                nc.vector.tensor_copy(WX[:], PS[0:32, 7, 0:256].rearrange("p (o c) -> p o c", o=NOP)).then_inc(w_step, 1)
                dve.wait_ge(w_step, 4)
                for ro in range(NOP):
                    last = nc.vector.tensor_tensor(WD[:, ro, :, :], over(WX[:, ro, :], SIDE), bc(k("x_diag", 32), C), ALU.mult)
                last.then_inc(wd_ready, 1)
                wv = WQKV[:, 512:768].rearrange("p (h e) -> p h e", h=NH1)
                nc.vector.tensor_reduce(VM[:], wv, op=ALU.add, axis=AX.X).then_inc(w_step, 1)
                dve.wait_ge(w_step, 5)
                nc.vector.scalar_tensor_tensor(out=wv, in0=bc(VM[:], DV), scalar=-1.0 / DV, in1=wv, op0=ALU.mult, op1=ALU.add)
                for w in range(2):
                    nc.vector.tensor_scalar(WOUT2[:, w], WOUT[:], LNH[:, w:w + 1], 1 - LAMBDA_INIT, ALU.mult, ALU.mult)
                nc.vector.tensor_scalar(QMASK[:], k("head_mask"), HD ** -0.5, None, ALU.mult)
                nc.vector.memset(LAMU[0:L], 1.0)
                dve.wait_ge(lam_exp, 1)
                nc.vector.scalar_tensor_tensor(out=LAMU[L:P], in0=LE[L:P, 1:2], scalar=-LAMBDA_INIT, in1=LE[L:P, 0:1],
                                               op0=ALU.add, op1=ALU.subtract)
                dve.wait_ge(prep_mm, 2)
                nc.vector.tensor_copy(M1[:], PS[0:C, 6, 0:64])
                nc.vector.tensor_copy(M2[:], PS[0:C, 6, 64:128])
                nc.vector.tensor_scalar(WQ2[:], PS[0:C, 6, 128:256], LNW[:, 0:1], HD ** -0.5, ALU.mult, ALU.mult)
                nc.vector.tensor_scalar(WK2[:], PS[0:C, 6, 256:384], LNW[:, 0:1], None, ALU.mult)
                nc.vector.tensor_scalar(WV0[:], WV0R[:], LNW[:, 0:1], None, ALU.mult).then_inc(prep_done, 1)
                for t in range(NG // 2):
                    dve.wait_ge(tok_mm, t + 1)
                    nc.vector.tensor_tensor(HT[:, t, :].rearrange("p (x c) -> p x c", x=SIDE),
                                            PS[:, t, :].rearrange("p (x c) -> p x c", x=SIDE),
                                            over(BTOK[:], SIDE), ALU.add).then_inc(tok_ready, 1)

        X2 = tile(top, "X2", [P, NT, C])
        LG = tile(top, "LG", [P, NT, NE])
        ROW = tile(top, "ROW", [P, 2, NT, RW_])
        LNB = tile(top, "LNB", [P, 2, C])
        XD = [nc.dram_tensor(f"rows{n}", ((NET + 1) * ETOK, RW_), F32, kind="Internal").ap() for n in range(2)]
        YD = [nc.dram_tensor(f"outs{n}", (2 * NTOK + (NET + 1) * ETOK, C), F32, kind="Internal").ap() for n in range(2)]

        def wait_apart(eng, *waits):
            counts = [eng.snap(eng.to_reg(n)) for n in waits[1::2]]
            eng.wait_ge(consts_ok, 1)
            for what, n in zip(waits[0::2], counts):
                eng.wait_ge(what, n)

        class Norm:
            def __init__(self, ctx, name):
                self.total, self.ssq, self.var, self.rstd = (
                    tile(ctx, f"{name}_{f}", [P, STREAMS, GT]) for f in ("total", "ssq", "var", "rstd"))
                self.cen, self.sq, self.z = (tile(ctx, f"{name}_{f}", [P, STREAMS, GT, C]) for f in ("cen", "sq", "z"))
                self.total_ok, self.cen_ok, self.sq_ok, self.ssq_ok, self.var_ok, self.rstd_ok, self.z_ok = (
                    sem(ctx, f"{name}_{f}_ok") for f in ("total", "cen", "sq", "ssq", "var", "rstd", "z"))

            def centre(self, dve, s, n, src):
                nc.vector.tensor_reduce(self.total[:, s], src, op=ALU.add, axis=AX.X).then_inc(self.total_ok, 1)
                dve.wait_ge(self.total_ok, n)
                nc.vector.scalar_tensor_tensor(out=self.cen[:, s], in0=bc(self.total[:, s], C), scalar=-1.0 / C,
                                               in1=src, op0=ALU.mult, op1=ALU.add).then_inc(self.cen_ok, 1)

            def square(self, act, s, n):
                act.wait_ge(self.cen_ok, n)
                nc.scalar.activation(self.sq[:, s], self.cen[:, s], ACT.Square).then_inc(self.sq_ok, 1)

            def variance(self, dve, s, n, eps):
                dve.wait_ge(self.sq_ok, n)
                nc.vector.tensor_reduce(self.ssq[:, s], self.sq[:, s], op=ALU.add, axis=AX.X).then_inc(self.ssq_ok, 1)
                dve.wait_ge(self.ssq_ok, n)
                nc.vector.tensor_scalar(self.var[:, s], self.ssq[:, s], 1.0 / C, eps, ALU.mult, ALU.add).then_inc(self.var_ok, 1)

            def power(self, pool, s, n):
                pool.wait_ge(self.var_ok, n)
                nc.gpsimd.tensor_tensor(self.rstd[:, s], self.var[:, s], NHALF[:, 0:GT], ALU.pow).then_inc(self.rstd_ok, 1)

            def scale(self, dve, s, n):
                dve.wait_ge(self.rstd_ok, n)
                nc.vector.tensor_tensor(self.z[:, s], self.cen[:, s], bc(self.rstd[:, s], C), ALU.mult).then_inc(self.z_ok, 1)

        def tiles(a, g):
            return a[:, bass.ds(g * GT, GT), :]

        with ExitStack() as ctx:
            ln = Norm(ctx, "b_ln")
            zT = tile(ctx, "b_zT", [C, STREAMS, GTOK])
            uT = tile(ctx, "b_uT", [C, STREAMS, GTOK])
            val = tile(ctx, "b_val", [P, STREAMS, GT, C])
            att = tile(ctx, "b_att", [P, STREAMS, GT, P])
            filled, lnb_in = sem(ctx, "b_filled"), sem(ctx, "b_lnb_in")
            zT_mm, zT_ok, u_mm, u_ok, v_mm, v_ok, sc_mm, att_ok, ctx_mm, h_ok = (
                sem(ctx, "b_" + n) for n in ("zT_mm", "zT_ok", "u_mm", "u_ok", "v_mm", "v_ok", "sc_mm", "att_ok", "ctx_mm", "h_ok"))
            block = phase_block(ctx)

            @block.sync
            def _(sp):
                sp.dma_start(LNB[:], d["ln_rows"]).then_inc(lnb_in, 16)
                for rows in XD:
                    sp.dma_start(rows, d["empty"]).then_inc(filled, 16)
                sp.wait_ge(lnb_in, 16)
                sp.wait_ge(filled, 16 * len(XD))

            @block.vector
            def _(dve):
                with dve.Fori(0, NG // STREAMS) as it:
                    ns = [it * STREAMS + s + 1 for s in range(STREAMS)]
                    hs = [tiles(H, it * STREAMS + s) for s in range(STREAMS)]
                    for s, n in enumerate(ns):
                        ln.centre(dve, s, n, hs[s])
                    for s, n in enumerate(ns):
                        ln.variance(dve, s, n, LN_EPS)
                    for s, n in enumerate(ns):
                        ln.scale(dve, s, n)
                    for s, n in enumerate(ns):
                        dve.wait_ge(v_mm, n)
                        nc.vector.tensor_copy(val[:, s], PS[:, 4 * s + 2, 0:GT * C].rearrange("p (t c) -> p t c", c=C)).then_inc(v_ok, 1)
                    for s, n in enumerate(ns):
                        dve.wait_ge(sc_mm, n)
                        nc.vector.scalar_tensor_tensor(
                            out=att[:, s], in0=PS[:, 4 * s + 3, :].rearrange("p (t l) -> p t l", l=P), scalar=0.0,
                            in1=over(k("lin_mask"), GT), op0=ALU.max, op1=ALU.mult).then_inc(att_ok, 1)
                    for s, n in enumerate(ns):
                        dve.wait_ge(ctx_mm, n)
                        nc.vector.tensor_tensor(hs[s], hs[s], PS[:, 4 * s, 0:GT * C].rearrange("p (t c) -> p t c", c=C),
                                                ALU.add).then_inc(h_ok, 1)

            @block.scalar
            def _(act):
                with act.Fori(0, NG // STREAMS) as it:
                    ns = [it * STREAMS + s + 1 for s in range(STREAMS)]
                    for s, n in enumerate(ns):
                        ln.square(act, s, n)
                    for s, n in enumerate(ns):
                        act.wait_ge(zT_mm, n)
                        nc.scalar.activation(zT[:, s], PS[0:C, 4 * s, :], ACT.Copy).then_inc(zT_ok, 1)
                    for s, n in enumerate(ns):
                        act.wait_ge(u_mm, n)
                        nc.scalar.activation(uT[:, s], PS[0:C, 4 * s + 1, :], ACT.Copy).then_inc(u_ok, 1)

            @block.gpsimd
            def _(pool):
                with pool.Fori(0, NG // STREAMS) as it:
                    for s in range(STREAMS):
                        ln.power(pool, s, it * STREAMS + s + 1)

            @block.tensor
            def _(pe):
                with pe.Fori(0, NG // STREAMS) as it:
                    ns = [it * STREAMS + s + 1 for s in range(STREAMS)]
                    for s, n in enumerate(ns):
                        wait_apart(pe, ln.z_ok, n)
                        for t in range(GT):
                            last = nc.tensor.transpose(PS[0:C, 4 * s, t * P:(t + 1) * P], ln.z[:, s, t, :], ident)
                        last.then_inc(zT_mm, 1)
                    for s, n in enumerate(ns):
                        wait_apart(pe, zT_ok, n)
                        nc.tensor.matmul(PS[0:C, 4 * s + 1, :], M1[:], zT[:, s], start=True, stop=True).then_inc(u_mm, 1)
                        for t in range(GT):
                            last = nc.tensor.matmul(PS[:, 4 * s + 2, t * C:(t + 1) * C], zT[:, s, t * P:(t + 1) * P], M2[:],
                                                    start=True, stop=True)
                        last.then_inc(v_mm, 1)
                    for s, n in enumerate(ns):
                        pe.wait_ge(u_ok, n)
                        for t in range(GT):
                            last = nc.tensor.matmul(PS[:, 4 * s + 3, t * P:(t + 1) * P], zT[:, s, t * P:(t + 1) * P],
                                                    uT[:, s, t * P:(t + 1) * P], start=True, stop=True)
                        last.then_inc(sc_mm, 1)
                    for s, n in enumerate(ns):
                        pe.wait_ge(att_ok, n)
                        pe.wait_ge(v_ok, n)
                        for t in range(GT):
                            last = nc.tensor.matmul(PS[:, 4 * s, t * C:(t + 1) * C], att[:, s, t, :], val[:, s, t, :],
                                                    start=True, stop=True)
                        last.then_inc(ctx_mm, 1)

        with ExitStack() as ctx:
            ln = Norm(ctx, "c_ln")
            rq = tile(ctx, "c_rq", [P, STREAMS, GT])
            rr = tile(ctx, "c_rr", [P, STREAMS, GT])
            vz = tile(ctx, "c_vz", [P, STREAMS, GT])
            nz = tile(ctx, "c_nz", [P, STREAMS, GT, C])
            nT = tile(ctx, "c_nT", [C, STREAMS, GTOK])
            q2 = tile(ctx, "c_q2", [P, STREAMS, GTOK])
            k2 = tile(ctx, "c_k2", [P, STREAMS, GTOK])
            kb = tile(ctx, "c_kb", [P, STREAMS, GB, NH0, L])
            vb = tile(ctx, "c_vb", [P, STREAMS, GB, 2, 2, HD + 1])
            sc = tile(ctx, "c_sc", [P, STREAMS, GT * NH0, L])
            mx = tile(ctx, "c_mx", [P, STREAMS, GT * NH0])
            eT = tile(ctx, "c_eT", [P, STREAMS, GT, 2, P])
            rs = tile(ctx, "c_rs", [P, STREAMS, GT * NH0])
            y = tile(ctx, "c_y", [P, STREAMS, GT, C])
            yT = tile(ctx, "c_yT", [C, STREAMS, GTOK])
            names = ("vz_ok", "rq_ok", "rr_ok", "nz_ok", "nT_mm", "nT_ok", "q_mm", "k_mm", "v_mm", "q_ok", "k_ok", "kr_mm",
                     "kb_ok", "vb_ok", "sc_mm", "sm_ok", "mx_ok", "sub_ok", "exp_ok", "eT_mm", "eT_ok", "av_mm", "rs_ok", "y_ok",
                     "yT_mm", "yT_ok", "o_mm", "x2_ok", "h_ok", "init")
            (vz_ok, rq_ok, rr_ok, nz_ok, nT_mm, nT_ok, q_mm, k_mm, v_mm, q_ok, k_ok, kr_mm, kb_ok, vb_ok, sc_mm, sm_ok, mx_ok,
             sub_ok, exp_ok, eT_mm, eT_ok, av_mm, rs_ok, y_ok, yT_mm, yT_ok, o_mm, x2_ok, h_ok, init) = (sem(ctx, "c_" + n) for n in names)
            block = phase_block(ctx)

            def by_seq(ap):
                return ap.rearrange("p (b l) -> p b l", l=L)

            @block.vector
            def _(dve):
                with dve.Fori(0, NG // STREAMS) as it:
                    ns = [it * STREAMS + s + 1 for s in range(STREAMS)]
                    gs = [it * STREAMS + s for s in range(STREAMS)]
                    for s, n in enumerate(ns):
                        ln.centre(dve, s, n, tiles(H, gs[s]))
                    for s, n in enumerate(ns):
                        ln.variance(dve, s, n, LN_EPS)
                    for s, n in enumerate(ns):
                        ln.scale(dve, s, n)
                        nc.vector.scalar_tensor_tensor(out=vz[:, s], in0=ln.ssq[:, s], scalar=1.0 / C, in1=ln.rstd[:, s],
                                                       op0=ALU.mult, op1=ALU.mult).then_inc(vz_ok, 1)
                        dve.wait_ge(vz_ok, 2 * n - 1)
                        nc.vector.tensor_tensor(vz[:, s], vz[:, s], ln.rstd[:, s], ALU.mult).then_inc(vz_ok, 1)
                        dve.wait_ge(vz_ok, 2 * n)
                        nc.vector.tensor_scalar(rq[:, s], vz[:, s], RMS_EPS, None, ALU.add).then_inc(rq_ok, 1)
                    for s, n in enumerate(ns):
                        dve.wait_ge(rr_ok, n)
                        nc.vector.tensor_tensor(nz[:, s], ln.z[:, s], bc(rr[:, s], C), ALU.mult).then_inc(nz_ok, 1)
                    for s, n in enumerate(ns):
                        for mm, dst, bank, ok in ((q_mm, q2, 1, q_ok), (k_mm, k2, 2, k_ok)):
                            dve.wait_ge(mm, n)
                            nc.vector.tensor_tensor(by_seq(dst[:, s]), by_seq(PS[:, 4 * s + bank, :]), over(k("cos_sin"), GB),
                                                    ALU.mult).then_inc(ok, 1)
                    for s, n in enumerate(ns):
                        dve.wait_ge(v_mm, n)
                        for h in range(2):
                            last = nc.vector.tensor_copy(vb[h * L:(h + 1) * L, s, :, :, h, 0:HD],
                                                         PS[h * L:(h + 1) * L, 4 * s, 0:GB * 32].rearrange("p (b k e) -> p b k e", k=2, e=HD))
                        last.then_inc(vb_ok, 1)
                    for s, n in enumerate(ns):
                        dve.wait_ge(sc_mm, n)
                        s4 = PS[:, 4 * s + 1:4 * s + 3, :].rearrange("p k (h l) -> p (k h) l", l=L)
                        nc.vector.tensor_tensor(sc[:, s], s4, over(k("causal"), GT * NH0), ALU.add).then_inc(sm_ok, 1)
                        dve.wait_ge(sm_ok, n)
                        nc.vector.tensor_reduce(mx[:, s], sc[:, s], op=ALU.max, axis=AX.X).then_inc(mx_ok, 1)
                        dve.wait_ge(mx_ok, n)
                        nc.vector.tensor_tensor(sc[:, s], sc[:, s], bc(mx[:, s], L), ALU.subtract).then_inc(sub_ok, 1)
                    for s, n in enumerate(ns):
                        dve.wait_ge(av_mm, n)
                        av = PS[:, 4 * s, 0:GT * NH0 * (HD + 1)].rearrange("p (h e) -> p h e", e=HD + 1)
                        nc.vector.reciprocal(rs[:, s], av[:, :, HD]).then_inc(rs_ok, 1)
                        dve.wait_ge(rs_ok, n)
                        nc.vector.tensor_tensor(y[:, s].rearrange("p t (h e) -> p (t h) e", e=HD), av[:, :, 0:HD],
                                                bc(rs[:, s], HD), ALU.mult).then_inc(y_ok, 1)
                    for s, n in enumerate(ns):
                        dve.wait_ge(o_mm, n)
                        x2 = tiles(X2, gs[s])
                        nc.vector.tensor_tensor(x2, ln.z[:, s], PS[:, 4 * s, 0:GT * C].rearrange("p (t c) -> p t c", c=C),
                                                ALU.add).then_inc(x2_ok, 1)
                        dve.wait_ge(x2_ok, n)
                        h = tiles(H, gs[s])
                        nc.vector.tensor_tensor(h, h, x2, ALU.add).then_inc(h_ok, 1)

            @block.scalar
            def _(act):
                with act.Fori(0, NG // STREAMS) as it:
                    ns = [it * STREAMS + s + 1 for s in range(STREAMS)]
                    for s, n in enumerate(ns):
                        ln.square(act, s, n)
                    for s, n in enumerate(ns):
                        act.wait_ge(nT_mm, n)
                        nc.scalar.activation(nT[:, s], PS[0:C, 4 * s, :], ACT.Copy).then_inc(nT_ok, 1)
                    for s, n in enumerate(ns):
                        act.wait_ge(kr_mm, n)
                        for h in range(NH0):
                            last = nc.scalar.activation(kb[:, s, :, h, :], by_seq(PS[:, 4 * s + 3, :]), ACT.Copy,
                                                        scale=k("head_mask")[:, h:h + 1])
                        last.then_inc(kb_ok, 1)
                    for s, n in enumerate(ns):
                        act.wait_ge(sub_ok, n)
                        nc.scalar.activation(sc[:, s], sc[:, s], ACT.Exp).then_inc(exp_ok, 1)
                    for s, n in enumerate(ns):
                        act.wait_ge(eT_mm, n)
                        nc.scalar.activation(eT[:, s].rearrange("p t k l -> p (t k l)"),
                                             PS[:, 4 * s + 1:4 * s + 3, :].rearrange("p k n -> p (k n)"), ACT.Copy).then_inc(eT_ok, 1)
                    for s, n in enumerate(ns):
                        act.wait_ge(yT_mm, n)
                        nc.scalar.activation(yT[:, s], PS[0:C, 4 * s + 3, :], ACT.Copy).then_inc(yT_ok, 1)

            @block.gpsimd
            def _(pool):
                nc.gpsimd.memset(vb[:], 0.0).then_inc(init, 1)
                pool.wait_ge(init, 1)
                for h in range(2):
                    nc.gpsimd.memset(vb[h * L:(h + 1) * L, :, :, :, h, HD:HD + 1], 1.0).then_inc(init, 1)
                    pool.wait_ge(init, h + 2)
                with pool.Fori(0, NG // STREAMS) as it:
                    ns = [it * STREAMS + s + 1 for s in range(STREAMS)]
                    for s, n in enumerate(ns):
                        ln.power(pool, s, n)
                    for s, n in enumerate(ns):
                        pool.wait_ge(rq_ok, n)
                        nc.gpsimd.tensor_tensor(rr[:, s], rq[:, s], NHALF[:, 0:GT], ALU.pow).then_inc(rr_ok, 1)

            @block.tensor
            def _(pe):
                pe.wait_ge(init, 3)
                with pe.Fori(0, NG // STREAMS) as it:
                    ns = [it * STREAMS + s + 1 for s in range(STREAMS)]
                    for s, n in enumerate(ns):
                        wait_apart(pe, nz_ok, n)
                        for t in range(GT):
                            last = nc.tensor.transpose(PS[0:C, 4 * s, t * P:(t + 1) * P], nz[:, s, t, :], ident)
                        last.then_inc(nT_mm, 1)
                    for s, n in enumerate(ns):
                        pe.wait_ge(nT_ok, n)
                        nc.tensor.matmul(PS[:, 4 * s + 1, :], WQ2[:], nT[:, s], start=True, stop=True).then_inc(q_mm, 1)
                        nc.tensor.matmul(PS[:, 4 * s + 2, :], WK2[:], nT[:, s], start=True, stop=True).then_inc(k_mm, 1)
                        for b in range(GB):
                            for h in range(2):
                                last = nc.tensor.matmul(PS[h * L:(h + 1) * L, 4 * s, b * 32:(b + 1) * 32], nT[:, s, b * L:(b + 1) * L],
                                                        WV0[:], start=True, stop=True)
                        last.then_inc(v_mm, 1)
                    for s, n in enumerate(ns):
                        pe.wait_ge(k_ok, n)
                        nc.tensor.matmul(PS[:, 4 * s + 3, :], k("fold"), k2[:, s], start=True, stop=True).then_inc(kr_mm, 1)
                    for s, n in enumerate(ns):
                        wait_apart(pe, q_ok, n)
                        pe.wait_ge(kb_ok, n)
                        for b in range(GB):
                            at = (b // 2) * NH0 * L
                            last = nc.tensor.matmul(PS[b % 2 * L:(b % 2 + 1) * L, 4 * s + 1 + at // 512, at % 512:at % 512 + NH0 * L],
                                                    q2[:, s, b * L:(b + 1) * L], kb[:, s, b].rearrange("p h l -> p (h l)"),
                                                    start=True, stop=True)
                        last.then_inc(sc_mm, 1)
                    for s, n in enumerate(ns):
                        pe.wait_ge(exp_ok, n)
                        for t in range(GT):
                            for m in range(2):
                                i = 2 * t + m
                                last = nc.tensor.transpose(PS[:, 4 * s + 1 + i // 4, i % 4 * P:(i % 4 + 1) * P],
                                                           sc[:, s, 2 * i:2 * i + 2, :].rearrange("p h l -> p (h l)"), ident)
                        last.then_inc(eT_mm, 1)
                    for s, n in enumerate(ns):
                        pe.wait_ge(eT_ok, n)
                        pe.wait_ge(vb_ok, n)
                        for b in range(GB):
                            for m in range(2):
                                at = ((b // 2) * 2 + m) * 2 * (HD + 1)
                                last = nc.tensor.matmul(PS[b % 2 * L:(b % 2 + 1) * L, 4 * s, at:at + 2 * (HD + 1)],
                                                        eT[:, s, b // 2, m, b % 2 * L:(b % 2 + 1) * L],
                                                        vb[:, s, b, m].rearrange("p h e -> p (h e)"), start=True, stop=True)
                        last.then_inc(av_mm, 1)
                    for s, n in enumerate(ns):
                        wait_apart(pe, y_ok, n)
                        for t in range(GT):
                            last = nc.tensor.transpose(PS[0:C, 4 * s + 3, t * P:(t + 1) * P], y[:, s, t, :], ident)
                        last.then_inc(yT_mm, 1)
                    for s, n in enumerate(ns):
                        pe.wait_ge(yT_ok, n)
                        for t in range(GT):
                            last = nc.tensor.matmul(PS[:, 4 * s, t * C:(t + 1) * C], yT[:, s, t * P:(t + 1) * P], WO0[:],
                                                    start=True, stop=True)
                        last.then_inc(o_mm, 1)


        def features(layer):
            src = X2 if layer == 0 else H
            with ExitStack() as ctx:
                nm = f"f{layer}"
                ln = Norm(ctx, nm + "_ln")
                zw = tile(ctx, nm + "_zw", [P, STREAMS, GT, C])
                fT = tile(ctx, nm + "_fT", [C, STREAMS, GTOK])
                zw_ok, row_ok, fT_mm, fT_ok, lg_mm, lg_ok = (
                    sem(ctx, f"{nm}_{n}") for n in ("zw_ok", "row_ok", "fT_mm", "fT_ok", "lg_mm", "lg_ok"))
                block = phase_block(ctx)

                @block.vector
                def _(dve):
                    with dve.Fori(0, NG // STREAMS) as it:
                        ns = [it * STREAMS + s + 1 for s in range(STREAMS)]
                        gs = [it * STREAMS + s for s in range(STREAMS)]
                        for s, n in enumerate(ns):
                            if layer == 0:
                                nc.vector.tensor_copy(ln.cen[:, s], tiles(src, gs[s])).then_inc(ln.cen_ok, 1)
                            else:
                                ln.centre(dve, s, n, tiles(src, gs[s]))
                        for s, n in enumerate(ns):
                            ln.variance(dve, s, n, RMS_EPS if layer == 0 else LN_EPS)
                        for s, n in enumerate(ns):
                            ln.scale(dve, s, n)
                            dve.wait_ge(ln.z_ok, n)
                            nc.vector.tensor_tensor(zw[:, s], ln.z[:, s], over(LNB[:, layer, :], GT), ALU.mult).then_inc(zw_ok, 1)
                        for s, n in enumerate(ns):
                            dve.wait_ge(lg_mm, n)
                            nc.vector.tensor_copy(tiles(LG, gs[s]), PS[:, 4 * s + 1, 0:GT * NE].rearrange("p (t e) -> p t e", e=NE)).then_inc(lg_ok, 1)

                @block.scalar
                def _(act):
                    with act.Fori(0, NG // STREAMS) as it:
                        ns = [it * STREAMS + s + 1 for s in range(STREAMS)]
                        for s, n in enumerate(ns):
                            ln.square(act, s, n)
                        for s, n in enumerate(ns):
                            act.wait_ge(fT_mm, n)
                            nc.scalar.activation(fT[:, s], PS[0:C, 4 * s, :], ACT.Copy).then_inc(fT_ok, 1)
                            for c in range(2):
                                last = nc.scalar.activation(ROW[:, c, bass.ds((it * STREAMS + s) * GT, GT), 0:C], zw[:, s], ACT.Copy)
                            last.then_inc(row_ok, 1)

                @block.gpsimd
                def _(pool):
                    with pool.Fori(0, NG // STREAMS) as it:
                        for s in range(STREAMS):
                            ln.power(pool, s, it * STREAMS + s + 1)

                @block.tensor
                def _(pe):
                    with pe.Fori(0, NG // STREAMS) as it:
                        ns = [it * STREAMS + s + 1 for s in range(STREAMS)]
                        for s, n in enumerate(ns):
                            wait_apart(pe, zw_ok, n)
                            for t in range(GT):
                                last = nc.tensor.transpose(PS[0:C, 4 * s, t * P:(t + 1) * P], zw[:, s, t, :], ident)
                            last.then_inc(fT_mm, 1)
                        for s, n in enumerate(ns):
                            pe.wait_ge(fT_ok, n)
                            for t in range(GT):
                                last = nc.tensor.matmul(PS[:, 4 * s + 1, t * NE:(t + 1) * NE], fT[:, s, t * P:(t + 1) * P],
                                                        RW[:, layer, :], start=True, stop=True)
                            last.then_inc(lg_mm, 1)

        def experts(layer):
            hid = HID0 if layer == 0 else HID1
            full, rest = hid // P, hid % P
            wcols = (2 * full + 1) * P
            units = [(j, j + 1) for j in range(0, full - 1, 2)] + [(full - 1, full)]
            U, LAG, UN = len(units), 2, 8
            PAIRS = 3
            YB = 6
            rows_dram, out_dram = XD[layer], YD[layer]
            with ExitStack() as ctx:
                nm = f"x{layer}"
                stage = tile(ctx, nm + "_stage", [P, 2, wcols])
                whi = tile(ctx, nm + "_whi", [P, NE * wcols], F16)
                wlo = tile(ctx, nm + "_wlo", [P, NE * wcols], F16)
                w2 = tile(ctx, nm + "_w2", [P, NE * (full + 1) * C])
                xt = tile(ctx, nm + "_xt", [P, UN, 2, RW_])
                xs = tile(ctx, nm + "_xs", [P, UN, ETOK], F16)
                sil = tile(ctx, nm + "_sil", [P, PAIRS, 2 * ETOK])
                hid_t = tile(ctx, nm + "_hid", [P, PAIRS, 2 * ETOK])
                yg = tile(ctx, nm + "_yg", [P, UN, 2, C])
                yid = tile(ctx, nm + "_yid", [P, UN, 2], U32)
                y12 = tile(ctx, nm + "_y12", [P, 2, NT, C])
                rt = [tile(ctx, f"{nm}_rt{n}", [P, NT, NE]) for n in range(10)]
                rv = [tile(ctx, f"{nm}_rv{n}", [P, NT]) for n in range(6)]
                re = [tile(ctx, f"{nm}_re{n}", [P, NE]) for n in range(4)]
                of_tile = tile(ctx, nm + "_of_tile", [P, NET, NE])
                ex_f = tile(ctx, nm + "_ex_f", [P, NET])
                ex_i = tile(ctx, nm + "_ex_i", [P, NET], I32)
                pos = tile(ctx, nm + "_pos", [P, 2, NT], U32)
                (whi_ok, wlo_ok, r_step, r_exp, picked, counted, routed, xT_mm, hi_ok, xs_ok, up_mm, sil_ok, hid_ok, y_mm, yg_ok,
                 pre_in, sent, y_in, y_free) = (
                    sem(ctx, f"{nm}_{n}") for n in ("whi_ok", "wlo_ok", "r_step", "r_exp", "picked", "counted", "routed", "xT_mm", "hi_ok",
                                                     "xs_ok", "up_mm", "sil_ok", "hid_ok", "y_mm", "yg_ok", "pre_in", "sent", "y_in", "y_free"))
                w_in = [sem(ctx, f"{nm}_w_in{i}") for i in range(2)]
                w2_in = sem(ctx, nm + "_w2_in")
                x_in = [sem(ctx, f"{nm}_x_in{i}") for i in range(UN)]
                y_out = [sem(ctx, f"{nm}_y_out{i}") for i in range(UN)]
                block = phase_block(ctx)
                seq = [(a, u) for a in range(UN) for u in range(U)]

                def turned(a):
                    return PS[0:C, 2 * ((a * U - 1) % PAIRS) + 1, ETOK:2 * ETOK]

                @block.sync
                def _(sp):
                    w13, w2d = d[f"w13_{layer}"], d[f"w2_{layer}"]
                    sp.dma_start(w2[:].rearrange("p (e n) -> p e n", e=NE), w2d.rearrange("e p j c -> p e (j c)")).then_inc(w2_in, 16)
                    for e in range(NE):
                        if e >= 2:
                            sp.wait_ge(wlo_ok, e - 1)
                        sp.dma_start(stage[:, e % 2, :], w13[e]).then_inc(w_in[e % 2], 16)
                    sp.wait_ge(sent, 16 * 2 * NT)

                    def load(a, n):
                        sp.dma_start(xt[:, a], rows_dram[bass.ds(n * ETOK, ETOK), :].rearrange("(b p) n -> p b n", p=P)).then_inc(x_in[a], 16)

                    for a in range(UN):
                        load(a, a)
                    with sp.Fori(0, NET // UN - 1) as it:
                        for a in range(UN):
                            sp.wait_ge(yg_ok, it * UN + a + 2)
                            load(a, (it + 1) * UN + a)
                    for a in range(UN):
                        sp.wait_ge(y_out[a], 32 * (NET // UN))
                    sp.dma_start(y12[:].rearrange("p k t c -> p (k t) c"), out_dram[0:2 * NTOK, :].rearrange("(t p) c -> p t c", p=P))\
                      .then_inc(y_in, 16)

                @block.gpsimd
                def _(pool):
                    pool.wait_ge(routed, 1)
                    for c in range(2):
                        for t in range(NT):
                            nc.gpsimd.indirect_dma_start(
                                out=rows_dram, out_offset=bass.IndirectOffsetOnAxis(ap=pos[:, c, t:t + 1], axis=0),
                                in_=ROW[:, c, t, :], in_offset=None).then_inc(sent, 16)
                    pool.wait_ge(sent, 16 * 2 * NT)
                    with pool.Fori(0, NET // UN) as it:
                        for a in range(UN):
                            wait_apart(pool, yg_ok, it * UN + a + 2)
                            for b in range(2):
                                nc.gpsimd.indirect_dma_start(
                                    out=out_dram, out_offset=bass.IndirectOffsetOnAxis(ap=yid[:, a, b:b + 1], axis=0),
                                    in_=yg[:, a, b, :], in_offset=None).then_inc(y_out[a], 16)
                            if a >= UN // 2:
                                pool.wait_ge(y_out[a - UN // 2], it * 32 + 32)
                                pool.sem_inc(y_free, 1)
                        for a in range(UN - UN // 2, UN):
                            pool.wait_ge(y_out[a], it * 32 + 32)
                            pool.sem_inc(y_free, 1)

                @block.scalar
                def _(act):
                    act.wait_ge(r_step, 2)
                    nc.scalar.activation(rt[0][:], rt[0][:], ACT.Exp).then_inc(r_exp, 1)
                    for e in range(NE):
                        act.wait_ge(w_in[e % 2], 16 * (e // 2 + 1))
                        nc.scalar.activation(whi[:, e * wcols:(e + 1) * wcols], stage[:, e % 2], ACT.Copy, scale=WSCALE).then_inc(whi_ok, 1)
                    with act.Fori(0, NET // UN) as it:
                        def split(a):
                            act.wait_ge(xT_mm, it * UN + a + 1)
                            nc.scalar.activation(xs[0:C, a], turned(a), ACT.Copy).then_inc(hi_ok, 1)

                        split(0)
                        for q, (a, u) in enumerate(seq):
                            if u == U - 1 and a + 1 < UN:
                                split(a + 1)
                            act.wait_ge(up_mm, it * len(seq) + q + 1)
                            nc.scalar.activation(sil[:, q % PAIRS], PS[:, 2 * (q % PAIRS), :], ACT.Silu, scale=1.0 / WSCALE).then_inc(sil_ok, 1)

                @block.tensor
                def _(pe):
                    pe.wait_ge(picked, 1)
                    both = rt[5][:].rearrange("p t e -> p (t e)")
                    nc.tensor.matmul(PS[:, 0, 0:NT * NE], k("before"), both, start=True, stop=True)
                    nc.tensor.matmul(PS[:, 1, 0:NT * NE], k("ones"), both, start=True, stop=True).then_inc(counted, 1)
                    pe.wait_ge(wlo_ok, NE)
                    pe.wait_ge(w2_in, 16)
                    pe.wait_ge(routed, 1)
                    with pe.Fori(0, NET // UN) as it:
                        ex = [pe.value_load(ex_i[0:1, bass.ds(it * UN + a, 1)], min_val=0, max_val=NE - 1) for a in range(UN)]

                        def turn(a):
                            wait_apart(pe, x_in[a], it * 16 + 16)
                            for b in range(2):
                                last = nc.tensor.transpose(turned(a)[:, b * P:(b + 1) * P], xt[:, a, b, 0:C], ident)
                            last.then_inc(xT_mm, 1)

                        def up(q):
                            a, u = seq[q]
                            if u == 0:
                                wait_apart(pe, xs_ok, it * UN + a + 1)
                            for v, j in enumerate(units[u]):
                                parts = ((0, j), (1, full + j)) if j < full else ((0, 2 * full),)
                                for bank, col in parts:
                                    o = PS[:, 2 * (q % PAIRS) + bank, v * ETOK:(v + 1) * ETOK]
                                    at = ex[a] * wcols + col * P
                                    nc.tensor.matmul(o, whi[:, bass.ds(at, P)], xs[:, a], start=True, stop=False)
                                    last = nc.tensor.matmul(o, wlo[:, bass.ds(at, P)], xs[:, a], start=False, stop=True)
                            last.then_inc(up_mm, 1)

                        def down(q):
                            a, u = seq[q]
                            pe.wait_ge(hid_ok, it * len(seq) + q + 1)
                            if u == 0:
                                pe.wait_ge(yg_ok, it * UN + a + 1)
                            for v, j in enumerate(units[u]):
                                rows = P if j < full else rest
                                for b in range(2):
                                    last = nc.tensor.matmul(
                                        PS[:, YB + b, 0:C], hid_t[0:rows, q % PAIRS, v * ETOK + b * P:v * ETOK + (b + 1) * P],
                                        w2[0:rows, bass.ds(ex[a] * ((full + 1) * C) + j * C, C)], start=(j == 0), stop=(j == full))
                            if u == U - 1:
                                last.then_inc(y_mm, 1)

                        turn(0)
                        nq = len(seq)
                        for q in range(nq + LAG):
                            if q < nq:
                                up(q)
                                if seq[q][1] == U - 1 and seq[q][0] + 1 < UN:
                                    turn(seq[q][0] + 1)
                            if q >= LAG:
                                down(q - LAG)

                @block.vector
                def _(dve):
                    r_at = [0]

                    def step(ins):
                        r_at[0] += 1
                        ins.then_inc(r_step, 1)
                        dve.wait_ge(r_step, r_at[0])

                    tt, red = nc.vector.tensor_tensor, nc.vector.tensor_reduce
                    prob, prob2, w, one1, both, cum, cum2, one2, full_pos, tmp = rt[0], rt[1], rt[2], rt[3], rt[5], rt[6], rt[7], rt[4], rt[8], rt[9]
                    mx, m1, m2, wm, den, psum = rv
                    step(red(mx[:], LG[:], op=ALU.max, axis=AX.X))
                    step(tt(prob[:], LG[:], bc(mx[:], NE), ALU.subtract))
                    dve.wait_ge(r_exp, 1)
                    step(red(psum[:], prob[:], op=ALU.add, axis=AX.X))
                    step(nc.vector.reciprocal(psum[:], psum[:]))
                    step(tt(prob[:], prob[:], bc(psum[:], NE), ALU.mult))

                    def pick(src, top, one):
                        step(red(top[:], src[:], op=ALU.max, axis=AX.X))
                        step(tt(w[:], src[:], bc(top[:], NE), ALU.is_equal))
                        step(tt(w[:], w[:], over(k("first"), NT), ALU.mult))
                        step(red(wm[:], w[:], op=ALU.max, axis=AX.X))
                        step(tt(one[:], w[:], bc(wm[:], NE), ALU.is_equal))

                    pick(prob, m1, one1)
                    step(nc.vector.scalar_tensor_tensor(out=prob2[:], in0=one1[:], scalar=-2.0, in1=prob[:], op0=ALU.mult, op1=ALU.add))
                    pick(prob2, m2, one2)
                    tt(both[:], one1[:], one2[:], ALU.add).then_inc(picked, 1)
                    step(nc.vector.scalar_tensor_tensor(out=den[:], in0=m1[:], scalar=1e-9, in1=m2[:], op0=ALU.add, op1=ALU.add))
                    step(nc.vector.reciprocal(den[:], den[:]))
                    step(nc.vector.tensor_scalar(den[:], den[:], 1.0 / WSCALE, None, ALU.mult))
                    step(tt(ROW[:, 0, :, C + 1], m1[:], den[:], ALU.mult))
                    step(tt(ROW[:, 1, :, C + 1], m2[:], den[:], ALU.mult))
                    dve.wait_ge(counted, 1)
                    totals = PS[:, 1, 0:NT * NE].rearrange("p (t e) -> p t e", e=NE)
                    step(nc.vector.tensor_copy(cum[:], totals))
                    a, b, sh = cum, cum2, 1
                    while sh < NT:
                        nc.vector.tensor_copy(b[:, 0:sh, :], a[:, 0:sh, :])
                        step(tt(b[:, sh:, :], a[:, sh:, :], a[:, :NT - sh, :], ALU.add))
                        a, b, sh = b, a, 2 * sh
                    cnt, tl, end, base = re
                    step(nc.vector.tensor_scalar(tl[:], a[:, NT - 1, :], ETOK / 2 - 0.5, 1.0 / ETOK, ALU.add, ALU.mult))
                    step(nc.vector.tensor_scalar(tl[:], tl[:], 8388608.0, None, ALU.add))
                    step(nc.vector.tensor_scalar(tl[:], tl[:], -8388608.0, float(ETOK), ALU.add, ALU.mult))
                    step(nc.vector.tensor_copy(end[:], tl[:]))
                    for e in range(1, NE):
                        step(tt(end[:, e:e + 1], end[:, e:e + 1], end[:, e - 1:e], ALU.add))
                    step(tt(base[:], end[:], tl[:], ALU.subtract))
                    step(tt(b[:], a[:], totals, ALU.subtract))
                    step(tt(b[:], b[:], PS[:, 0, 0:NT * NE].rearrange("p (t e) -> p t e", e=NE), ALU.add))
                    step(tt(full_pos[:], b[:], over(base[:], NT), ALU.add))
                    for c, one in ((0, one1), (1, one2)):
                        step(tt(tmp[:], one[:], full_pos[:], ALU.mult))
                        step(red(wm[:], tmp[:], op=ALU.add, axis=AX.X))
                        step(nc.vector.tensor_copy(pos[:, c, :], wm[:]))
                        step(nc.vector.tensor_copy(ROW[:, c, :, C], k("token")[:, c * NT:(c + 1) * NT]))
                    step(tt(of_tile[:], over(end[:], NET), bc(k("tile_at"), NE), ALU.is_le))
                    step(red(ex_f[:], of_tile[:], op=ALU.add, axis=AX.X))
                    step(nc.vector.tensor_scalar(ex_f[:], ex_f[:], NE - 1.0, None, ALU.min))
                    nc.vector.tensor_copy(ex_i[:], ex_f[:]).then_inc(routed, 1)
                    for e in range(NE):
                        dve.wait_ge(whi_ok, e + 1)
                        nc.vector.scalar_tensor_tensor(out=wlo[:, e * wcols:(e + 1) * wcols], in0=stage[:, e % 2], scalar=WSCALE,
                                                       in1=whi[:, e * wcols:(e + 1) * wcols], op0=ALU.mult, op1=ALU.subtract)\
                            .then_inc(wlo_ok, 1)
                    dve.sem_inc(yg_ok, 1)
                    dve.sem_inc(y_free, UN)
                    with dve.Fori(0, NET // UN) as it:
                        def split(a):
                            dve.wait_ge(hi_ok, it * UN + a + 1)
                            nc.vector.tensor_tensor(xs[C:P, a], turned(a), xs[0:C, a], ALU.subtract).then_inc(xs_ok, 1)

                        def gated(a):
                            dve.wait_ge(y_free, it * UN + a + 1)
                            dve.wait_ge(y_mm, it * UN + a + 1)
                            nc.vector.tensor_copy(yid[:, a], xt[:, a, :, C])
                            last = nc.vector.tensor_tensor(yg[:, a], PS[:, YB:YB + 2, 0:C], bc(xt[:, a, :, C + 1], C), ALU.mult)
                            last.then_inc(yg_ok, 1)

                        split(0)
                        for q, (a, u) in enumerate(seq):
                            if u == U - 1 and a + 1 < UN:
                                split(a + 1)
                            dve.wait_ge(sil_ok, it * len(seq) + q + 1)
                            last = None
                            j, j2, w = *units[u], q % PAIRS
                            if j2 < full:
                                last = nc.vector.tensor_tensor(hid_t[:, w], sil[:, w], PS[:, 2 * w + 1, :], ALU.mult)
                            else:
                                nc.vector.tensor_tensor(hid_t[:, w, 0:ETOK], sil[:, w, 0:ETOK], PS[:, 2 * w + 1, 0:ETOK], ALU.mult)
                                last = nc.vector.tensor_tensor(hid_t[0:rest, w, ETOK:], sil[0:rest, w, ETOK:],
                                                               PS[C:C + rest, 2 * w, ETOK:], ALU.mult)
                            last.then_inc(hid_ok, 1)
                            if q >= LAG and seq[q - LAG][1] == U - 1:
                                gated(seq[q - LAG][0])
                        for a, u in seq[-LAG:]:
                            if u == U - 1:
                                gated(a)
                    dve.wait_ge(y_in, 16)
                    nc.vector.tensor_tensor(y12[:, 0], y12[:, 0], y12[:, 1], ALU.add).then_inc(r_step, 1)
                    dve.wait_ge(r_step, r_at[0] + 1)
                    nc.vector.tensor_tensor(H[:], H[:], y12[:, 0], ALU.add).then_inc(r_step, 1)

        features(0)
        experts(0)

        def norm_phase(ctx_name, src, eps, dst):
            NC = 4
            CT = NT // NC
            with ExitStack() as ctx:
                nm = ctx_name
                total, ssq, rstd = (tile(ctx, f"{nm}_{f}", [P, NT]) for f in ("total", "ssq", "rstd"))
                cen, sq = (tile(ctx, f"{nm}_{f}", [P, NT, C]) for f in ("cen", "sq"))
                total_ok, cen_ok, sq_ok, ssq_ok, var_ok, rstd_ok, z_ok, zT_mm, zT_ok = (
                    sem(ctx, f"{nm}_{f}") for f in ("total_ok", "cen_ok", "sq_ok", "ssq_ok", "var_ok", "rstd_ok", "z_ok", "zT_mm", "zT_ok"))
                block = phase_block(ctx)
                part = [slice(c * CT, (c + 1) * CT) for c in range(NC)]

                @block.vector
                def _(dve):
                    for c in range(NC):
                        nc.vector.tensor_reduce(total[:, part[c]], src[:, part[c]], op=ALU.add, axis=AX.X).then_inc(total_ok, 1)
                        dve.wait_ge(total_ok, c + 1)
                        nc.vector.scalar_tensor_tensor(out=cen[:, part[c]], in0=bc(total[:, part[c]], C), scalar=-1.0 / C,
                                                       in1=src[:, part[c]], op0=ALU.mult, op1=ALU.add).then_inc(cen_ok, 1)
                    for c in range(NC):
                        dve.wait_ge(sq_ok, c + 1)
                        nc.vector.tensor_reduce(ssq[:, part[c]], sq[:, part[c]], op=ALU.add, axis=AX.X).then_inc(ssq_ok, 1)
                        dve.wait_ge(ssq_ok, c + 1)
                        nc.vector.tensor_scalar(ssq[:, part[c]], ssq[:, part[c]], 1.0 / C, eps, ALU.mult, ALU.add).then_inc(var_ok, 1)
                    for c in range(NC):
                        dve.wait_ge(rstd_ok, c + 1)
                        nc.vector.tensor_tensor(cen[:, part[c]], cen[:, part[c]], bc(rstd[:, part[c]], C), ALU.mult).then_inc(z_ok, 1)

                @block.scalar
                def _(act):
                    for c in range(NC):
                        act.wait_ge(cen_ok, c + 1)
                        nc.scalar.activation(sq[:, part[c]], cen[:, part[c]], ACT.Square).then_inc(sq_ok, 1)
                    for g in range(NG):
                        act.wait_ge(zT_mm, g + 1)
                        nc.scalar.activation(dst[0:C, g * GTOK:(g + 1) * GTOK], PS[0:C, g, :], ACT.Copy).then_inc(zT_ok, 1)

                @block.gpsimd
                def _(pool):
                    for c in range(NC):
                        pool.wait_ge(var_ok, c + 1)
                        nc.gpsimd.tensor_tensor(rstd[:, part[c]], ssq[:, part[c]], NHALF[:, 0:CT], ALU.pow).then_inc(rstd_ok, 1)

                @block.tensor
                def _(pe):
                    for g in range(NG):
                        pe.wait_ge(z_ok, g * GT // CT + 1)
                        for t in range(GT):
                            last = nc.tensor.transpose(PS[0:C, g, t * P:(t + 1) * P], cen[:, g * GT + t], ident)
                        last.then_inc(zT_mm, 1)

        e_ctx = ExitStack()
        with e_ctx:
            ZT = tile(e_ctx, "e_ZT", [C + 1, (NG + 1) * GTOK])
            O = tile(e_ctx, "e_O", [P, NT, NH1 * DV])
            OR = tile(e_ctx, "e_OR", [P, NT, NH1])
            norm_phase("e_ln", H, LN_EPS, ZT)

            with ExitStack() as ctx:
                TB = 2 * GT
                ONE = DV + 1
                qb = tile(ctx, "e_qb", [P, 2, GB, 2, 4, L])
                kT = tile(ctx, "e_kT", [P, 2, 2, GTOK])
                vb = tile(ctx, "e_vb", [P, 2, GB, NH1 // 2, 2, ONE])
                zd = tile(ctx, "e_zd", [C, 2, GB, 2, L])
                sc = tile(ctx, "e_sc", [P, 2, 2, 2, 4, L])
                mx = tile(ctx, "e_mx", [P, 2, 16])
                eT = tile(ctx, "e_eT", [P, 2, 4, P])
                rs = tile(ctx, "e_rs", [P, 2, NH1])
                o2 = tile(ctx, "e_o2", [L, 2, 2, 2, NH1, DV])
                sq = tile(ctx, "e_sq", [P, 2, NH1, DV])
                var = tile(ctx, "e_var", [P, 2, NH1])
                names = ("init", "zd_ok", "piece_mm", "piece_ok", "sc_mm", "mx_ok", "sub_ok", "exp_ok", "eT_mm", "eT_ok",
                         "av_mm", "rs_ok", "o2_ok", "o_ok", "sq_ok", "ss_ok", "var_ok", "or_ok")
                (init, zd_ok, piece_mm, piece_ok, sc_mm, mx_ok, sub_ok, exp_ok, eT_mm, eT_ok,
                 av_mm, rs_ok, o2_ok, o_ok, sq_ok, ss_ok, var_ok, or_ok) = (sem(ctx, "e_" + n) for n in names)
                block = phase_block(ctx)
                NPC = 2 * GT
                PRIME = 4
                QK = 4
                EB, AB, JB = 4, 6, 7

                @block.tensor
                def _(pe):
                    def piece(g, par, i, n):
                        wait_apart(pe, *((piece_ok, n) + ((zd_ok, g + 1) if i >= QK else ())))
                        if i < QK:
                            col = i // 2 + 2 * (i % 2)
                            nc.tensor.matmul(PS[:, JB, :], WQKV[:, col * P:(col + 1) * P], ZT[0:C, bass.ds(g * GTOK, GTOK)],
                                             start=True, stop=True).then_inc(piece_mm, 1)
                        else:
                            for s in range(2):
                                last = nc.tensor.matmul(PS[:, JB, s * 256:(s + 1) * 256],
                                                        zd[:, par, 2 * (i - QK) + s].rearrange("p u l -> p (u l)"),
                                                        WQKV[:, 512:768], start=True, stop=True)
                            last.then_inc(piece_mm, 1)

                    def scores(t):
                        par, tt = t // GT % 2, t % GT
                        for b in range(2):
                            for hf in range(2):
                                for pr in range(2):
                                    for r in range(2):
                                        s, at = 2 * tt + b, (b * 4 + hf * 2 + pr) * L
                                        last = nc.tensor.matmul(
                                            PS[:, 2 * (t % 2) + r, at:at + L],
                                            qb[r * L:(r + 1) * L, par, s, hf, 2 * pr:2 * pr + 2].rearrange("p h l -> p (h l)"),
                                            kT[r * L:(r + 1) * L, par, hf, s * L:(s + 1) * L], start=True, stop=True)
                        last.then_inc(sc_mm, 1)

                    def turn(t, b):
                        for c in range(4):
                            r, hf = c // 2, c % 2
                            last = nc.tensor.transpose(PS[:, EB + b, c * P:(c + 1) * P],
                                                       sc[:, t % 2, r, b, 2 * hf:2 * hf + 2, :].rearrange("p m l -> p (m l)"), ident)
                        last.then_inc(eT_mm, 1)

                    def weigh(t, b):
                        par, s = t // GT, 2 * (t % GT) + b
                        for c in range(4):
                            r, hf = c // 2, c % 2
                            m2 = hf * 2 + r
                            last = nc.tensor.matmul(PS[:, AB, m2 * 2 * ONE:(m2 + 1) * 2 * ONE], eT[:, b, c],
                                                    vb[:, par, s, m2].rearrange("p u e -> p (u e)"), start=True, stop=True)
                        last.then_inc(av_mm, 1)

                    pe.wait_ge(init, 3)
                    pe.wait_ge(zd_ok, 1)
                    for i in range(NPC):
                        piece(0, 0, i, i + 1)
                    pe.wait_ge(piece_ok, NPC + 1)
                    scores(0)
                    scores(1)
                    with pe.Fori(0, NT // TB) as it:
                        for t in range(TB):
                            n = it * TB + t
                            g = it * 2 + t // GT + 1
                            par, i, pc = (t // GT + 1) % 2, 2 * (t % GT), it * 2 * NPC + NPC + 2 * t
                            wait_apart(pe, exp_ok, n + 1)
                            turn(t, 0)
                            turn(t, 1)
                            piece(g, par, i, pc + 1)
                            wait_apart(pe, eT_ok, 2 * n + 1, o2_ok, 2 * n + 1, piece_ok, it * 2 * NPC + t // GT * NPC + NPC + 1)
                            weigh(t, 0)
                            wait_apart(pe, sub_ok, n + 1, piece_ok, (it * 2 + (t + 2) // GT) * NPC + QK + 1)
                            scores(t + 2)
                            wait_apart(pe, eT_ok, 2 * n + 2, o2_ok, 2 * n + 2)
                            weigh(t, 1)
                            piece(g, par, i + 1, pc + 2)

                @block.vector
                def _(dve):
                    def softmax(t, n):
                        s4 = PS[:, 2 * (t % 2):2 * (t % 2) + 2, :].rearrange("p k (m l) -> p (k m) l", l=L)
                        dve.wait_ge(sc_mm, n + 1)
                        nc.vector.tensor_reduce(mx[:, t % 2], s4, op=ALU.max, axis=AX.X).then_inc(mx_ok, 1)
                        dve.wait_ge(mx_ok, n + 1)
                        if not isinstance(n, int):
                            dve.wait_ge(eT_mm, 2 * n - 2)
                        nc.vector.tensor_tensor(sc[:, t % 2].rearrange("p r b m l -> p (r b m) l"), s4, bc(mx[:, t % 2], L),
                                                ALU.subtract).then_inc(sub_ok, 1)

                    def combine(t, b, n):
                        m = 2 * n + b
                        dve.wait_ge(av_mm, m + 1)
                        av = PS[:, AB, 0:NH1 * ONE].rearrange("p (m e) -> p m e", e=ONE)
                        nc.vector.reciprocal(rs[:, b], av[:, :, DV]).then_inc(rs_ok, 1)
                        dve.wait_ge(rs_ok, m + 1)
                        dve.wait_ge(o_ok, m + 1)
                        for u in range(2):
                            h = slice(u * L, (u + 1) * L)
                            last = nc.vector.scalar_tensor_tensor(out=o2[:, t % 2, b, u], in0=av[h, :, 0:DV], scalar=LAMU[h],
                                                                  in1=bc(rs[h, b], DV), op0=ALU.mult, op1=ALU.mult)
                        last.then_inc(o2_ok, 1)

                    dve.sem_inc(o2_ok, 1)
                    softmax(0, 0)
                    with dve.Fori(0, NT // TB) as it:
                        for t in range(TB):
                            n = it * TB + t
                            softmax(t + 1, n + 1)
                            combine(t, 0, n)
                            combine(t, 1, n)
                            dve.wait_ge(sq_ok, n + 1)
                            nc.vector.tensor_reduce(var[:, t % 2], sq[:, t % 2], op=ALU.add, axis=AX.X).then_inc(ss_ok, 1)
                            dve.wait_ge(ss_ok, n + 1)
                            nc.vector.tensor_scalar(var[:, t % 2], var[:, t % 2], 1.0 / DV, LN_EPS, ALU.mult, ALU.add).then_inc(var_ok, 1)

                @block.scalar
                def _(act):
                    def piece(par, i, n):
                        act.wait_ge(piece_mm, n)
                        if i < QK and i % 2 == 0:
                            for h in range(4):
                                last = nc.scalar.activation(qb[:, par, :, i // 2, h, :], PS[:, JB, :].rearrange("p (b l) -> p b l", l=L),
                                                            ACT.Copy, scale=QMASK[:, h:h + 1])
                        elif i < QK:
                            last = nc.scalar.activation(kT[:, par, i // 2], PS[:, JB, :], ACT.Copy)
                        else:
                            s = 2 * (i - QK)
                            for u in range(2):
                                last = nc.scalar.activation(
                                    vb[u * L:(u + 1) * L, par, s:s + 2, :, u, 0:DV],
                                    PS[u * L:(u + 1) * L, JB, :].rearrange("p (b m v e) -> p b m v e", b=2, v=2, e=DV)[:, :, :, u, :], ACT.Copy)
                        last.then_inc(piece_ok, 1)

                    def exps(t, n):
                        act.wait_ge(sub_ok, n + 1)
                        nc.scalar.activation(sc[:, t % 2], sc[:, t % 2], ACT.Exp).then_inc(exp_ok, 1)

                    act.wait_ge(init, 3)
                    act.sem_inc(piece_ok, 1)
                    for i in range(NPC):
                        piece(0, i, i + 1)
                    exps(0, 0)
                    with act.Fori(0, NT // TB) as it:
                        for t in range(TB):
                            n = it * TB + t
                            par, i, pc = (t // GT + 1) % 2, 2 * (t % GT), it * 2 * NPC + NPC + 2 * t
                            for b in range(2):
                                act.wait_ge(eT_mm, 2 * n + b + 1)
                                nc.scalar.activation(eT[:, b].rearrange("p m l -> p (m l)"), PS[:, EB + b, :], ACT.Copy).then_inc(eT_ok, 1)
                            exps(t + 1, n + 1)
                            piece(par, i, pc + 1)
                            piece(par, i + 1, pc + 2)

                @block.gpsimd
                def _(pool):
                    def spread(g, par):
                        nc.gpsimd.tensor_copy(zd[:, par], ZT[0:C, bass.ds(g * GTOK, GTOK)].rearrange("p (b l) -> p b l", l=L).unsqueeze(2)
                                              .broadcast_to([C, GB, 2, L])).then_inc(zd_ok, 1)

                    nc.gpsimd.memset(vb[:], 0.0).then_inc(init, 1)
                    pool.wait_ge(init, 1)
                    nc.gpsimd.memset(vb[0:L, :, :, :, 0, DV:ONE], 1.0)
                    nc.gpsimd.memset(ZT[:, NG * GTOK:], 0.0).then_inc(init, 1)
                    pool.wait_ge(init, 2)
                    nc.gpsimd.memset(vb[L:P, :, :, :, 1, DV:ONE], 1.0)
                    nc.gpsimd.memset(ZT[C:C + 1, 0:NG * GTOK], 1.0).then_inc(init, 1)
                    pool.wait_ge(init, 3)
                    spread(0, 0)
                    pool.sem_inc(o_ok, PRIME)
                    pool.wait_ge(zd_ok, 1)
                    nc.gpsimd.tensor_tensor(H[:], H[:], over(BOUT[:], NT), ALU.add).then_inc(init, 1)
                    pool.wait_ge(init, 4)
                    pool.sem_inc(or_ok, 1)
                    with pool.Fori(0, NT // TB) as it:
                        for t in range(TB):
                            n = it * TB + t
                            if t % GT == 0:
                                wait_apart(pool, or_ok, n + 1)
                                spread(it * 2 + t // GT + 1, (t // GT + 1) % 2)
                                wait_apart(pool, zd_ok, it * 2 + t // GT + 2)
                            for b in range(2):
                                wait_apart(pool, *((or_ok, n + 1) if b == 0 else (o_ok, 2 * n + 1 + PRIME)), o2_ok, 2 * n + b + 2)
                                both = [o2[:, t % 2, b, u].rearrange("p m e -> p (m e)").unsqueeze(1) for u in range(2)]
                                nc.gpsimd.tensor_tensor(O[b * L:(b + 1) * L, bass.ds(n, 1), :], both[0], both[1], ALU.add).then_inc(o_ok, 1)
                            wait_apart(pool, o_ok, 2 * n + 2 + PRIME)
                            o = O[:, bass.ds(n, 1), :]
                            nc.gpsimd.tensor_tensor(sq[:, t % 2].rearrange("p m e -> p (m e)").unsqueeze(1), o, o, ALU.mult).then_inc(sq_ok, 1)
                            wait_apart(pool, var_ok, n + 1)
                            nc.gpsimd.tensor_tensor(OR[:, bass.ds(n, 1), :], var[:, t % 2].unsqueeze(1), NHALF[:, 0:NH1].unsqueeze(1),
                                                    ALU.pow).then_inc(or_ok, 1)

            with ExitStack() as ctx:
                on = tile(ctx, "g_on", [P, STREAMS, GT, NH1, DV])
                sg = tile(ctx, "g_sg", [P, STREAMS, 2, GTOK])
                og = tile(ctx, "g_og", [P, STREAMS, 2, GTOK])
                on_ok, g_mm, sg_ok, oT_mm, og_ok, out_mm, h_ok = (
                    sem(ctx, "g_" + n) for n in ("on_ok", "g_mm", "sg_ok", "oT_mm", "og_ok", "out_mm", "h_ok"))
                block = phase_block(ctx)

                @block.vector
                def _(dve):
                    with dve.Fori(0, NG // STREAMS) as it:
                        ns = [it * STREAMS + s + 1 for s in range(STREAMS)]
                        for s, n in enumerate(ns):
                            nc.vector.tensor_tensor(on[:, s], tiles(O, n - 1).rearrange("p t (m e) -> p t m e", e=DV),
                                                    tiles(OR, n - 1).unsqueeze(3).broadcast_to([P, GT, NH1, DV]), ALU.mult).then_inc(on_ok, 1)
                        for s, n in enumerate(ns):
                            dve.wait_ge(sg_ok, n)
                            dve.wait_ge(oT_mm, n)
                            nc.vector.tensor_tensor(og[:, s], sg[:, s], PS[:, 4 * s + 2:4 * s + 4, :], ALU.mult).then_inc(og_ok, 1)
                        for s, n in enumerate(ns):
                            dve.wait_ge(out_mm, n)
                            h = tiles(H, n - 1)
                            nc.vector.tensor_tensor(h, h, PS[:, 4 * s, 0:GT * C].rearrange("p (t c) -> p t c", c=C), ALU.add).then_inc(h_ok, 1)

                @block.scalar
                def _(act):
                    with act.Fori(0, NG // STREAMS) as it:
                        for s in range(STREAMS):
                            act.wait_ge(g_mm, it * STREAMS + s + 1)
                            nc.scalar.activation(sg[:, s], PS[:, 4 * s:4 * s + 2, :], ACT.Sigmoid).then_inc(sg_ok, 1)

                @block.tensor
                def _(pe):
                    pe.sem_inc(h_ok, 1)
                    with pe.Fori(0, NG // STREAMS) as it:
                        ns = [it * STREAMS + s + 1 for s in range(STREAMS)]
                        for s, n in enumerate(ns):
                            wait_apart(pe, h_ok, it * STREAMS + 1)
                            for hf in range(2):
                                last = nc.tensor.matmul(PS[:, 4 * s + hf, :], WG[:, hf * P:(hf + 1) * P], ZT[:, bass.ds((n - 1) * GTOK, GTOK)],
                                                        start=True, stop=True)
                            last.then_inc(g_mm, 1)
                        for s, n in enumerate(ns):
                            wait_apart(pe, on_ok, n)
                            for t in range(GT):
                                for hf in range(2):
                                    last = nc.tensor.transpose(PS[:, 4 * s + 2 + hf, t * P:(t + 1) * P],
                                                               on[:, s, t, 4 * hf:4 * hf + 4].rearrange("p m e -> p (m e)"), ident)
                            last.then_inc(oT_mm, 1)
                        for s, n in enumerate(ns):
                            wait_apart(pe, og_ok, n)
                            for t in range(GT):
                                for i, (src, w) in enumerate(((og, 0), (sg, 1))):
                                    for hf in range(2):
                                        last = nc.tensor.matmul(PS[:, 4 * s, t * C:(t + 1) * C], src[:, s, hf, t * P:(t + 1) * P],
                                                                WOUT2[:, w, hf], start=(i == 0 and hf == 0), stop=(i == 1 and hf == 1))
                            last.then_inc(out_mm, 1)

        features(1)
        experts(1)

        with ExitStack() as ctx:
            out_done = sem(ctx, "out_done")
            block = phase_block(ctx)

            @block.sync
            def _(sp):
                sp.dma_start(out.rearrange("(t p) c -> p t c", p=P), H[:]).then_inc(out_done, 16)
                sp.wait_ge(out_done, 16)


def kernel(**inputs):
    import numpy as _np
    import concourse.bacc as _bacc
    from concourse import mybir as _mybir
    from concourse.bass_utils import run_bass_kernel_spmd as _run

    a = {n: _np.asarray(v) for n, v in inputs.items()}
    consts, cols = constants()

    empty = _np.zeros(((NET + 1) * ETOK, RW_), _np.float32)
    empty[:, C] = 2 * NTOK + _np.arange(len(empty))

    def rows(v):
        return _np.broadcast_to(v[None], (P,) + v.shape)

    def up_weights(w1, w3):
        ne, hid, c = w1.shape
        full = hid // P * P
        t1, t3 = w1.transpose(0, 2, 1), w3.transpose(0, 2, 1)
        last = _np.zeros((ne, c, P), w1.dtype)
        last[:, :, 0:hid - full] = t1[:, :, full:]
        last[:, :, C:C + hid - full] = t3[:, :, full:]
        one = _np.concatenate([t1[:, :, :full], t3[:, :, :full], last], 2)
        return _np.concatenate([one, one], 1)

    def down_weights(w2):
        ne, c, hid = w2.shape
        chunks = hid // P + 1
        t = _np.zeros((ne, chunks * P, c), w2.dtype)
        t[:, :hid] = w2.transpose(0, 2, 1)
        return t.reshape(ne, chunks, P, c).transpose(0, 2, 1, 3)

    host = {
        "consts": consts, "empty": empty,
        "x": a["x"][:, 0],
        "L0_tok_W": a["L0_tok_W"],
        "L0_attn_Wq": a["L0_attn_Wq"], "L0_attn_Wk": a["L0_attn_Wk"], "L0_attn_Wv": a["L0_attn_Wv"],
        "L0_attn_WoT": a["L0_attn_Wo"].T,
        "L0_ffn_wq": a["L0_ffn_wq"], "L0_ffn_wk": a["L0_ffn_wk"],
        "L0_ffn_wvT": a["L0_ffn_wv"].T, "L0_ffn_woT": a["L0_ffn_wo"].T,
        "L1_qkv": _np.concatenate([a["L1_attn_Wq"], a["L1_attn_Wkv"]], 1),
        "L1_gate": _np.concatenate([a["L1_attn_Wg"], a["L1_attn_bg"][None]], 0),
        "L1_out": a["L1_attn_Wout"].reshape(2, P, C).transpose(1, 0, 2),
        "router": _np.stack([a["L0_ffn_router_w"].T, a["L1_ffn_router_w"].T], 1),
        "ln_w": _np.stack([a["L0_ffn_ln1_w"], a["L0_ffn_ln2_w"]], 1),
        "ln_rows": rows(_np.stack([a["L0_ffn_ln2_w"], _np.ones(C, _np.float32)])),
        "tok_b": rows(a["L0_tok_b"]), "bout": rows(a["L1_attn_bout"]),
        "ln_head": _np.tile(_np.stack([a["L1_attn_ln_gamma"], a["L1_attn_ln_beta"]], 1), (P // DV, 1)),
        "lam_q": rows(_np.stack([a["L1_attn_lq1"], a["L1_attn_lk1"], a["L1_attn_lq2"], a["L1_attn_lk2"]])),
        "w13_0": up_weights(a["L0_ffn_w1"], a["L0_ffn_w3"]), "w2_0": down_weights(a["L0_ffn_w2"]),
        "w13_1": up_weights(a["L1_ffn_w1"], a["L1_ffn_w3"]), "w2_1": down_weights(a["L1_ffn_w2"]),
    }
    nc = _bacc.Bacc("TRN2", target_bir_lowering=False, num_devices=1)
    arrays, dram = {}, {}
    for name, v in host.items():
        v = _np.ascontiguousarray(v)
        arrays[f"in_{name}"] = v
        dram[name] = nc.dram_tensor(f"in_{name}", v.shape, _mybir.dt.from_np(v.dtype), kind="ExternalInput").ap()
    out = nc.dram_tensor("out", (NTOK, C), _mybir.dt.float32, kind="ExternalOutput").ap()
    build(nc, dram, out, cols)
    r = _run(nc, [arrays], core_ids=[0])
    return r.results[0]["out"].reshape(B, L, C)
```

```python
import math

import numpy as np
import concourse.bass as bass
from concourse import mybir
from contextlib import ExitStack

B = 64
IMG = 128
SIDE = 8
L = SIDE * SIDE
C = 64
P = 128
NTOK = B * L
NT = NTOK // P
GT = 4
NG = NT // GT
GTOK = GT * P
GB = GTOK // L
NF = 7
NOP = 4
NE = 8
HID0, HID1 = 170, 682
NH0, HD = 4, 16
NH1 = 8
DV = 32
LAMBDA_INIT = 0.8 - 0.6 * math.exp(-0.3)
LN_EPS, RMS_EPS = 1e-5, 1e-6
WSCALE = 64.0
STREAMS = 2
NB = 4
ETOK = 256
NET = 40
RW_ = C + 2
assert NET % 8 == 0 and NET * ETOK >= 2 * NTOK + (NE - 1) * ETOK

MAPS = [(0, 0), (1, 0), (0, 1), (1, 1), (3, 2), (2, 3), (3, 3)]


def constants():
    def resize(n):
        scale = n / SIDE
        centre = (np.arange(SIDE) + 0.5) * scale - 0.5
        w = np.maximum(0, 1 - np.abs(centre[None, :] - np.arange(n)[:, None]) / scale)
        return (w / w.sum(0, keepdims=True)).T

    def haar(n, sign):
        m = np.zeros((n // 2, n))
        m[np.arange(n // 2), 2 * np.arange(n // 2)] = 1
        m[np.arange(n // 2), 2 * np.arange(n // 2) + 1] = sign
        return m * 0.7071067811865476

    ops = np.concatenate([resize(IMG // 4) @ haar(IMG // 2, 1) @ haar(IMG, 1),
                          resize(IMG // 4) @ haar(IMG // 2, -1) @ haar(IMG, 1),
                          resize(IMG // 2) @ haar(IMG, 1),
                          resize(IMG // 2) @ haar(IMG, -1)])
    parts = {}

    def add(name, a):
        full = np.zeros((P, a.shape[1]), np.float32)
        full[:a.shape[0]] = a
        parts[name] = full

    p = np.arange(P)
    add("ident", np.eye(P))
    add("fold", (p[:, None] % C == p[None, :] % C).astype(float))
    add("ops_t", ops.T)
    sel = np.zeros((NF, NOP, NOP * SIDE))
    for f, (ro, co) in enumerate(MAPS):
        sel[f, ro, co * SIDE:(co + 1) * SIDE] = 1
    add("map_sel", sel.reshape(NF, -1))
    add("x_diag", (p[:, None] % SIDE == np.arange(SIDE)[None, :]).astype(float))
    same = (p[:, None] // L == p[None, :] // L) & (p[:, None] <= p[None, :])
    add("lin_mask", same / np.maximum(p[None, :] % L, 1))
    inv_freq = 1.0 / 10000.0 ** (np.arange(0, HD, 2, dtype=np.float32) / HD)
    angle = np.outer(np.arange(L, dtype=np.float32), inv_freq).astype(np.float32)
    angle = np.concatenate([angle, angle], -1).T
    add("cos_sin", np.concatenate([np.tile(np.cos(angle), (NH0, 1)), np.tile(np.sin(angle), (NH0, 1))]))
    rot = np.zeros((HD, HD))
    rot[np.arange(8), np.arange(8) + 8] = -1
    rot[np.arange(8) + 8, np.arange(8)] = 1
    q_rot = np.kron(np.eye(NH0), rot)
    add("q_sel", np.concatenate([np.eye(C), q_rot.T], 1))
    rep = np.zeros((C, C // 2))
    for h in range(NH0):
        rep[h * HD:(h + 1) * HD, (h // 2) * HD:(h // 2 + 1) * HD] = np.eye(HD)
    add("k_sel", np.concatenate([rep.T, (q_rot @ rep).T], 1))
    add("causal", np.where(p[:, None] % L >= np.arange(L)[None, :], 0.0, -1e30))
    add("head_mask", ((p[:, None] % C) // HD == np.arange(NH0)[None, :]).astype(float))
    add("before", (p[:, None] < p[None, :]).astype(float))
    add("ones", np.ones((P, P)))
    add("token", p[:, None] + P * np.arange(2 * NT)[None, :])
    add("tile_at", np.tile(ETOK * np.arange(NET, dtype=float), (P, 1)))
    add("first", np.tile(np.arange(NE, 0, -1.0), (P, 1)))
    cols, at = {}, 0
    for name, a in parts.items():
        cols[name] = (at, at + a.shape[1])
        at += a.shape[1]
    return np.concatenate(list(parts.values()), 1).astype(np.float32), cols


def build(nc, d, out, cols):
    F32, F16, I32, U32 = mybir.dt.float32, mybir.dt.float16, mybir.dt.int32, mybir.dt.uint32
    ALU, ACT, AX = mybir.AluOpType, mybir.ActivationFunctionType, mybir.AxisListType
    with ExitStack() as top:
        def tile(ctx, name, shape, dt=F32):
            return ctx.enter_context(nc.sbuf_tensor(name, shape, dt))

        phase_sems = []

        def sem(ctx, name):
            s = ctx.enter_context(nc.semaphore(name))
            if ctx is not top:
                phase_sems.append(s)
            return s

        def phase_block(ctx):
            def clear():
                for s in phase_sems:
                    nc.gpsimd.sem_clear(s)
                phase_sems.clear()
                nc.all_engine_barrier()

            ctx.callback(clear)
            return ctx.enter_context(nc.Block())

        def bc(ap, dims):
            return ap.unsqueeze(2).broadcast_to(list(ap.shape) + [dims])

        def over(ap, n):
            return ap.unsqueeze(1).broadcast_to([ap.shape[0], n, ap.shape[1]])

        PS = top.enter_context(nc.psum_tensor("PS", [P, 8, 512], F32))
        H = tile(top, "H", [P, NT, C])
        KC = tile(top, "KC", [P, sum(b - a for a, b in [cols[k] for k in cols])])

        def k(name, rows=P):
            a, b = cols[name]
            return KC[0:rows, a:b]

        ident = k("ident")
        UCOL = 2 * P + 32
        WC = [tile(top, f"WC{n}", [P, UCOL + P + C], F16) for n in range(2)]
        WO0 = tile(top, "WO0", [C, C])
        VCOL, GCOL = 8 * P, 8 * P + 256
        WE = [tile(top, f"WE{n}", [P, GCOL + 256], F16) for n in range(2)]
        BG = tile(top, "BG", [P, 2])
        WOUT = tile(top, "WOUT", [P, 2, C])
        RW = tile(top, "RW", [C, 2, NE])
        LNW = tile(top, "LNW", [C, 2])
        BTOK = tile(top, "BTOK", [P, C])
        BOUT = tile(top, "BOUT", [P, C])
        LNH = tile(top, "LNH", [P, 2])
        LAMU = tile(top, "LAMU", [P, 1])
        NHALF = tile(top, "NHALF", [P, NT * 8])

        consts_ok = sem(top, "consts_ok")

        with ExitStack() as ctx:
            IM = tile(ctx, "IM", [P, B, IMG])
            A1 = tile(ctx, "A1", [P, B, NOP * SIDE])
            A2 = tile(ctx, "A2", [P, B * SIDE])
            WT = tile(ctx, "WT", [NF, C])
            WX = tile(ctx, "WX", [P, C])
            WD = tile(ctx, "WD", [P, SIDE, C])
            HT = tile(ctx, "HT", [P, NG // 2, SIDE * C])
            WQKVG = tile(ctx, "WQKVG", [P, GCOL + 256])
            RAW = tile(ctx, "RAW", [C, 7, C])
            WKR = tile(ctx, "WKR", [32, C])
            WV0R = tile(ctx, "WV0R", [C, 32])
            WCR = tile(ctx, "WCR", [C, UCOL + P + C])
            VM = tile(ctx, "VM", [P, NH1])
            LQ = tile(ctx, "LQ", [P, 4, HD])
            LP = tile(ctx, "LP", [P, 2, HD])
            LS = tile(ctx, "LS", [P, 2])
            LE = tile(ctx, "LE", [P, 2])
            tok_dram = nc.dram_tensor("tok_scratch", (NTOK, C), F32, kind="Internal").ap()
            NIM = 8
            img_in = [sem(ctx, f"img_in{i}") for i in range(B // NIM)]
            consts_in, weights_in = sem(ctx, "consts_in"), sem(ctx, "weights_in")
            prep_mm, prep_done, w_step = sem(ctx, "prep_mm"), sem(ctx, "prep_done"), sem(ctx, "w_step")
            lam_exp = sem(ctx, "lam_exp")
            rows_mm, rows_copied = sem(ctx, "rows_mm"), sem(ctx, "rows_copied")
            cols_mm, cols_copied = sem(ctx, "cols_mm"), sem(ctx, "cols_copied")
            tok_mm, tok_ready, tok_out, tok_in = (sem(ctx, n) for n in ("tok_mm", "tok_ready", "tok_out", "tok_in"))
            wd_ready = sem(ctx, "wd_ready")
            NWL = 17
            block = phase_block(ctx)

            @block.sync
            def _(sp):
                sp.dma_start(KC[:], d["consts"]).then_inc(consts_in, 16)
                sp.dma_start(WT[:], d["L0_tok_W"]).then_inc(consts_in, 16)
                for i in range(B // NIM):
                    sp.dma_start(IM[:, i * NIM:(i + 1) * NIM, :],
                                 d["x"][i * NIM:(i + 1) * NIM].rearrange("b r c -> r b c")).then_inc(img_in[i], 16)
                tok_rows = tok_dram.rearrange("(t p x) c -> t p (x c)", p=P, x=SIDE)
                for t in range(NG // 2):
                    sp.wait_ge(tok_ready, t + 1)
                    sp.dma_start(tok_rows[t], HT[:, t, :]).then_inc(tok_out, 16)
                    sp.wait_ge(tok_out, 16 * (t + 1))
                    part = slice(t * 2 * GT, (t + 1) * 2 * GT)
                    sp.dma_start(H[:, part], tok_dram.rearrange("(t p) c -> p t c", p=P)[:, part]).then_inc(tok_in, 16)
                sp.wait_ge(tok_in, 16 * (NG // 2))

            @block.scalar
            def _(act):
                for dst, name in ((RAW[:, 0, :], "L0_attn_Wq"), (RAW[:, 1, :], "L0_attn_Wk"), (RAW[:, 2, :], "L0_attn_Wv"),
                                  (RAW[:, 3, :], "L0_attn_WoT"), (RAW[:, 4, :], "L0_ffn_wq"), (WKR[:], "L0_ffn_wk"),
                                  (WV0R[:], "L0_ffn_wvT"), (WO0[:], "L0_ffn_woT"), (WQKVG[:], "L1_qkvg"), (BG[:], "L1_bg"),
                                  (WOUT[:], "L1_out"), (RW[:], "router"), (LNW[:], "ln_w"), (BTOK[:], "tok_b"),
                                  (BOUT[:], "bout"), (LNH[:], "ln_head"), (LQ[:], "lam_q")):
                    act.dma_start(dst, d[name]).then_inc(weights_in, 16)
                act.wait_ge(w_step, 3)
                nc.scalar.activation(LE[:], LS[:], ACT.Exp).then_inc(lam_exp, 1)
                for i in range(B // 16):
                    act.wait_ge(rows_mm, i + 1)
                    nc.scalar.activation(A1[:, i * 16:(i + 1) * 16, :].rearrange("p b o -> p (b o)"),
                                         PS[:, i % 4, :], ACT.Copy).then_inc(rows_copied, 1)
                    act.wait_ge(cols_mm, i + 1)
                    for ro in range(NOP):
                        last = nc.scalar.activation(A2[ro * 32:(ro + 1) * 32, i * P:(i + 1) * P].rearrange("p (b y) -> p b y", b=16),
                                                    PS[0:32, 4 + i % 2, :].rearrange("p (b o y) -> p b o y", o=NOP, y=SIDE)[:, :, ro, :], ACT.Copy)
                    last.then_inc(cols_copied, 1)

            @block.tensor
            def _(pe):
                pe.wait_ge(consts_in, 32)
                nc.tensor.matmul(PS[:, 7, 0:C], k("map_sel", NF), WT[:], start=True, stop=True).then_inc(prep_mm, 1)

                def rows(i):
                    for b in range(16):
                        im = i * 16 + b
                        if im % NIM == 0:
                            pe.wait_ge(img_in[im // NIM], 16)
                        last = nc.tensor.matmul(PS[:, i, b * 32:(b + 1) * 32], IM[:, im, :], k("ops_t"), start=True, stop=True)
                    last.then_inc(rows_mm, 1)

                def columns(i):
                    pe.wait_ge(rows_copied, i + 1)
                    if i >= 2:
                        pe.wait_ge(cols_copied, i - 1)
                    nc.tensor.matmul(PS[0:32, 4 + i % 2, :], k("ops_t"), A1[:, i * 16:(i + 1) * 16, :].rearrange("p b o -> p (b o)"),
                                     start=True, stop=True).then_inc(cols_mm, 1)

                def tokens(i):
                    pe.wait_ge(wd_ready, 1)
                    pe.wait_ge(cols_copied, i + 1)
                    nc.tensor.matmul(PS[:, i, :], A2[:, i * P:(i + 1) * P], WD[:].rearrange("p x c -> p (x c)"),
                                     start=True, stop=True).then_inc(tok_mm, 1)

                last_i = B // 16 - 1
                for i in range(last_i + 1):
                    rows(i)
                    if i >= 1:
                        columns(i - 1)
                    if i >= 2:
                        tokens(i - 2)
                columns(last_i)
                tokens(last_i - 1)
                pe.wait_ge(weights_in, 16 * NWL)
                for col, lhs, rhs, n in ((0, RAW[:, 0, :], RAW[:, 1, :], C), (64, RAW[:, 2, :], RAW[:, 3, :], C),
                                         (128, RAW[:, 4, :], k("q_sel", C), P), (256, WKR[:], k("k_sel", 32), P)):
                    last = nc.tensor.matmul(PS[0:C, 6, col:col + n], lhs, rhs, start=True, stop=True)
                last.then_inc(prep_mm, 1)
                tokens(last_i)

            @block.vector
            def _(dve):
                dve.wait_ge(weights_in, 16 * NWL)
                nc.vector.memset(NHALF[:], -0.5).then_inc(consts_ok, 1)
                nc.vector.tensor_tensor(LP[:], LQ[:, 0::2, :], LQ[:, 1::2, :], ALU.mult).then_inc(w_step, 1)
                dve.wait_ge(w_step, 1)
                nc.vector.tensor_reduce(LS[:], LP[:], op=ALU.add, axis=AX.X).then_inc(w_step, 2)
                dve.wait_ge(prep_mm, 1)
                nc.vector.tensor_copy(WX[:], PS[:, 7, 0:C]).then_inc(w_step, 1)
                dve.wait_ge(w_step, 4)
                nc.vector.tensor_tensor(WD[:], over(WX[:], SIDE), bc(k("x_diag"), C), ALU.mult).then_inc(wd_ready, 1)
                wv = WQKVG[:, VCOL:GCOL].rearrange("p (h e) -> p h e", h=NH1)
                nc.vector.tensor_reduce(VM[:], wv, op=ALU.add, axis=AX.X).then_inc(w_step, 1)
                dve.wait_ge(w_step, 5)
                nc.vector.scalar_tensor_tensor(out=wv, in0=bc(VM[:], DV), scalar=-1.0 / DV, in1=wv, op0=ALU.mult, op1=ALU.add)\
                    .then_inc(w_step, 1)
                dve.wait_ge(w_step, 6)
                nc.vector.tensor_scalar(WE[0][:], WQKVG[:], WSCALE, None, ALU.mult).then_inc(w_step, 1)
                dve.wait_ge(w_step, 7)
                nc.vector.scalar_tensor_tensor(out=WE[1][:], in0=WQKVG[:], scalar=WSCALE, in1=WE[0][:], op0=ALU.mult, op1=ALU.subtract)
                nc.vector.tensor_scalar(LNH[:], LNH[:], 1 - LAMBDA_INIT, None, ALU.mult)
                nc.vector.memset(LAMU[0:L], 1.0)
                dve.wait_ge(lam_exp, 1)
                nc.vector.scalar_tensor_tensor(out=LAMU[L:P], in0=LE[L:P, 1:2], scalar=-LAMBDA_INIT, in1=LE[L:P, 0:1],
                                               op0=ALU.add, op1=ALU.subtract)

                def tokens(t):
                    dve.wait_ge(tok_mm, t + 1)
                    nc.vector.tensor_tensor(HT[:, t, :].rearrange("p (x c) -> p x c", x=SIDE),
                                            PS[:, t, :].rearrange("p (x c) -> p x c", x=SIDE),
                                            over(BTOK[:], SIDE), ALU.add).then_inc(tok_ready, 1)

                for t in range(NG // 2 - 1):
                    tokens(t)
                dve.wait_ge(prep_mm, 2)
                nc.vector.tensor_copy(WCR[:, UCOL:UCOL + C], PS[0:C, 6, 0:64])
                nc.vector.tensor_copy(WCR[:, UCOL + C:], PS[0:C, 6, 0:128])
                nc.vector.tensor_scalar(WCR[:, 0:P], PS[0:C, 6, 128:256], LNW[:, 0:1], HD ** -0.5, ALU.mult, ALU.mult)
                nc.vector.tensor_scalar(WCR[:, P:2 * P], PS[0:C, 6, 256:384], LNW[:, 0:1], None, ALU.mult)
                nc.vector.tensor_scalar(WCR[:, 2 * P:UCOL], WV0R[:], LNW[:, 0:1], None, ALU.mult).then_inc(w_step, 1)
                dve.wait_ge(w_step, 8)
                nc.vector.tensor_scalar(WC[0][0:C], WCR[:], WSCALE, None, ALU.mult).then_inc(w_step, 1)
                dve.wait_ge(w_step, 9)
                nc.vector.scalar_tensor_tensor(out=WC[1][0:C], in0=WCR[:], scalar=WSCALE, in1=WC[0][0:C], op0=ALU.mult, op1=ALU.subtract)\
                    .then_inc(w_step, 1)
                nc.vector.tensor_copy(WC[0][C:P], WC[0][0:C])
                dve.wait_ge(w_step, 10)
                nc.vector.tensor_copy(WC[1][C:P], WC[1][0:C]).then_inc(prep_done, 1)
                tokens(NG // 2 - 1)

        X2 = tile(top, "X2", [P, NT, C])
        LG = tile(top, "LG", [P, NT, NE])
        ROW = tile(top, "ROW", [P, 2, NT, RW_])
        LNB = tile(top, "LNB", [P, C])
        XD = [nc.dram_tensor(f"rows{n}", ((NET + 2) * ETOK, RW_), F32, kind="Internal").ap() for n in range(2)]
        YD = [nc.dram_tensor(f"outs{n}", (2 * NTOK + (NET + 2) * ETOK, C), F32, kind="Internal").ap() for n in range(2)]

        def wait_apart(eng, *waits):
            counts = [eng.snap(eng.to_reg(n)) for n in waits[1::2]]
            eng.wait_ge(consts_ok, 1)
            for what, n in zip(waits[0::2], counts):
                eng.wait_ge(what, n)

        def tiles(a, g):
            return a[:, bass.ds(g * GT, GT), :]

        def staggered(n, *stages):
            for step in range(n + max(lag for _, lag in stages)):
                for stage, lag in stages:
                    if 0 <= step - lag < n:
                        stage(step - lag)

        def norm_phase(nm, src, eps, dst, keep=None):
            NC = 4
            CT = NT // NC
            with ExitStack() as ctx:
                total, ssq, var, rstd, msq, rrms = (tile(ctx, f"{nm}_{f}", [P, NT]) for f in ("total", "ssq", "var", "rstd", "msq", "rrms"))
                cen, sq = (tile(ctx, f"{nm}_{f}", [P, NT, C]) for f in ("cen", "sq"))
                total_ok, cen_ok, sq_ok, ssq_ok, var_ok, rstd_ok, msq_ok, rrms_ok, both_ok, kept_ok, z_ok, zT_mm, zT_ok, pad_ok = (
                    sem(ctx, f"{nm}_{f}") for f in ("total_ok", "cen_ok", "sq_ok", "ssq_ok", "var_ok", "rstd_ok", "msq_ok", "rrms_ok",
                                                    "both_ok", "kept_ok", "z_ok", "zT_mm", "zT_ok", "pad_ok"))
                block = phase_block(ctx)
                part = [slice(c * CT, (c + 1) * CT) for c in range(NC)]

                @block.vector
                def _(dve):
                    def centre(c):
                        nc.vector.tensor_reduce(total[:, part[c]], src[:, part[c]], op=ALU.add, axis=AX.X).then_inc(total_ok, 1)
                        dve.wait_ge(total_ok, c + 1)
                        nc.vector.scalar_tensor_tensor(out=cen[:, part[c]], in0=bc(total[:, part[c]], C), scalar=-1.0 / C,
                                                       in1=src[:, part[c]], op0=ALU.mult, op1=ALU.add).then_inc(cen_ok, 1)

                    def variance(c):
                        dve.wait_ge(sq_ok, c + 1)
                        nc.vector.tensor_reduce(ssq[:, part[c]], sq[:, part[c]], op=ALU.add, axis=AX.X).then_inc(ssq_ok, 1)
                        dve.wait_ge(ssq_ok, c + 1)
                        nc.vector.tensor_scalar(var[:, part[c]], ssq[:, part[c]], 1.0 / C, eps, ALU.mult, ALU.add).then_inc(var_ok, 1)

                    def mean_square(c):
                        v, m = rstd[:, part[c]], msq[:, part[c]]
                        dve.wait_ge(rstd_ok, c + 1)
                        nc.vector.scalar_tensor_tensor(out=m, in0=ssq[:, part[c]], scalar=1.0 / C, in1=v,
                                                       op0=ALU.mult, op1=ALU.mult).then_inc(msq_ok, 1)
                        dve.wait_ge(msq_ok, 3 * c + 1)
                        nc.vector.tensor_tensor(m, m, v, ALU.mult).then_inc(msq_ok, 1)
                        dve.wait_ge(msq_ok, 3 * c + 2)
                        nc.vector.tensor_scalar(m, m, RMS_EPS, None, ALU.add).then_inc(msq_ok, 1)
                        nc.vector.tensor_tensor(keep[:, part[c]], cen[:, part[c]], bc(v, C), ALU.mult).then_inc(kept_ok, 1)

                    def scale(c):
                        if keep is None:
                            dve.wait_ge(rstd_ok, c + 1)
                            factor = rstd
                        else:
                            dve.wait_ge(kept_ok, c + 1)
                            dve.wait_ge(rrms_ok, c + 1)
                            nc.vector.tensor_tensor(rrms[:, part[c]], rstd[:, part[c]], rrms[:, part[c]], ALU.mult).then_inc(both_ok, 1)
                            dve.wait_ge(both_ok, c + 1)
                            factor = rrms
                        nc.vector.tensor_tensor(cen[:, part[c]], cen[:, part[c]], bc(factor[:, part[c]], C), ALU.mult).then_inc(z_ok, 1)

                    def low(c):
                        for g in range(c * NG // NC, (c + 1) * NG // NC):
                            dve.wait_ge(zT_ok, g + 1)
                            cols_g = slice(g * GTOK, (g + 1) * GTOK)
                            nc.vector.tensor_tensor(dst[C:P, cols_g], PS[0:C, g, :], dst[0:C, cols_g], ALU.subtract)

                    if keep is None:
                        staggered(NC, (centre, 0), (variance, 1), (scale, 3), (low, 4))
                    else:
                        staggered(NC, (centre, 0), (variance, 1), (mean_square, 3), (scale, 5), (low, 6))

                @block.scalar
                def _(act):
                    for c in range(NC):
                        act.wait_ge(cen_ok, c + 1)
                        nc.scalar.activation(sq[:, part[c]], cen[:, part[c]], ACT.Square).then_inc(sq_ok, 1)
                    for g in range(NG):
                        act.wait_ge(zT_mm, g + 1)
                        nc.scalar.activation(dst[0:C, g * GTOK:(g + 1) * GTOK], PS[0:C, g, :], ACT.Copy).then_inc(zT_ok, 1)

                @block.gpsimd
                def _(pool):
                    def power(c):
                        pool.wait_ge(var_ok, c + 1)
                        nc.gpsimd.tensor_tensor(rstd[:, part[c]], var[:, part[c]], NHALF[:, 0:CT], ALU.pow).then_inc(rstd_ok, 1)

                    def rms_power(c):
                        pool.wait_ge(msq_ok, 3 * c + 3)
                        nc.gpsimd.tensor_tensor(rrms[:, part[c]], msq[:, part[c]], NHALF[:, 0:CT], ALU.pow).then_inc(rrms_ok, 1)

                    staggered(NC, *((power, 0),) + (() if keep is None else ((rms_power, 2),)))
                    if dst.shape[1] > NTOK:
                        nc.gpsimd.memset(dst[:, NTOK:], 0.0).then_inc(pad_ok, 1)

                @block.tensor
                def _(pe):
                    for g in range(NG):
                        pe.wait_ge(z_ok, g * GT // CT + 1)
                        for t in range(GT):
                            last = nc.tensor.transpose(PS[0:C, g, t * P:(t + 1) * P], cen[:, g * GT + t], ident)
                        last.then_inc(zT_mm, 1)

        b_ctx = ExitStack()
        with b_ctx:
            BS = tile(b_ctx, "b_BS", [P, NTOK], F16)
            norm_phase("b_ln", H, LN_EPS, BS)
            with ExitStack() as ctx:
                uh = tile(ctx, "b_uh", [P, STREAMS, GTOK], F16)
                ul = tile(ctx, "b_ul", [P, STREAMS, GTOK], F16)
                val = tile(ctx, "b_val", [P, STREAMS, GT, C])
                att = tile(ctx, "b_att", [P, STREAMS, GT, P])
                filled, lnb_in = sem(ctx, "b_filled"), sem(ctx, "b_lnb_in")
                u_mm, uh_ok, ul_ok, v_mm, v_ok, sc_mm, att_ok, ctx_mm, h_ok = (
                    sem(ctx, "b_" + n) for n in ("u_mm", "uh_ok", "ul_ok", "v_mm", "v_ok", "sc_mm", "att_ok", "ctx_mm", "h_ok"))
                block = phase_block(ctx)

                @block.sync
                def _(sp):
                    sp.dma_start(LNB[:], d["ln_rows"]).then_inc(lnb_in, 16)
                    for rows in XD:
                        sp.dma_start(rows, d["empty"]).then_inc(filled, 16)
                    sp.wait_ge(lnb_in, 16)
                    sp.wait_ge(filled, 16 * len(XD))

                @block.vector
                def _(dve):
                    with dve.Fori(0, NG // NB) as it:
                        def low(g):
                            s, n = g % STREAMS, it * NB + g
                            dve.wait_ge(uh_ok, n + 1)
                            nc.vector.scalar_tensor_tensor(out=ul[:, s], in0=PS[:, 4 * s, :], scalar=1 / WSCALE, in1=uh[:, s],
                                                           op0=ALU.mult, op1=ALU.subtract).then_inc(ul_ok, 1)

                        def masked(g):
                            s, n = g % STREAMS, it * NB + g
                            dve.wait_ge(sc_mm, n + 1)
                            nc.vector.scalar_tensor_tensor(
                                out=att[:, s], in0=PS[:, 4 * s + 2, :].rearrange("p (t l) -> p t l", l=P), scalar=0.0,
                                in1=over(k("lin_mask"), GT), op0=ALU.max, op1=ALU.mult).then_inc(att_ok, 1)

                        def add(g):
                            s, n = g % STREAMS, it * NB + g
                            dve.wait_ge(ctx_mm, n + 1)
                            h = tiles(H, n)
                            nc.vector.tensor_tensor(h, h, PS[:, 4 * s + 3, 0:GT * C].rearrange("p (t c) -> p t c", c=C), ALU.add).then_inc(h_ok, 1)

                        staggered(NB, (add, 2), (masked, 1), (low, 0))

                @block.scalar
                def _(act):
                    with act.Fori(0, NG // NB) as it:
                        for g in range(NB):
                            s, n = g % STREAMS, it * NB + g
                            act.wait_ge(u_mm, n + 1)
                            nc.scalar.activation(uh[:, s], PS[:, 4 * s, :], ACT.Copy, scale=1 / WSCALE).then_inc(uh_ok, 1)
                            act.wait_ge(v_mm, n + 1)
                            nc.scalar.activation(val[:, s], PS[:, 4 * s + 1, 0:GT * C].rearrange("p (t c) -> p t c", c=C), ACT.Copy,
                                                 scale=1 / WSCALE).then_inc(v_ok, 1)

                @block.tensor
                def _(pe):
                    pe.sem_inc(h_ok, STREAMS)
                    with pe.Fori(0, NG // NB) as it:
                        def project(g):
                            s, n = g % STREAMS, it * NB + g
                            for w in range(2):
                                last = nc.tensor.matmul(PS[:, 4 * s, :], WC[w][:, UCOL:UCOL + P], BS[:, bass.ds(n * GTOK, GTOK)],
                                                        start=(w == 0), stop=(w == 1))
                            last.then_inc(u_mm, 1)
                            for t in range(GT):
                                for w in range(2):
                                    last = nc.tensor.matmul(PS[:, 4 * s + 1, t * C:(t + 1) * C], BS[:, bass.ds(n * GTOK + t * P, P)],
                                                            WC[w][:, UCOL + P:UCOL + P + C], start=(w == 0), stop=(w == 1))
                            last.then_inc(v_mm, 1)

                        def scores(g):
                            s, n = g % STREAMS, it * NB + g
                            wait_apart(pe, ul_ok, n + 1)
                            for t in range(GT):
                                for w, u in enumerate((uh, ul)):
                                    last = nc.tensor.matmul(PS[:, 4 * s + 2, t * P:(t + 1) * P], BS[:, bass.ds(n * GTOK + t * P, P)],
                                                            u[:, s, t * P:(t + 1) * P], start=(w == 0), stop=(w == 1))
                            last.then_inc(sc_mm, 1)

                        def context(g):
                            s, n = g % STREAMS, it * NB + g
                            wait_apart(pe, att_ok, n + 1, v_ok, n + 1, h_ok, n + 1)
                            for t in range(GT):
                                last = nc.tensor.matmul(PS[:, 4 * s + 3, t * C:(t + 1) * C], att[:, s, t, :], val[:, s, t, :],
                                                        start=True, stop=True)
                            last.then_inc(ctx_mm, 1)

                        staggered(NB, (context, 2), (scores, 1), (project, 0))

        c_ctx = ExitStack()
        with c_ctx:
            NS = tile(c_ctx, "c_NS", [P, (NG + 2) * GTOK], F16)
            norm_phase("c_ln", H, LN_EPS, NS, X2)

            with ExitStack() as ctx:
                KV, ONE = 2, HD + 1
                q2 = tile(ctx, "c_q2", [P, 2, GTOK])
                qb = tile(ctx, "c_qb", [P, 2, GB, NH0, L])
                kc = tile(ctx, "c_kc", [P, 2, GTOK])
                vb = tile(ctx, "c_vb", [P, 2, GB, KV, ONE])
                zd = tile(ctx, "c_zd", [P, 2, GB, 2, L], F16)
                sc = tile(ctx, "c_sc", [P, 2, GB * KV, L])
                mx = tile(ctx, "c_mx", [P, 2, GB * KV])
                eT = tile(ctx, "c_eT", [P, GB, P])
                rs = tile(ctx, "c_rs", [P, GB, KV])
                y = tile(ctx, "c_y", [P, GT, KV, 2, HD])
                yT = tile(ctx, "c_yT", [C, GTOK])
                names = ("init", "zd_ok", "k_mm", "k_ok", "q_mm", "q2_ok", "f_mm", "qb_ok", "v_mm", "vb_ok", "sc_mm", "sm_ok", "mx_ok",
                         "sub_ok", "exp_ok", "eT_mm", "eT_ok", "av_mm", "rs_ok", "y_ok", "yT_mm", "yT_ok", "o_mm", "x2_ok", "h_ok")
                (init, zd_ok, k_mm, k_ok, q_mm, q2_ok, f_mm, qb_ok, v_mm, vb_ok, sc_mm, sm_ok, mx_ok,
                 sub_ok, exp_ok, eT_mm, eT_ok, av_mm, rs_ok, y_ok, yT_mm, yT_ok, o_mm, x2_ok, h_ok) = (sem(ctx, "c_" + n) for n in names)
                block = phase_block(ctx)
                EB, AB, JB = 4, 6, 7

                @block.tensor
                def _(pe):
                    def keys(g, JB=JB):
                        for w in range(2):
                            last = nc.tensor.matmul(PS[:, JB, :], WC[w][:, P:2 * P], NS[:, bass.ds(g * GTOK, GTOK)], start=(w == 0), stop=(w == 1))
                        last.then_inc(k_mm, 1)

                    def queries(g, JB=JB):
                        for w in range(2):
                            last = nc.tensor.matmul(PS[:, JB, :], WC[w][:, 0:P], NS[:, bass.ds(g * GTOK, GTOK)], start=(w == 0), stop=(w == 1))
                        last.then_inc(q_mm, 1)

                    def fold(par, JB=JB):
                        nc.tensor.matmul(PS[:, JB, :], k("fold"), q2[:, par], start=True, stop=True).then_inc(f_mm, 1)

                    def values(par, JB=JB):
                        for s in range(GB):
                            for w in range(2):
                                last = nc.tensor.matmul(PS[:, JB, s * 32:(s + 1) * 32], zd[:, par, s].rearrange("p u l -> p (u l)"),
                                                        WC[w][:, 2 * P:2 * P + 32], start=(w == 0), stop=(w == 1))
                        last.then_inc(v_mm, 1)

                    def scores(par):
                        for i in range(GB * KV):
                            s, m = i // KV, i % KV
                            last = nc.tensor.matmul(PS[:, 2 * par + i // 8, i % 8 * L:(i % 8 + 1) * L],
                                                    qb[:, par, s, 2 * m:2 * m + 2].rearrange("p h l -> p (h l)"),
                                                    kc[:, par, s * L:(s + 1) * L], start=True, stop=True)
                            if i % 8 == 7:
                                last.then_inc(sc_mm, 1)

                    for g in range(2):
                        keys(g, 4 * g)
                        queries(g, 4 * g + 1)
                    for g in range(2):
                        pe.wait_ge(q2_ok, g + 1)
                        fold(g, 4 * g + 2)
                        pe.wait_ge(zd_ok, g + 1)
                        values(g, 4 * g + 3)
                    pe.wait_ge(k_ok, 2)
                    pe.wait_ge(vb_ok, 2)
                    scores(0)
                    def turn_outputs(n):
                        wait_apart(pe, y_ok, n + 1)
                        for t in range(GT):
                            last = nc.tensor.transpose(PS[0:C, AB, t * P:(t + 1) * P], y[:, t].rearrange("p m u e -> p (m u e)"), ident)
                        last.then_inc(yT_mm, 1)

                    def project(n):
                        wait_apart(pe, yT_ok, n + 1)
                        for t in range(GT):
                            last = nc.tensor.matmul(PS[:, AB, t * C:(t + 1) * C], yT[:, t * P:(t + 1) * P], WO0[:], start=True, stop=True)
                        last.then_inc(o_mm, 1)

                    def slot(n, par, first=False):
                        wait_apart(pe, vb_ok, n + 2)
                        keys(n + 2)
                        for hf in range(2):
                            wait_apart(pe, exp_ok, 2 * n + hf + 1)
                            for c in range(4 * hf, 4 * hf + 4):
                                last = nc.tensor.transpose(PS[:, EB + hf, c % 4 * P:(c % 4 + 1) * P],
                                                           sc[:, par, 2 * c:2 * c + 2, :].rearrange("p m l -> p (m l)"), ident)
                            last.then_inc(eT_mm, 1)
                        wait_apart(pe, k_ok, n + 3)
                        queries(n + 2)
                        scores(1 - par)
                        if not first:
                            turn_outputs(n - 1)
                        wait_apart(pe, q2_ok, n + 3)
                        fold(par)
                        if not first:
                            project(n - 1)
                        wait_apart(pe, *((eT_ok, 2 * n + 2) + (() if first else (x2_ok, n))))
                        for s in range(GB):
                            last = nc.tensor.matmul(PS[:, AB, s * KV * ONE:(s + 1) * KV * ONE], eT[:, s],
                                                    vb[:, par, s].rearrange("p m e -> p (m e)"), start=True, stop=True)
                        last.then_inc(av_mm, 1)
                        wait_apart(pe, qb_ok, n + 3, zd_ok, n + 3)
                        values(par)

                    slot(0, 0, first=True)
                    slot(1, 1)
                    with pe.Fori(1, NG // 2) as it:
                        slot(it * 2, 0)
                        slot(it * 2 + 1, 1)
                    turn_outputs(NG - 1)
                    project(NG - 1)

                @block.vector
                def _(dve):
                    def rotary(dst, mm, ok, par, n, JB=JB):
                        dve.wait_ge(mm, n)
                        nc.vector.scalar_tensor_tensor(out=dst[:, par].rearrange("p (b l) -> p b l", l=L),
                                                       in0=PS[:, JB, :].rearrange("p (b l) -> p b l", l=L), scalar=1 / WSCALE,
                                                       in1=over(k("cos_sin"), GB), op0=ALU.mult, op1=ALU.mult).then_inc(ok, 1)

                    def softmax(par, n):
                        halves = [(slice(hf * 8, (hf + 1) * 8), 2 * n + hf + 1) for hf in range(2)]
                        for hf, (c, m) in enumerate(halves):
                            dve.wait_ge(sc_mm, m)
                            nc.vector.tensor_tensor(sc[:, par, c], PS[:, 2 * par + hf, :].rearrange("p (m l) -> p m l", l=L),
                                                    over(k("causal"), 8), ALU.add).then_inc(sm_ok, 1)
                            dve.wait_ge(sm_ok, m)
                            nc.vector.tensor_reduce(mx[:, par, c], sc[:, par, c], op=ALU.max, axis=AX.X).then_inc(mx_ok, 1)
                            dve.wait_ge(mx_ok, m)
                            nc.vector.tensor_tensor(sc[:, par, c], sc[:, par, c], bc(mx[:, par, c], L), ALU.subtract).then_inc(sub_ok, 1)

                    for g in range(2):
                        rotary(kc, k_mm, k_ok, g, g + 1, 4 * g)
                        rotary(q2, q_mm, q2_ok, g, g + 1, 4 * g + 1)
                    softmax(0, 0)

                    def add(n):
                        dve.wait_ge(o_mm, n + 1)
                        x2 = tiles(X2, n)
                        nc.vector.tensor_tensor(x2, x2, PS[:, AB, 0:GT * C].rearrange("p (t c) -> p t c", c=C), ALU.add).then_inc(x2_ok, 1)
                        dve.wait_ge(x2_ok, n + 1)
                        h = tiles(H, n)
                        nc.vector.tensor_tensor(h, h, x2, ALU.add).then_inc(h_ok, 1)

                    def slot(n, par, first=False):
                        rotary(kc, k_mm, k_ok, par, n + 3)
                        rotary(q2, q_mm, q2_ok, par, n + 3)
                        softmax(1 - par, n + 1)
                        if not first:
                            add(n - 1)
                        dve.wait_ge(av_mm, n + 1)
                        av = PS[:, AB, 0:GB * KV * ONE].rearrange("p (s m e) -> p s m e", m=KV, e=ONE)
                        nc.vector.reciprocal(rs[:], av[:, :, :, HD]).then_inc(rs_ok, 1)
                        dve.wait_ge(rs_ok, n + 1)
                        for u in range(2):
                            for b in range(2):
                                h = slice(u * L, (u + 1) * L)
                                last = nc.vector.tensor_tensor(y[b * L:(b + 1) * L, :, :, u, :], av[h, b::2, :, 0:HD],
                                                               rs[h, b::2, :].unsqueeze(3).broadcast_to([L, GT, KV, HD]), ALU.mult)
                        last.then_inc(y_ok, 1)

                    slot(0, 0, first=True)
                    slot(1, 1)
                    with dve.Fori(1, NG // 2) as it:
                        slot(it * 2, 0)
                        slot(it * 2 + 1, 1)
                    add(NG - 1)

                @block.scalar
                def _(act):
                    def spread(par, n, JB=JB):
                        act.wait_ge(f_mm, n)
                        for h in range(NH0):
                            last = nc.scalar.activation(qb[:, par, :, h, :], PS[:, JB, :].rearrange("p (b l) -> p b l", l=L), ACT.Copy,
                                                        scale=k("head_mask")[:, h:h + 1])
                        last.then_inc(qb_ok, 1)

                    def values(par, n, JB=JB):
                        act.wait_ge(v_mm, n)
                        for m in range(KV):
                            last = nc.scalar.activation(vb[m * L:(m + 1) * L, par, :, m, 0:HD],
                                                        PS[m * L:(m + 1) * L, JB, 0:GB * 32].rearrange("p (b k e) -> p b k e", k=KV, e=HD)[:, :, m, :],
                                                        ACT.Copy, scale=1 / WSCALE)
                        last.then_inc(vb_ok, 1)

                    def exps(par, n):
                        for hf in range(2):
                            c = slice(hf * 8, (hf + 1) * 8)
                            act.wait_ge(sub_ok, 2 * n + hf + 1)
                            nc.scalar.activation(sc[:, par, c], sc[:, par, c], ACT.Exp).then_inc(exp_ok, 1)

                    act.wait_ge(init, 3)
                    for g in range(2):
                        spread(g, g + 1, 4 * g + 2)
                        values(g, g + 1, 4 * g + 3)
                    exps(0, 0)

                    def yt(n):
                        act.wait_ge(yT_mm, n + 1)
                        nc.scalar.activation(yT[:], PS[0:C, AB, :], ACT.Copy).then_inc(yT_ok, 1)

                    def slot(n, par, first=False):
                        for hf in range(2):
                            act.wait_ge(eT_mm, 2 * n + hf + 1)
                            nc.scalar.activation(eT[:, 4 * hf:4 * hf + 4].rearrange("p s l -> p (s l)"), PS[:, EB + hf, :], ACT.Copy).then_inc(eT_ok, 1)
                        if not first:
                            yt(n - 1)
                        spread(par, n + 3)
                        exps(1 - par, n + 1)
                        values(par, n + 3)

                    slot(0, 0, first=True)
                    slot(1, 1)
                    with act.Fori(1, NG // 2) as it:
                        slot(it * 2, 0)
                        slot(it * 2 + 1, 1)
                    yt(NG - 1)

                @block.gpsimd
                def _(pool):
                    def spread(par, g):
                        nc.gpsimd.tensor_copy(zd[:, par], NS[:, bass.ds(g * GTOK, GTOK)].rearrange("p (b l) -> p b l", l=L).unsqueeze(2)
                                              .broadcast_to([P, GB, 2, L])).then_inc(zd_ok, 1)

                    nc.gpsimd.memset(vb[:], 0.0).then_inc(init, 1)
                    pool.wait_ge(init, 1)
                    for m in range(KV):
                        nc.gpsimd.memset(vb[m * L:(m + 1) * L, :, :, m, HD:ONE], 1.0).then_inc(init, 1)
                        pool.wait_ge(init, m + 2)
                    for g in range(2):
                        spread(g, g)
                    with pool.Fori(0, NG // 2) as it:
                        for par in range(2):
                            n = it * 2 + par
                            wait_apart(pool, sc_mm, 2 * n + 2)
                            spread(par, n + 2)

        def features(layer):
            src, eps = (X2, RMS_EPS) if layer == 0 else (H, LN_EPS)
            NC = 4
            CT = NT // NC
            with ExitStack() as ctx:
                nm = f"f{layer}"
                total, ssq, rstd = (tile(ctx, f"{nm}_{f}", [P, NT]) for f in ("total", "ssq", "rstd"))
                cen = tile(ctx, nm + "_cen", [P, NT, C]) if layer == 1 else X2
                sq = tile(ctx, nm + "_sq", [P, NT, C])
                zw = ROW[:, 0, :, 0:C]
                fT = tile(ctx, nm + "_fT", [C, NTOK])
                total_ok, cen_ok, sq_ok, ssq_ok, var_ok, rstd_ok, z_ok, zw_ok, row_ok, fT_mm, fT_ok, lg_mm, lg_ok = (
                    sem(ctx, f"{nm}_{f}") for f in ("total_ok", "cen_ok", "sq_ok", "ssq_ok", "var_ok", "rstd_ok", "z_ok", "zw_ok",
                                                    "row_ok", "fT_mm", "fT_ok", "lg_mm", "lg_ok"))
                block = phase_block(ctx)
                part = [slice(c * CT, (c + 1) * CT) for c in range(NC)]
                LB, TBK = 7, 7

                @block.vector
                def _(dve):
                    def centre(c):
                        nc.vector.tensor_reduce(total[:, part[c]], src[:, part[c]], op=ALU.add, axis=AX.X).then_inc(total_ok, 1)
                        dve.wait_ge(total_ok, c + 1)
                        nc.vector.scalar_tensor_tensor(out=cen[:, part[c]], in0=bc(total[:, part[c]], C), scalar=-1.0 / C,
                                                       in1=src[:, part[c]], op0=ALU.mult, op1=ALU.add).then_inc(cen_ok, 1)

                    def variance(c):
                        dve.wait_ge(sq_ok, c + 1)
                        nc.vector.tensor_reduce(ssq[:, part[c]], sq[:, part[c]], op=ALU.add, axis=AX.X).then_inc(ssq_ok, 1)
                        dve.wait_ge(ssq_ok, c + 1)
                        nc.vector.tensor_scalar(ssq[:, part[c]], ssq[:, part[c]], 1.0 / C, eps, ALU.mult, ALU.add).then_inc(var_ok, 1)

                    def scale(c):
                        dve.wait_ge(rstd_ok, c + 1)
                        z = nc.vector.tensor_tensor(zw[:, part[c]], cen[:, part[c]], bc(rstd[:, part[c]], C), ALU.mult)
                        if layer == 0:
                            z.then_inc(z_ok, 1)
                            dve.wait_ge(z_ok, c + 1)
                            z = nc.vector.tensor_tensor(zw[:, part[c]], zw[:, part[c]], over(LNB[:], CT), ALU.mult)
                        z.then_inc(zw_ok, 1)

                    if layer == 0:
                        staggered(NC, (variance, 0), (scale, 2))
                    else:
                        staggered(NC, (centre, 0), (variance, 1), (scale, 3))
                    dve.wait_ge(lg_mm, NG)
                    nc.vector.tensor_copy(LG[:], PS[:, LB, 0:NT * NE].rearrange("p (t e) -> p t e", e=NE)).then_inc(lg_ok, 1)

                @block.scalar
                def _(act):
                    for c in range(NC):
                        if layer == 1:
                            act.wait_ge(cen_ok, c + 1)
                        nc.scalar.activation(sq[:, part[c]], cen[:, part[c]], ACT.Square).then_inc(sq_ok, 1)
                    for g in range(NG):
                        act.wait_ge(fT_mm, g + 1)
                        nc.scalar.activation(fT[:, g * GTOK:(g + 1) * GTOK], PS[0:C, g % TBK, :], ACT.Copy).then_inc(fT_ok, 1)
                        if g % 2:
                            nc.scalar.activation(ROW[:, 1, part[g // 2], 0:C], zw[:, part[g // 2]], ACT.Copy).then_inc(row_ok, 1)

                @block.gpsimd
                def _(pool):
                    for c in range(NC):
                        pool.wait_ge(var_ok, c + 1)
                        nc.gpsimd.tensor_tensor(rstd[:, part[c]], ssq[:, part[c]], NHALF[:, 0:CT], ALU.pow).then_inc(rstd_ok, 1)

                @block.tensor
                def _(pe):
                    def logits(g):
                        pe.wait_ge(fT_ok, g + 1)
                        for t in range(g * GT, (g + 1) * GT):
                            last = nc.tensor.matmul(PS[:, LB, t * NE:(t + 1) * NE], fT[:, t * P:(t + 1) * P], RW[:, layer, :],
                                                    start=True, stop=True)
                        last.then_inc(lg_mm, 1)

                    for g in range(NG):
                        pe.wait_ge(zw_ok, g * GT // CT + 1)
                        if g >= TBK:
                            pe.wait_ge(fT_ok, g - TBK + 1)
                        for t in range(GT):
                            last = nc.tensor.transpose(PS[0:C, g % TBK, t * P:(t + 1) * P], zw[:, g * GT + t], ident)
                        last.then_inc(fT_mm, 1)
                        if g > 0:
                            logits(g - 1)
                    logits(NG - 1)

        def experts(layer):
            hid = HID0 if layer == 0 else HID1
            full, rest = hid // P, hid % P
            wcols = (2 * full + 1) * P
            units = [(j, j + 1) for j in range(0, full - 1, 2)] + [(full - 1, full)]
            U, LAG, UN = len(units), 2, 8
            PAIRS = 3
            PRIME = 2
            OUT_BANK, TURN_BANK = 6, 7
            rows_dram, out_dram = XD[layer], YD[layer]
            with ExitStack() as ctx:
                nm = f"x{layer}"
                stage = tile(ctx, nm + "_stage", [P, 2, wcols])
                whi = tile(ctx, nm + "_whi", [P, NE * wcols], F16)
                wlo = tile(ctx, nm + "_wlo", [P, NE * wcols], F16)
                w2 = tile(ctx, nm + "_w2", [P, NE * (full + 1) * C])
                xt = tile(ctx, nm + "_xt", [P, UN, 2, RW_])
                xs = tile(ctx, nm + "_xs", [P, UN, ETOK], F16)
                sil = tile(ctx, nm + "_sil", [P, PAIRS, 2 * ETOK])
                hid_t = tile(ctx, nm + "_hid", [P, PAIRS, 2 * ETOK])
                yg = tile(ctx, nm + "_yg", [P, UN, 2, C])
                yid = tile(ctx, nm + "_yid", [P, UN, 2], U32)
                y12 = tile(ctx, nm + "_y12", [P, 2, NT, C])
                rt = [tile(ctx, f"{nm}_rt{n}", [P, NT, NE]) for n in range(10)]
                rv = [tile(ctx, f"{nm}_rv{n}", [P, NT]) for n in range(6)]
                re = [tile(ctx, f"{nm}_re{n}", [P, NE]) for n in range(4)]
                of_tile = tile(ctx, nm + "_of_tile", [P, NET, NE])
                ex_f = tile(ctx, nm + "_ex_f", [P, NET])
                ex_i = tile(ctx, nm + "_ex_i", [P, NET], I32)
                pos = tile(ctx, nm + "_pos", [P, 2, NT], U32)
                (whi_ok, wlo_ok, r_step, r_exp, picked, counted, routed, xT_mm, hi_ok, xs_ok, up_mm, sil_ok, hid_ok, y_mm, yg_ok,
                 sent, placed, y_free, y_sum, h_ok, out_done) = (
                    sem(ctx, f"{nm}_{n}") for n in ("whi_ok", "wlo_ok", "r_step", "r_exp", "picked", "counted", "routed", "xT_mm", "hi_ok",
                                                     "xs_ok", "up_mm", "sil_ok", "hid_ok", "y_mm", "yg_ok", "sent", "placed", "y_free", "y_sum", "h_ok", "out_done"))
                w_in = [sem(ctx, f"{nm}_w_in{i}") for i in range(2)]
                w2_in = sem(ctx, nm + "_w2_in")
                NC = 4
                part = [slice(c * NT // NC, (c + 1) * NT // NC) for c in range(NC)]
                y_in = [sem(ctx, f"{nm}_y_in{c}") for c in range(NC)]
                x_in = [sem(ctx, f"{nm}_x_in{i}") for i in range(UN)]
                y_out = [sem(ctx, f"{nm}_y_out{i}") for i in range(UN)]
                block = phase_block(ctx)
                seq = [(a, u) for a in range(UN) for u in range(U)]

                AHEAD = 2 if U == 1 else 1

                def turned(a):
                    return PS[0:C, TURN_BANK if U == 1 else OUT_BANK + (a + 1) % 2, a % 2 * ETOK:(a % 2 + 1) * ETOK]

                def outputs(a):
                    return OUT_BANK if U == 1 else OUT_BANK + a % 2

                @block.sync
                def _(sp):
                    w13, w2d = d[f"w13_{layer}"], d[f"w2_{layer}"]
                    sp.dma_start(w2[:].rearrange("p (e n) -> p e n", e=NE), w2d.rearrange("e p j c -> p e (j c)")).then_inc(w2_in, 16)
                    for e in range(NE):
                        if e >= 2:
                            sp.wait_ge(wlo_ok, e - 1)
                        sp.dma_start(stage[:, e % 2, :], w13[e]).then_inc(w_in[e % 2], 16)
                    sp.wait_ge(sent, 16 * 2 * NT)

                    def load(a, n):
                        sp.dma_start(xt[:, a], rows_dram[bass.ds(n * ETOK, ETOK), :].rearrange("(b p) n -> p b n", p=P)).then_inc(x_in[a], 16)

                    for a in range(UN):
                        load(a, a)
                    with sp.Fori(0, NET // UN - 1) as it:
                        for a in range(UN):
                            sp.wait_ge(yg_ok, it * UN + a + 1 + PRIME)
                            load(a, (it + 1) * UN + a)
                    for a in range(AHEAD):
                        sp.wait_ge(yg_ok, NET - UN + a + 1 + PRIME)
                        load(a, NET + a)
                    for a in range(UN):
                        sp.wait_ge(y_out[a], 32 * (NET // UN))
                    for c in range(NC):
                        tok = out_dram[0:2 * NTOK, :].rearrange("(k t p) c -> p k t c", k=2, p=P)
                        for kk in range(2):
                            sp.dma_start(y12[:, kk, part[c]], tok[:, kk, part[c]]).then_inc(y_in[c], 16)
                    if layer == 1:
                        for c in range(NC):
                            sp.wait_ge(h_ok, c + 1)
                            sp.dma_start(out.rearrange("(t p) c -> p t c", p=P)[:, part[c]], H[:, part[c]]).then_inc(out_done, 16)
                        sp.wait_ge(out_done, 16 * NC)

                @block.gpsimd
                def _(pool):
                    for c in range(2):
                        pool.wait_ge(placed, c + 1)
                        for t in range(NT):
                            nc.gpsimd.indirect_dma_start(
                                out=rows_dram, out_offset=bass.IndirectOffsetOnAxis(ap=pos[:, c, t:t + 1], axis=0),
                                in_=ROW[:, c, t, :], in_offset=None).then_inc(sent, 16)
                    pool.wait_ge(sent, 16 * 2 * NT)
                    with pool.Fori(0, NET // UN) as it:
                        for a in range(UN):
                            wait_apart(pool, yg_ok, it * UN + a + 1 + PRIME)
                            for b in range(2):
                                nc.gpsimd.indirect_dma_start(
                                    out=out_dram, out_offset=bass.IndirectOffsetOnAxis(ap=yid[:, a, b:b + 1], axis=0),
                                    in_=yg[:, a, b, :], in_offset=None).then_inc(y_out[a], 16)
                            if a >= UN // 2:
                                pool.wait_ge(y_out[a - UN // 2], it * 32 + 32)
                                pool.sem_inc(y_free, 1)
                        for a in range(UN - UN // 2, UN):
                            pool.wait_ge(y_out[a], it * 32 + 32)
                            pool.sem_inc(y_free, 1)

                @block.scalar
                def _(act):
                    act.wait_ge(r_step, 2)
                    nc.scalar.activation(rt[0][:], rt[0][:], ACT.Exp).then_inc(r_exp, 1)
                    for e in range(NE):
                        act.wait_ge(w_in[e % 2], 16 * (e // 2 + 1))
                        nc.scalar.activation(whi[:, e * wcols:(e + 1) * wcols], stage[:, e % 2], ACT.Copy, scale=WSCALE).then_inc(whi_ok, 1)

                    def split(a, n):
                        act.wait_ge(xT_mm, n + a + 1)
                        nc.scalar.activation(xs[0:C, a % UN], turned(a), ACT.Copy).then_inc(hi_ok, 1)

                    for a in range(AHEAD):
                        split(a, 0)
                    with act.Fori(0, NET // UN) as it:
                        for q, (a, u) in enumerate(seq):
                            act.wait_ge(up_mm, it * len(seq) + q + 1)
                            nc.scalar.activation(sil[:, q % PAIRS], PS[:, 2 * (q % PAIRS), :], ACT.Silu, scale=1.0 / WSCALE).then_inc(sil_ok, 1)
                            if u == 0:
                                split(a + AHEAD, it * UN)

                @block.tensor
                def _(pe):
                    pe.wait_ge(picked, 1)
                    both = rt[5][:].rearrange("p t e -> p (t e)")
                    nc.tensor.matmul(PS[:, 0, 0:NT * NE], k("before"), both, start=True, stop=True)
                    nc.tensor.matmul(PS[:, 1, 0:NT * NE], k("ones"), both, start=True, stop=True).then_inc(counted, 1)
                    pe.wait_ge(wlo_ok, NE)
                    pe.wait_ge(w2_in, 16)
                    pe.wait_ge(routed, 1)

                    def turn(a, rows_in, split_before, made=None):
                        wait_apart(pe, x_in[a % UN], rows_in, *((xs_ok, split_before) if split_before is not None else ()),
                                   *((yg_ok, made) if made is not None else ()))
                        for b in range(2):
                            last = nc.tensor.transpose(turned(a)[:, b * P:(b + 1) * P], xt[:, a % UN, b, 0:C], ident)
                        last.then_inc(xT_mm, 1)

                    for a in range(AHEAD):
                        turn(a, 16, a if a > 0 else None)
                    with pe.Fori(0, NET // UN) as it:
                        _, ex = nc.values_load_multi_w_load_instructions(ex_i[0:1, bass.ds(it * UN, UN)], engines=[mybir.EngineType.PE],
                                                                         min_val=0, max_val=NE - 1)

                        def up(q):
                            a, u = seq[q]
                            if u == 0:
                                wait_apart(pe, xs_ok, it * UN + a + 1)
                            for v, j in enumerate(units[u]):
                                parts = ((0, j), (1, full + j)) if j < full else ((0, 2 * full),)
                                for bank, col in parts:
                                    o = PS[:, 2 * (q % PAIRS) + bank, v * ETOK:(v + 1) * ETOK]
                                    at = ex[a] * wcols + col * P
                                    nc.tensor.matmul(o, whi[:, bass.ds(at, P)], xs[:, a], start=True, stop=False)
                                    last = nc.tensor.matmul(o, wlo[:, bass.ds(at, P)], xs[:, a], start=False, stop=True)
                            last.then_inc(up_mm, 1)

                        def down(q):
                            a, u = seq[q]
                            pe.wait_ge(hid_ok, it * len(seq) + q + 1)
                            if u == 0 and U == 1:
                                pe.wait_ge(yg_ok, it * UN + a + PRIME)
                            elif u == 0:
                                pe.wait_ge(xs_ok, it * UN + a + 2)
                            for v, j in enumerate(units[u]):
                                rows = P if j < full else rest
                                for b in range(2):
                                    last = nc.tensor.matmul(
                                        PS[:, outputs(a), b * C:(b + 1) * C], hid_t[0:rows, q % PAIRS, v * ETOK + b * P:v * ETOK + (b + 1) * P],
                                        w2[0:rows, bass.ds(ex[a] * ((full + 1) * C) + j * C, C)], start=(j == 0 and b == 0), stop=(j == full and b == 1))
                            if u == U - 1:
                                last.then_inc(y_mm, 1)

                        nq = len(seq)
                        for q in range(nq + LAG):
                            if q < nq:
                                up(q)
                                if seq[q][1] == 0:
                                    a = seq[q][0] + AHEAD
                                    turn(a, it * 16 + (16 if a < UN else 32), it * UN + a, None if U == 1 else it * UN + a)
                            if q >= LAG:
                                down(q - LAG)

                @block.vector
                def _(dve):
                    r_at = [0]

                    def step(ins):
                        r_at[0] += 1
                        ins.then_inc(r_step, 1)
                        dve.wait_ge(r_step, r_at[0])

                    tt, red = nc.vector.tensor_tensor, nc.vector.tensor_reduce
                    prob, prob2, w, one1, both, cum, cum2, one2, full_pos, tmp = rt[0], rt[1], rt[2], rt[3], rt[5], rt[6], rt[7], rt[4], rt[8], rt[9]
                    mx, m1, m2, wm, den, psum = rv
                    step(red(mx[:], LG[:], op=ALU.max, axis=AX.X))
                    step(tt(prob[:], LG[:], bc(mx[:], NE), ALU.subtract))
                    dve.wait_ge(r_exp, 1)
                    step(red(psum[:], prob[:], op=ALU.add, axis=AX.X))
                    step(nc.vector.reciprocal(psum[:], psum[:]))
                    step(tt(prob[:], prob[:], bc(psum[:], NE), ALU.mult))

                    def pick(src, top, one):
                        step(red(top[:], src[:], op=ALU.max, axis=AX.X))
                        step(tt(w[:], src[:], bc(top[:], NE), ALU.is_equal))
                        step(tt(w[:], w[:], over(k("first"), NT), ALU.mult))
                        step(red(wm[:], w[:], op=ALU.max, axis=AX.X))
                        step(tt(one[:], w[:], bc(wm[:], NE), ALU.is_equal))

                    pick(prob, m1, one1)
                    step(nc.vector.scalar_tensor_tensor(out=prob2[:], in0=one1[:], scalar=-2.0, in1=prob[:], op0=ALU.mult, op1=ALU.add))
                    pick(prob2, m2, one2)
                    tt(both[:], one1[:], one2[:], ALU.add).then_inc(picked, 1)
                    step(nc.vector.scalar_tensor_tensor(out=den[:], in0=m1[:], scalar=1e-9, in1=m2[:], op0=ALU.add, op1=ALU.add))
                    step(nc.vector.reciprocal(den[:], den[:]))
                    for c, m in enumerate((m1, m2)):
                        nc.vector.scalar_tensor_tensor(out=ROW[:, c, :, C + 1], in0=m[:], scalar=1.0 / WSCALE, in1=den[:],
                                                       op0=ALU.mult, op1=ALU.mult)
                        nc.vector.tensor_copy(ROW[:, c, :, C], k("token")[:, c * NT:(c + 1) * NT])
                    dve.wait_ge(counted, 1)
                    totals = PS[:, 1, 0:NT * NE].rearrange("p (t e) -> p t e", e=NE)
                    step(nc.vector.tensor_copy(cum[:], totals))
                    a, b, sh = cum, cum2, 1
                    while sh < NT:
                        nc.vector.tensor_copy(b[:, 0:sh, :], a[:, 0:sh, :])
                        step(tt(b[:, sh:, :], a[:, sh:, :], a[:, :NT - sh, :], ALU.add))
                        a, b, sh = b, a, 2 * sh
                    cnt, tl, end, base = re
                    step(nc.vector.tensor_scalar(tl[:], a[:, NT - 1, :], ETOK / 2 - 0.5, 1.0 / ETOK, ALU.add, ALU.mult))
                    step(nc.vector.tensor_scalar(tl[:], tl[:], 8388608.0, None, ALU.add))
                    step(nc.vector.tensor_scalar(tl[:], tl[:], -8388608.0, float(ETOK), ALU.add, ALU.mult))
                    step(nc.vector.tensor_copy(end[:], tl[:]))
                    for e in range(1, NE):
                        step(tt(end[:, e:e + 1], end[:, e:e + 1], end[:, e - 1:e], ALU.add))
                    step(tt(base[:], end[:], tl[:], ALU.subtract))
                    step(tt(b[:], a[:], totals, ALU.subtract))
                    step(tt(b[:], b[:], PS[:, 0, 0:NT * NE].rearrange("p (t e) -> p t e", e=NE), ALU.add))
                    step(tt(full_pos[:], b[:], over(base[:], NT), ALU.add))
                    for c, one in ((0, one1), (1, one2)):
                        step(tt(tmp[:], one[:], full_pos[:], ALU.mult))
                        step(red(wm[:], tmp[:], op=ALU.add, axis=AX.X))
                        nc.vector.tensor_copy(pos[:, c, :], wm[:]).then_inc(placed, 1)
                        dve.wait_ge(placed, c + 1)
                    step(tt(of_tile[:], over(end[:], NET), bc(k("tile_at"), NE), ALU.is_le))
                    step(red(ex_f[:], of_tile[:], op=ALU.add, axis=AX.X))
                    step(nc.vector.tensor_scalar(ex_f[:], ex_f[:], NE - 1.0, None, ALU.min))
                    nc.vector.tensor_copy(ex_i[:], ex_f[:]).then_inc(routed, 1)
                    for e in range(NE):
                        dve.wait_ge(whi_ok, e + 1)
                        nc.vector.scalar_tensor_tensor(out=wlo[:, e * wcols:(e + 1) * wcols], in0=stage[:, e % 2], scalar=WSCALE,
                                                       in1=whi[:, e * wcols:(e + 1) * wcols], op0=ALU.mult, op1=ALU.subtract)\
                            .then_inc(wlo_ok, 1)
                    dve.sem_inc(yg_ok, PRIME)
                    dve.sem_inc(y_free, UN)

                    def split(a, n):
                        dve.wait_ge(hi_ok, n + a + 1)
                        nc.vector.tensor_tensor(xs[C:P, a % UN], turned(a), xs[0:C, a % UN], ALU.subtract).then_inc(xs_ok, 1)

                    for a in range(AHEAD):
                        split(a, 0)
                    with dve.Fori(0, NET // UN) as it:
                        def gated(a):
                            dve.wait_ge(y_free, it * UN + a + 1)
                            dve.wait_ge(y_mm, it * UN + a + 1)
                            nc.vector.tensor_copy(yid[:, a], xt[:, a, :, C])
                            last = nc.vector.tensor_tensor(yg[:, a], PS[:, outputs(a), 0:2 * C].rearrange("p (b c) -> p b c", b=2), bc(xt[:, a, :, C + 1], C), ALU.mult)
                            last.then_inc(yg_ok, 1)

                        for q, (a, u) in enumerate(seq):
                            dve.wait_ge(sil_ok, it * len(seq) + q + 1)
                            last = None
                            j, j2, w = *units[u], q % PAIRS
                            if j2 < full:
                                last = nc.vector.tensor_tensor(hid_t[:, w], sil[:, w], PS[:, 2 * w + 1, :], ALU.mult)
                            else:
                                nc.vector.tensor_tensor(hid_t[:, w, 0:ETOK], sil[:, w, 0:ETOK], PS[:, 2 * w + 1, 0:ETOK], ALU.mult)
                                last = nc.vector.tensor_tensor(hid_t[0:rest, w, ETOK:], sil[0:rest, w, ETOK:],
                                                               PS[C:C + rest, 2 * w, ETOK:], ALU.mult)
                            last.then_inc(hid_ok, 1)
                            if u == 0:
                                split(a + AHEAD, it * UN)
                            if q >= LAG and seq[q - LAG][1] == U - 1:
                                gated(seq[q - LAG][0])
                        for a, u in seq[-LAG:]:
                            if u == U - 1:
                                gated(a)
                    for c in range(NC):
                        dve.wait_ge(y_in[c], 32)
                        nc.vector.tensor_tensor(y12[:, 0, part[c]], y12[:, 0, part[c]], y12[:, 1, part[c]], ALU.add).then_inc(y_sum, 1)
                        dve.wait_ge(y_sum, c + 1)
                        nc.vector.tensor_tensor(H[:, part[c]], H[:, part[c]], y12[:, 0, part[c]], ALU.add).then_inc(h_ok, 1)

        features(0)
        experts(0)

        e_ctx = ExitStack()
        with e_ctx:
            ZS = tile(e_ctx, "e_ZS", [P, (NG + 1) * GTOK], F16)
            O = tile(e_ctx, "e_O", [P, NT, NH1 * DV])
            OR = tile(e_ctx, "e_OR", [P, NT + 1, NH1])
            norm_phase("e_ln", H, LN_EPS, ZS)

            with ExitStack() as ctx:
                TB = 2 * GT
                NQ = 4
                ONE = DV + 1
                qs = tile(ctx, "e_qs", [P, 2, GTOK], F16)
                qb = tile(ctx, "e_qb", [P, 2, NQ, GB, 4, L], F16)
                kh = tile(ctx, "e_kh", [P, 2, NQ, GTOK], F16)
                kl = tile(ctx, "e_kl", [P, 2, NQ, GTOK], F16)
                vb = tile(ctx, "e_vb", [P, 2, GB, NH1 // 2, 2, ONE])
                zd = tile(ctx, "e_zd", [P, 2, GB, 2, L], F16)
                sc = tile(ctx, "e_sc", [P, 2, 2, NH1, L])
                mx = tile(ctx, "e_mx", [P, 2, 16])
                eT = tile(ctx, "e_eT", [P, 2, 4, P])
                rs = tile(ctx, "e_rs", [P, 2, NH1])
                o2 = tile(ctx, "e_o2", [L, 2, 2, 2, NH1, DV])
                sq = tile(ctx, "e_sq", [P, 2, NH1, DV])
                var = tile(ctx, "e_var", [P, 2, NH1])
                names = ("init", "zd_ok", "piece_mm", "hi_ok", "piece_ok", "qs_ok", "q_ok", "sc_mm", "mx_ok", "sub_ok", "exp_ok", "eT_mm", "eT_ok",
                         "av_mm", "rs_ok", "o2_ok", "o_ok", "sq_ok", "ss_ok", "var_ok", "or_ok")
                (init, zd_ok, piece_mm, hi_ok, piece_ok, qs_ok, q_ok, sc_mm, mx_ok, sub_ok, exp_ok, eT_mm, eT_ok,
                 av_mm, rs_ok, o2_ok, o_ok, sq_ok, ss_ok, var_ok, or_ok) = (sem(ctx, "e_" + n) for n in names)
                block = phase_block(ctx)
                PIECES = [(kind, j) for j in range(NQ) for kind in "qk"] + [("v", j) for j in range(GB // 2)]
                NPC, NQK, PT = len(PIECES), 2 * NQ, len(PIECES) // GT
                EB, AB, JB = 4, 6, 7
                PRIME = 4

                def bank(i):
                    return (JB + i) % 8

                def ahead(it, t, x):
                    return it * 2 + t // GT + 1, (t // GT + 1) % 2, PT * (t % GT) + x, (it * 2 + t // GT + 1) * NPC + PT * (t % GT) + x + 1

                @block.tensor
                def _(pe):
                    def piece(g, par, i, n, JB=JB):
                        kind, j = PIECES[i]
                        if isinstance(n, int):
                            if kind == "v":
                                pe.wait_ge(piece_ok, 2 * NQ + 1)
                                pe.wait_ge(zd_ok, 1)
                            return product(g, par, i, JB)
                        wait_apart(pe, *((piece_ok, n) + ((zd_ok, g + 1) if kind == "v" else ())))
                        product(g, par, i, JB)

                    def product(g, par, i, JB):
                        kind, j = PIECES[i]
                        if kind == "v":
                            for s in range(2):
                                z = zd[:, par, 2 * j + s].rearrange("p u l -> p (u l)")
                                for w in range(2):
                                    last = nc.tensor.matmul(PS[:, JB, s * 256:(s + 1) * 256], z,
                                                            WE[w][:, VCOL:GCOL], start=(w == 0), stop=(w == 1))
                        else:
                            col = (j if kind == "q" else NQ + j) * P
                            for w in range(2):
                                last = nc.tensor.matmul(PS[:, JB, :], WE[w][:, col:col + P], ZS[:, bass.ds(g * GTOK, GTOK)],
                                                        start=(w == 0), stop=(w == 1))
                        last.then_inc(piece_mm, 1)

                    def scores(t):
                        par, tt = t // GT % 2, t % GT
                        for b in range(2):
                            for m in range(NH1):
                                s, j, pr = 2 * tt + b, m // 2, m % 2
                                for i, key in enumerate((kh, kl)):
                                    last = nc.tensor.matmul(
                                        PS[:, 2 * (t % 2) + b, m * L:(m + 1) * L],
                                        qb[:, par, j, s, 2 * pr:2 * pr + 2].rearrange("p h l -> p (h l)"),
                                        key[:, par, j, s * L:(s + 1) * L], start=(i == 0), stop=(i == 1))
                            last.then_inc(sc_mm, 1)

                    def turn(t, b):
                        for c in range(4):
                            last = nc.tensor.transpose(PS[:, EB + b, c * P:(c + 1) * P],
                                                       sc[:, t % 2, b, 2 * c:2 * c + 2, :].rearrange("p m l -> p (m l)"), ident)
                        last.then_inc(eT_mm, 1)

                    def weigh(t, b):
                        par, s = t // GT, 2 * (t % GT) + b
                        for c in range(4):
                            last = nc.tensor.matmul(PS[:, AB, c * 2 * ONE:(c + 1) * 2 * ONE], eT[:, b, c],
                                                    vb[:, par, s, c].rearrange("p u e -> p (u e)"), start=True, stop=True)
                        last.then_inc(av_mm, 1)

                    for i in range(NPC):
                        piece(0, 0, i, i + 1, bank(i))
                    pe.wait_ge(init, 3)
                    pe.wait_ge(piece_ok, NPC + 1)
                    pe.wait_ge(q_ok, 2 * NQ)
                    scores(0)
                    scores(1)
                    with pe.Fori(0, NT // TB) as it:
                        for t in range(TB):
                            n = it * TB + t
                            for b in range(2):
                                wait_apart(pe, exp_ok, 2 * n + b + 1)
                                turn(t, b)
                            piece(*ahead(it, t, 0))
                            wait_apart(pe, eT_ok, 2 * n + 1, o2_ok, 2 * n + 1, piece_ok, (it * 2 + t // GT + 1) * NPC + 1)
                            weigh(t, 0)
                            piece(*ahead(it, t, 1))
                            wait_apart(pe, eT_ok, 2 * n + 2, o2_ok, 2 * n + 2)
                            weigh(t, 1)
                            piece(*ahead(it, t, 2))
                            wait_apart(pe, sub_ok, 2 * n + 2, q_ok, (it * 2 + (t + 2) // GT + 1) * 2 * NQ,
                                       piece_ok, (it * 2 + (t + 2) // GT) * NPC + NQK + 1)
                            scores(t + 2)

                @block.vector
                def _(dve):
                    def softmax(t, n):
                        s4 = [PS[:, 2 * (t % 2) + b, :].rearrange("p (m l) -> p m l", l=L) for b in range(2)]
                        for b in range(2):
                            dve.wait_ge(sc_mm, 2 * n + b + 1)
                            nc.vector.tensor_reduce(mx[:, t % 2, 8 * b:8 * b + 8], s4[b], op=ALU.max, axis=AX.X).then_inc(mx_ok, 1)
                        for b in range(2):
                            dve.wait_ge(mx_ok, 2 * n + b + 1)
                            nc.vector.tensor_tensor(sc[:, t % 2, b], s4[b], bc(mx[:, t % 2, 8 * b:8 * b + 8], L), ALU.subtract).then_inc(sub_ok, 1)

                    def combine(t, b, n):
                        m = 2 * n + b
                        dve.wait_ge(av_mm, m + 1)
                        av = PS[:, AB, 0:NH1 * ONE].rearrange("p (m e) -> p m e", e=ONE)
                        nc.vector.reciprocal(rs[:, b], av[:, :, DV]).then_inc(rs_ok, 1)
                        dve.wait_ge(rs_ok, m + 1)
                        dve.wait_ge(o_ok, m + 1)
                        for u in range(2):
                            h = slice(u * L, (u + 1) * L)
                            last = nc.vector.scalar_tensor_tensor(out=o2[:, t % 2, b, u], in0=av[h, :, 0:DV], scalar=LAMU[h],
                                                                  in1=bc(rs[h, b], DV), op0=ALU.mult, op1=ALU.mult)
                        last.then_inc(o2_ok, 1)

                    def low(g, par, i, n, JB=JB):
                        kind, j = PIECES[i]
                        if kind == "v":
                            return
                        dve.wait_ge(hi_ok, g * 2 * NQ + i + 1)
                        if kind == "k":
                            nc.vector.scalar_tensor_tensor(out=kl[:, par, j], in0=PS[:, JB, :], scalar=1 / WSCALE, in1=kh[:, par, j],
                                                           op0=ALU.mult, op1=ALU.subtract).then_inc(piece_ok, 1)
                            return
                        q = qs[:, j % 2]
                        nc.vector.scalar_tensor_tensor(out=q[C:P], in0=PS[C:P, JB, :], scalar=HD ** -0.5 / WSCALE, in1=q[C:P],
                                                       op0=ALU.mult, op1=ALU.subtract).then_inc(piece_ok, 1)

                    def spread(g, par, i, n):
                        kind, j = PIECES[i]
                        if kind == "q":
                            dve.wait_ge(piece_ok, n + 1)
                            for h in range(2):
                                last = nc.vector.tensor_scalar(qb[:, par, j, :, h, :], qs[:, j % 2].rearrange("p (b l) -> p b l", l=L),
                                                               k("head_mask")[:, h:h + 1], None, ALU.mult)
                            last.then_inc(q_ok, 1)

                    def variance(t, n):
                        v = var[:, (t + 1) % 2]
                        dve.wait_ge(sq_ok, n + 1)
                        nc.vector.tensor_reduce(v, sq[:, (t + 1) % 2], op=ALU.add, axis=AX.X).then_inc(ss_ok, 1)
                        dve.wait_ge(ss_ok, n + 1)
                        nc.vector.tensor_scalar(v, v, 1.0 / DV, LN_EPS, ALU.mult, ALU.add).then_inc(var_ok, 1)

                    dve.sem_inc(o2_ok, 1)
                    for i in range(NPC):
                        low(0, 0, i, i + 1, bank(i))
                        spread(0, 0, i, i + 1)
                    softmax(0, 0)
                    with dve.Fori(0, NT // TB) as it:
                        for t in range(TB):
                            n = it * TB + t
                            softmax(t + 1, n + 1)
                            variance(t, n)
                            low(*ahead(it, t, 0))
                            combine(t, 0, n)
                            spread(*ahead(it, t, 0))
                            low(*ahead(it, t, 1))
                            combine(t, 1, n)
                            spread(*ahead(it, t, 1))
                            low(*ahead(it, t, 2))
                            spread(*ahead(it, t, 2))
                    variance(0, NT)

                @block.scalar
                def _(act):
                    def high(g, par, i, n, JB=JB):
                        kind, j = PIECES[i]
                        act.wait_ge(piece_mm, n)
                        if kind == "q":
                            if isinstance(n, int) and j >= 2:
                                act.wait_ge(piece_ok, n - 2)
                            nc.scalar.activation(qs[:, j % 2], PS[:, JB, :], ACT.Copy, scale=HD ** -0.5 / WSCALE).then_inc(hi_ok, 1)
                        elif kind == "k":
                            nc.scalar.activation(kh[:, par, j], PS[:, JB, :], ACT.Copy, scale=1 / WSCALE).then_inc(hi_ok, 1)
                        else:
                            for u in range(2):
                                last = nc.scalar.activation(
                                    vb[u * L:(u + 1) * L, par, 2 * j:2 * j + 2, :, u, 0:DV],
                                    PS[u * L:(u + 1) * L, JB, :].rearrange("p (b m v e) -> p b m v e", b=2, v=2, e=DV)[:, :, :, u, :],
                                    ACT.Copy, scale=1 / WSCALE)
                            last.then_inc(piece_ok, 1)

                    def spread(g, par, i, n):
                        kind, j = PIECES[i]
                        if kind == "q":
                            act.wait_ge(piece_ok, n + 1)
                            for h in range(2, 4):
                                last = nc.scalar.activation(qb[:, par, j, :, h, :], qs[:, j % 2].rearrange("p (b l) -> p b l", l=L), ACT.Copy,
                                                            scale=k("head_mask")[:, h:h + 1])
                            last.then_inc(q_ok, 1)

                    def exps(t, n):
                        for b in range(2):
                            act.wait_ge(sub_ok, 2 * n + b + 1)
                            nc.scalar.activation(sc[:, t % 2, b], sc[:, t % 2, b], ACT.Exp).then_inc(exp_ok, 1)

                    act.sem_inc(piece_ok, 1)
                    for i in range(NPC):
                        if i == NPC - GB // 2:
                            act.wait_ge(init, 3)
                        high(0, 0, i, i + 1, bank(i))
                        spread(0, 0, i, i + 1)
                    exps(0, 0)
                    with act.Fori(0, NT // TB) as it:
                        for t in range(TB):
                            n = it * TB + t
                            for b in range(2):
                                act.wait_ge(eT_mm, 2 * n + b + 1)
                                nc.scalar.activation(eT[:, b].rearrange("p m l -> p (m l)"), PS[:, EB + b, :], ACT.Copy).then_inc(eT_ok, 1)
                            high(*ahead(it, t, 0))
                            exps(t + 1, n + 1)
                            spread(*ahead(it, t, 0))
                            high(*ahead(it, t, 1))
                            spread(*ahead(it, t, 1))
                            high(*ahead(it, t, 2))
                            spread(*ahead(it, t, 2))

                @block.gpsimd
                def _(pool):
                    def spread(g, par):
                        nc.gpsimd.tensor_copy(zd[:, par], ZS[:, bass.ds(g * GTOK, GTOK)].rearrange("p (b l) -> p b l", l=L).unsqueeze(2)
                                              .broadcast_to([P, GB, 2, L])).then_inc(zd_ok, 1)

                    def power(t, n):
                        wait_apart(pool, var_ok, n + 1)
                        nc.gpsimd.tensor_tensor(OR[:, bass.ds(n, 1), :], var[:, (t + 1) % 2].unsqueeze(1), NHALF[:, 0:NH1].unsqueeze(1),
                                                ALU.pow).then_inc(or_ok, 1)

                    nc.gpsimd.memset(vb[:], 0.0).then_inc(init, 1)
                    pool.wait_ge(init, 1)
                    nc.gpsimd.memset(vb[0:L, :, :, :, 0, DV:ONE], 1.0)
                    pool.sem_inc(init, 1)
                    pool.wait_ge(init, 2)
                    nc.gpsimd.memset(vb[L:P, :, :, :, 1, DV:ONE], 1.0).then_inc(init, 1)
                    pool.wait_ge(init, 3)
                    spread(0, 0)
                    pool.sem_inc(o_ok, PRIME)
                    pool.wait_ge(zd_ok, 1)
                    nc.gpsimd.tensor_tensor(H[:], H[:], over(BOUT[:], NT), ALU.add).then_inc(init, 1)
                    pool.wait_ge(init, 4)
                    nc.gpsimd.memset(sq[:, 1], 0.0).then_inc(sq_ok, 1)
                    with pool.Fori(0, NT // TB) as it:
                        for t in range(TB):
                            n = it * TB + t
                            wait_apart(pool, sq_ok, n + 1)
                            power(t, n)
                            if t % GT == 0:
                                wait_apart(pool, or_ok, n + 1)
                                spread(it * 2 + t // GT + 1, (t // GT + 1) % 2)
                                wait_apart(pool, zd_ok, it * 2 + t // GT + 2)
                            for b in range(2):
                                wait_apart(pool, *((or_ok, n + 1) if b == 0 else (o_ok, 2 * n + 1 + PRIME)), o2_ok, 2 * n + b + 2)
                                both = [o2[:, t % 2, b, u].rearrange("p m e -> p (m e)").unsqueeze(1) for u in range(2)]
                                nc.gpsimd.tensor_tensor(O[b * L:(b + 1) * L, bass.ds(n, 1), :], both[0], both[1], ALU.add).then_inc(o_ok, 1)
                            wait_apart(pool, o_ok, 2 * n + 2 + PRIME)
                            o = O[:, bass.ds(n, 1), :]
                            nc.gpsimd.tensor_tensor(sq[:, t % 2].rearrange("p m e -> p (m e)").unsqueeze(1), o, o, ALU.mult).then_inc(sq_ok, 1)
                    pool.wait_ge(sq_ok, NT + 1)
                    power(0, NT)

            with ExitStack() as ctx:
                on = tile(ctx, "g_on", [P, STREAMS, GT, NH1, DV])
                sg = tile(ctx, "g_sg", [P, STREAMS, 2, GTOK])
                og = tile(ctx, "g_og", [P, STREAMS, 2, GTOK])
                on_ok, g_mm, sg_ok, oT_mm, af_ok, og_ok, out_mm, h_ok = (
                    sem(ctx, "g_" + n) for n in ("on_ok", "g_mm", "sg_ok", "oT_mm", "af_ok", "og_ok", "out_mm", "h_ok"))
                block = phase_block(ctx)

                @block.vector
                def _(dve):
                    with dve.Fori(0, NG // NB) as it:
                        def normalise(g):
                            s, n = g % STREAMS, it * NB + g
                            nc.vector.tensor_tensor(on[:, s], tiles(O, n).rearrange("p t (m e) -> p t m e", e=DV),
                                                    OR[:, bass.ds(n * GT + 1, GT), :].unsqueeze(3).broadcast_to([P, GT, NH1, DV]),
                                                    ALU.mult).then_inc(on_ok, 1)

                        def gate(g):
                            s, n = g % STREAMS, it * NB + g
                            dve.wait_ge(af_ok, n + 1)
                            nc.vector.tensor_tensor(og[:, s], sg[:, s], og[:, s], ALU.mult).then_inc(og_ok, 1)

                        def add(g):
                            s, n = g % STREAMS, it * NB + g
                            dve.wait_ge(out_mm, n + 1)
                            h = tiles(H, n)
                            nc.vector.tensor_tensor(h, h, PS[:, 4 * s, 0:GT * C].rearrange("p (t c) -> p t c", c=C), ALU.add).then_inc(h_ok, 1)

                        staggered(NB, (normalise, 0), (gate, 1), (add, 2))

                @block.scalar
                def _(act):
                    with act.Fori(0, NG // NB) as it:
                        for g in range(NB):
                            s = g % STREAMS
                            act.wait_ge(g_mm, it * NB + g + 1)
                            for hf in range(2):
                                last = nc.scalar.activation(sg[:, s, hf], PS[:, 4 * s + hf, :], ACT.Sigmoid, scale=1 / WSCALE, bias=BG[:, hf:hf + 1])
                            last.then_inc(sg_ok, 1)
                            act.wait_ge(oT_mm, it * NB + g + 1)
                            nc.scalar.activation(og[:, s], PS[:, 4 * s + 2:4 * s + 4, :], ACT.Identity, scale=LNH[:, 0:1],
                                                 bias=LNH[:, 1:2]).then_inc(af_ok, 1)

                @block.tensor
                def _(pe):
                    pe.sem_inc(h_ok, STREAMS)
                    with pe.Fori(0, NG // NB) as it:
                        def gates(g):
                            s, n = g % STREAMS, it * NB + g
                            wait_apart(pe, h_ok, n + 1)
                            for hf, w in ((0, 0), (0, 1), (1, 0), (1, 1)):
                                last = nc.tensor.matmul(PS[:, 4 * s + hf, :], WE[w][:, GCOL + hf * P:GCOL + (hf + 1) * P],
                                                        ZS[:, bass.ds(n * GTOK, GTOK)], start=(w == 0), stop=(w == 1))
                            last.then_inc(g_mm, 1)

                        def turn(g):
                            s, n = g % STREAMS, it * NB + g
                            wait_apart(pe, on_ok, n + 1)
                            for t in range(GT):
                                for hf in range(2):
                                    last = nc.tensor.transpose(PS[:, 4 * s + 2 + hf, t * P:(t + 1) * P],
                                                               on[:, s, t, 4 * hf:4 * hf + 4].rearrange("p m e -> p (m e)"), ident)
                            last.then_inc(oT_mm, 1)

                        def project(g):
                            s, n = g % STREAMS, it * NB + g
                            wait_apart(pe, og_ok, n + 1)
                            for t in range(GT):
                                for hf in range(2):
                                    last = nc.tensor.matmul(PS[:, 4 * s, t * C:(t + 1) * C], og[:, s, hf, t * P:(t + 1) * P],
                                                            WOUT[:, hf], start=(hf == 0), stop=(hf == 1))
                            last.then_inc(out_mm, 1)

                        staggered(NB, (gates, 0), (turn, 0), (project, 1))

        features(1)
        experts(1)


def kernel(**inputs):
    import numpy as _np
    import concourse.bacc as _bacc
    from concourse import mybir as _mybir
    from concourse.bass_utils import run_bass_kernel_spmd as _run

    a = {n: _np.asarray(v) for n, v in inputs.items()}
    consts, cols = constants()

    empty = _np.zeros(((NET + 2) * ETOK, RW_), _np.float32)
    empty[:, C] = 2 * NTOK + _np.arange(len(empty))

    def rows(v):
        return _np.broadcast_to(v[None], (P,) + v.shape)

    def twice(w):
        return _np.repeat(w.reshape(C, -1, 1, C), 2, 2).reshape(C, -1)

    def up_weights(w1, w3):
        ne, hid, c = w1.shape
        full = hid // P * P
        t1, t3 = w1.transpose(0, 2, 1), w3.transpose(0, 2, 1)
        last = _np.zeros((ne, c, P), w1.dtype)
        last[:, :, 0:hid - full] = t1[:, :, full:]
        last[:, :, C:C + hid - full] = t3[:, :, full:]
        one = _np.concatenate([t1[:, :, :full], t3[:, :, :full], last], 2)
        return _np.concatenate([one, one], 1)

    def down_weights(w2):
        ne, c, hid = w2.shape
        chunks = hid // P + 1
        t = _np.zeros((ne, chunks * P, c), w2.dtype)
        t[:, :hid] = w2.transpose(0, 2, 1)
        return t.reshape(ne, chunks, P, c).transpose(0, 2, 1, 3)

    host = {
        "consts": consts, "empty": empty,
        "x": a["x"][:, 0],
        "L0_tok_W": a["L0_tok_W"],
        "L0_attn_Wq": a["L0_attn_Wq"], "L0_attn_Wk": a["L0_attn_Wk"], "L0_attn_Wv": a["L0_attn_Wv"],
        "L0_attn_WoT": a["L0_attn_Wo"].T,
        "L0_ffn_wq": a["L0_ffn_wq"], "L0_ffn_wk": a["L0_ffn_wk"],
        "L0_ffn_wvT": a["L0_ffn_wv"].T, "L0_ffn_woT": a["L0_ffn_wo"].T,
        "L1_qkvg": _np.concatenate([_np.concatenate([twice(a["L1_attn_Wq"]), twice(a["L1_attn_Wkv"][:, :256]), a["L1_attn_Wkv"][:, 256:],
                                                     a["L1_attn_Wg"]], 1)] * 2, 0),
        "L1_bg": a["L1_attn_bg"].reshape(2, P).T,
        "L1_out": a["L1_attn_Wout"].reshape(2, P, C).transpose(1, 0, 2),
        "router": _np.stack([a["L0_ffn_router_w"].T, a["L1_ffn_router_w"].T], 1),
        "ln_w": _np.stack([a["L0_ffn_ln1_w"], a["L0_ffn_ln2_w"]], 1),
        "ln_rows": rows(a["L0_ffn_ln2_w"]),
        "tok_b": rows(a["L0_tok_b"]), "bout": rows(a["L1_attn_bout"]),
        "ln_head": _np.tile(_np.stack([a["L1_attn_ln_gamma"], a["L1_attn_ln_beta"]], 1), (P // DV, 1)),
        "lam_q": rows(_np.stack([a["L1_attn_lq1"], a["L1_attn_lk1"], a["L1_attn_lq2"], a["L1_attn_lk2"]])),
        "w13_0": up_weights(a["L0_ffn_w1"], a["L0_ffn_w3"]), "w2_0": down_weights(a["L0_ffn_w2"]),
        "w13_1": up_weights(a["L1_ffn_w1"], a["L1_ffn_w3"]), "w2_1": down_weights(a["L1_ffn_w2"]),
    }
    nc = _bacc.Bacc("TRN2", target_bir_lowering=False, num_devices=1)
    arrays, dram = {}, {}
    for name, v in host.items():
        v = _np.ascontiguousarray(v)
        arrays[f"in_{name}"] = v
        dram[name] = nc.dram_tensor(f"in_{name}", v.shape, _mybir.dt.from_np(v.dtype), kind="ExternalInput").ap()
    out = nc.dram_tensor("out", (NTOK, C), _mybir.dt.float32, kind="ExternalOutput").ap()
    build(nc, dram, out, cols)
    r = _run(nc, [arrays], core_ids=[0])
    return r.results[0]["out"].reshape(B, L, C)
```
